# Optimizing a Trainium2 kernel written in Bass

```python
import numpy as np
import jax
import jax.numpy as jnp

def _softmax(x, axis=-1):
    return jax.nn.softmax(x, axis=axis)

def _gelu(x):
    return jax.nn.gelu(x, approximate=True)

def _silu(x):
    return jax.nn.silu(x)

def _sigmoid(x):
    return jax.nn.sigmoid(x)

def _layernorm(x, axis=-1, eps=1e-05):
    m = jnp.mean(x, axis=axis, keepdims=True)
    v = jnp.var(x, axis=axis, keepdims=True)
    return (x - m) / jnp.sqrt(v + eps)

def _scatter_add(tgt, idx, src, axis=0):
    return tgt.at[idx].add(src)

def _segment_sum(src, seg, n):
    return jax.ops.segment_sum(src, seg, n)
kernel_name = 'mk_decoder_postln_d2_seqx_r8_64fd85'

def setup_inputs(seed: int=0):
    np.random.seed(seed)
    _w = jnp.asarray

    def _rec_inputs():
        import jax
        import jax.numpy as jnp
        _rk = jax.random.key(seed)
        x = -0.0005207 + 1.001 * jax.random.normal(jax.random.fold_in(_rk, 1), (8, 256, 256), jnp.float32)
        _lenS = 256 - jax.random.randint(jax.random.fold_in(_rk, 7), (8,), 0, max(1, 256 // 4) + 1, jnp.int32)
        _lenS2 = 64 - jax.random.randint(jax.random.fold_in(_rk, 8), (8,), 0, max(1, 64 // 4) + 1, jnp.int32)
        _ctx_2048P = jax.random.normal(jax.random.fold_in(_rk, 12), (8, 16, 256), jnp.float32)
        _ctx_2048c = jax.random.dirichlet(jax.random.fold_in(_rk, 512), 0.3 * jnp.ones((16,), jnp.float32), (8, 64))
        _ctx_2048t = jnp.einsum('bsk,bkd->bsd', _ctx_2048c, _ctx_2048P)
        _ctx_2048t = _ctx_2048t * jax.lax.rsqrt(jnp.mean(jnp.square(_ctx_2048t)) + 1e-12) * 0.953939
        ctx_2048 = -5.72187e-05 + 0.999849 * (_ctx_2048t + 0.3 * jax.random.normal(jax.random.fold_in(_rk, 612), (8, 64, 256), jnp.float32))
        _validS = jnp.arange(256)[None, :] < _lenS[:, None]
        _validS2 = jnp.arange(64)[None, :] < _lenS2[:, None]
        _causal = jnp.tril(jnp.ones((256, 256), dtype=bool))
        mask_BxSx4224_bf0 = jnp.logical_not(jnp.ones((8, 256, 528), dtype=bool))
        return (x, ctx_2048, mask_BxSx4224_bf0)
    x, ctx_2048, mask_BxSx4224_bf0 = _rec_inputs()

    def _L0_attn_setup():
        import jax, jax.numpy as jnp
        import numpy as np
        HIDDEN = 256
        HEADS = 16
        HEAD_DIM = HIDDEN // HEADS
        key = jax.random.key(seed)
        ks = jax.random.split(key, 5)
        x = jax.random.normal(ks[0], (2, 256, HIDDEN), dtype=jnp.float32)

        def w(k):
            return 0.02 * jax.random.normal(k, (HIDDEN, HIDDEN), dtype=jnp.float32)
        return {'x': x, 'wq': w(ks[1]), 'bq': jnp.zeros((HIDDEN,), jnp.float32), 'wk': w(ks[2]), 'bk': jnp.zeros((HIDDEN,), jnp.float32), 'wv': w(ks[3]), 'bv': jnp.zeros((HIDDEN,), jnp.float32), 'wo': w(ks[4]), 'bo': jnp.zeros((HIDDEN,), jnp.float32)}
    _L0_attn_all = _L0_attn_setup()
    _L0_attn_in = {k: v for k, v in _L0_attn_all.items() if k in ('wq', 'bq', 'wk', 'bk', 'wv', 'bv', 'wo', 'bo')}
    del _L0_attn_all

    def _L0_xattn_setup():
        import jax, jax.numpy as jnp
        import numpy as np
        import math
        DIM = 256
        B, Q_LEN, KV_LEN = (8, 128, 512)
        key = jax.random.key(seed)
        ks = jax.random.split(key, 8)
        x = jax.random.normal(ks[0], (B, Q_LEN, DIM), dtype=jnp.float32)
        mask = jnp.zeros((B, Q_LEN, KV_LEN + Q_LEN), dtype=bool)
        k_cache = jax.random.normal(ks[1], (B, KV_LEN, DIM), dtype=jnp.float32)
        v_cache = jax.random.normal(ks[2], (B, KV_LEN, DIM), dtype=jnp.float32)
        scale = 1.0 / math.sqrt(DIM)
        wq = jax.random.normal(ks[3], (DIM, DIM), dtype=jnp.float32) * scale
        wk = jax.random.normal(ks[4], (DIM, DIM), dtype=jnp.float32) * scale
        wv = jax.random.normal(ks[5], (DIM, DIM), dtype=jnp.float32) * scale
        wo = jax.random.normal(ks[6], (DIM, DIM), dtype=jnp.float32) * scale
        return {'x': x, 'mask': mask, 'k_cache': k_cache, 'v_cache': v_cache, 'wq': wq, 'wk': wk, 'wv': wv, 'wo': wo}
    _L0_xattn_all = _L0_xattn_setup()
    _L0_xattn_in = {k: v for k, v in _L0_xattn_all.items() if k in ('wq', 'wk', 'wv', 'wo')}
    del _L0_xattn_all

    def _L0_ffn_setup():
        import jax, jax.numpy as jnp
        import numpy as np
        HIDDEN = 256
        INTER = 1024
        RETRIEVAL = 128
        NUM_EXPERTS = 512
        NUM_KEYS = 64
        TOP_K = 8
        B, S = (4, 256)
        key = jax.random.key(seed)
        ks = jax.random.split(key, 8)
        sc = 0.02
        return {'hidden_states': jax.random.normal(ks[0], (B, S, HIDDEN), jnp.float32), 'W_q': jax.random.normal(ks[1], (HIDDEN, RETRIEVAL), jnp.float32) * sc, 'keys': jax.random.normal(ks[2], (2, RETRIEVAL // 2, NUM_KEYS), jnp.float32) * sc, 'down_embed': jax.random.normal(ks[3], (NUM_EXPERTS, HIDDEN), jnp.float32) * sc, 'up_embed': jax.random.normal(ks[4], (NUM_EXPERTS, HIDDEN), jnp.float32) * sc, 'gate_w': jax.random.normal(ks[5], (HIDDEN, INTER), jnp.float32) * sc, 'up_w': jax.random.normal(ks[6], (HIDDEN, INTER), jnp.float32) * sc, 'down_w': jax.random.normal(ks[7], (INTER, HIDDEN), jnp.float32) * sc}
    _L0_ffn_all = _L0_ffn_setup()
    _L0_ffn_in = {k: v for k, v in _L0_ffn_all.items() if k in ('W_q', 'keys', 'down_embed', 'up_embed', 'gate_w', 'up_w', 'down_w')}
    del _L0_ffn_all

    def _L1_attn_setup():
        import jax, jax.numpy as jnp
        import numpy as np
        D = 256
        key = jax.random.key(seed)
        ks = jax.random.split(key, 5)
        scale = 1.0 / np.sqrt(D)
        x = jax.random.normal(ks[0], (4, 512, D), dtype=jnp.float32)
        Wq = jax.random.normal(ks[1], (D, D), dtype=jnp.float32) * scale
        Wk = jax.random.normal(ks[2], (D, D), dtype=jnp.float32) * scale
        Wv = jax.random.normal(ks[3], (D, D), dtype=jnp.float32) * scale
        Wo = jax.random.normal(ks[4], (D, D), dtype=jnp.float32) * scale
        return {'x': x, 'Wq': Wq, 'Wk': Wk, 'Wv': Wv, 'Wo': Wo}
    _L1_attn_all = _L1_attn_setup()
    _L1_attn_in = {k: v for k, v in _L1_attn_all.items() if k in ('Wq', 'Wk', 'Wv', 'Wo')}
    del _L1_attn_all

    def _L1_xattn_setup():
        import jax, jax.numpy as jnp
        import numpy as np
        NUM_HEADS = 16

        def _qdq(x):
            s = jnp.maximum(jnp.max(jnp.abs(x), axis=-1, keepdims=True) / 127.0, 1e-08)
            return jnp.clip(jnp.round(x / s), -127.0, 127.0) * s
        key = jax.random.key(seed)
        ks = jax.random.split(key, 8)
        B, N, M, D = (2, 512, 64, 256)
        w_std = 0.02
        return {'x': jax.random.normal(ks[0], (B, N, D), jnp.float32), 'cond': jax.random.normal(ks[1], (B, M, D), jnp.float32), 'wq': jax.random.normal(ks[2], (D, D), jnp.float32) * w_std, 'bq': jax.random.normal(ks[3], (D,), jnp.float32) * w_std, 'wkv': jax.random.normal(ks[4], (2 * D, D), jnp.float32) * w_std, 'bkv': jax.random.normal(ks[5], (2 * D,), jnp.float32) * w_std, 'wp': jax.random.normal(ks[6], (D, D), jnp.float32) * w_std, 'bp': jax.random.normal(ks[7], (D,), jnp.float32) * w_std}
    _L1_xattn_all = _L1_xattn_setup()
    _L1_xattn_in = {k: v for k, v in _L1_xattn_all.items() if k in ('wq', 'bq', 'wkv', 'bkv', 'wp', 'bp')}
    del _L1_xattn_all

    def _L1_ffn_setup():
        import jax, jax.numpy as jnp
        import numpy as np
        E = 16
        K = 2
        D = 256
        F = 176
        B, S = (4, 256)

        def _swiglu(x, wg, wu, wd):
            return jax.nn.silu(x @ wg.T) * (x @ wu.T) @ wd.T
        key = jax.random.key(seed)
        ks = jax.random.split(key, 8)
        sc = 0.02
        return {'x': jax.random.normal(ks[0], (B, S, D), jnp.float32), 'gate_w': jax.random.normal(ks[1], (E, D), jnp.float32) * sc, 'w_gate': jax.random.normal(ks[2], (E, F, D), jnp.float32) * sc, 'w_up': jax.random.normal(ks[3], (E, F, D), jnp.float32) * sc, 'w_down': jax.random.normal(ks[4], (E, D, F), jnp.float32) * sc, 'sw_gate': jax.random.normal(ks[5], (F, D), jnp.float32) * sc, 'sw_up': jax.random.normal(ks[6], (F, D), jnp.float32) * sc, 'sw_down': jax.random.normal(ks[7], (D, F), jnp.float32) * sc, 'expert_bias': jnp.zeros((E,), jnp.float32)}
    _L1_ffn_all = _L1_ffn_setup()
    _L1_ffn_in = {k: v for k, v in _L1_ffn_all.items() if k in ('gate_w', 'w_gate', 'w_up', 'w_down', 'sw_gate', 'sw_up', 'sw_down', 'expert_bias')}
    del _L1_ffn_all
    return {'x': x, 'ctx_2048': ctx_2048, 'mask_BxSx4224_bf0': mask_BxSx4224_bf0, 'L0_attn_wq': _L0_attn_in['wq'], 'L0_attn_bq': _L0_attn_in['bq'], 'L0_attn_wk': _L0_attn_in['wk'], 'L0_attn_bk': _L0_attn_in['bk'], 'L0_attn_wv': _L0_attn_in['wv'], 'L0_attn_bv': _L0_attn_in['bv'], 'L0_attn_wo': _L0_attn_in['wo'], 'L0_attn_bo': _L0_attn_in['bo'], 'L0_xattn_wq': _L0_xattn_in['wq'], 'L0_xattn_wk': _L0_xattn_in['wk'], 'L0_xattn_wv': _L0_xattn_in['wv'], 'L0_xattn_wo': _L0_xattn_in['wo'], 'L0_ffn_W_q': _L0_ffn_in['W_q'], 'L0_ffn_keys': _L0_ffn_in['keys'], 'L0_ffn_down_embed': _L0_ffn_in['down_embed'], 'L0_ffn_up_embed': _L0_ffn_in['up_embed'], 'L0_ffn_gate_w': _L0_ffn_in['gate_w'], 'L0_ffn_up_w': _L0_ffn_in['up_w'], 'L0_ffn_down_w': _L0_ffn_in['down_w'], 'L1_attn_Wq': _L1_attn_in['Wq'], 'L1_attn_Wk': _L1_attn_in['Wk'], 'L1_attn_Wv': _L1_attn_in['Wv'], 'L1_attn_Wo': _L1_attn_in['Wo'], 'L1_xattn_wq': _L1_xattn_in['wq'], 'L1_xattn_bq': _L1_xattn_in['bq'], 'L1_xattn_wkv': _L1_xattn_in['wkv'], 'L1_xattn_bkv': _L1_xattn_in['bkv'], 'L1_xattn_wp': _L1_xattn_in['wp'], 'L1_xattn_bp': _L1_xattn_in['bp'], 'L1_ffn_gate_w': _L1_ffn_in['gate_w'], 'L1_ffn_w_gate': _L1_ffn_in['w_gate'], 'L1_ffn_w_up': _L1_ffn_in['w_up'], 'L1_ffn_w_down': _L1_ffn_in['w_down'], 'L1_ffn_sw_gate': _L1_ffn_in['sw_gate'], 'L1_ffn_sw_up': _L1_ffn_in['sw_up'], 'L1_ffn_sw_down': _L1_ffn_in['sw_down'], 'L1_ffn_expert_bias': _L1_ffn_in['expert_bias']}

def reference(x, ctx_2048, mask_BxSx4224_bf0, L0_attn_wq, L0_attn_bq, L0_attn_wk, L0_attn_bk, L0_attn_wv, L0_attn_bv, L0_attn_wo, L0_attn_bo, L0_xattn_wq, L0_xattn_wk, L0_xattn_wv, L0_xattn_wo, L0_ffn_W_q, L0_ffn_keys, L0_ffn_down_embed, L0_ffn_up_embed, L0_ffn_gate_w, L0_ffn_up_w, L0_ffn_down_w, L1_attn_Wq, L1_attn_Wk, L1_attn_Wv, L1_attn_Wo, L1_xattn_wq, L1_xattn_bq, L1_xattn_wkv, L1_xattn_bkv, L1_xattn_wp, L1_xattn_bp, L1_ffn_gate_w, L1_ffn_w_gate, L1_ffn_w_up, L1_ffn_w_down, L1_ffn_sw_gate, L1_ffn_sw_up, L1_ffn_sw_down, L1_ffn_expert_bias):
    import jax
    import jax.numpy as jnp

    def _L0_attn_ref(x, wq, bq, wk, bk, wv, bv, wo, bo):
        import jax, jax.numpy as jnp
        import numpy as np
        HIDDEN = 256
        HEADS = 16
        HEAD_DIM = HIDDEN // HEADS
        B, S, D = x.shape
        scale = 1.0 / jnp.sqrt(jnp.asarray(HEAD_DIM, x.dtype))

        def split_heads(t):
            return t.reshape(B, S, HEADS, HEAD_DIM).transpose(0, 2, 1, 3)
        q = split_heads(x @ wq + bq)
        k = split_heads(x @ wk + bk)
        v = split_heads(x @ wv + bv)
        scores = jnp.einsum('bhqd,bhkd->bhqk', q, k) * scale
        probs = jax.nn.softmax(scores, axis=-1)
        ctx = jnp.einsum('bhqk,bhkd->bhqd', probs, v)
        ctx = ctx.transpose(0, 2, 1, 3).reshape(B, S, D)
        return ctx @ wo + bo

    def _L0_xattn_ref(x, mask, k_cache, v_cache, wq, wk, wv, wo):
        import jax, jax.numpy as jnp
        import numpy as np
        import math
        DIM = 256
        B, Q_LEN, KV_LEN = (8, 128, 512)
        q = jnp.einsum('bsd,ed->bse', x, wq)
        k_new = jnp.einsum('bsd,ed->bse', x, wk)
        v_new = jnp.einsum('bsd,ed->bse', x, wv)
        k = jnp.concatenate([k_cache, k_new], axis=1)
        v = jnp.concatenate([v_cache, v_new], axis=1)
        scale = 1.0 / math.sqrt(q.shape[-1])
        scores = jnp.einsum('bqd,bkd->bqk', q, k) * scale
        attn = jax.nn.softmax(scores, axis=-1)
        out = jnp.einsum('bqk,bkd->bqd', attn, v)
        return jnp.einsum('bqd,ed->bqe', out, wo)

    def _L0_ffn_ref(hidden_states, W_q, keys, down_embed, up_embed, gate_w, up_w, down_w):
        import jax, jax.numpy as jnp
        import numpy as np
        HIDDEN = 256
        INTER = 1024
        RETRIEVAL = 128
        NUM_EXPERTS = 512
        NUM_KEYS = 64
        TOP_K = 8
        B, S = (4, 256)
        b, s, h = hidden_states.shape
        n = b * s
        queries = (hidden_states @ W_q).reshape(2, n, RETRIEVAL // 2)
        routing = jnp.einsum('tnd,tdk->tnk', queries, keys)
        scores2, idx2 = jax.lax.top_k(routing, TOP_K)
        sx, sy = (scores2[0], scores2[1])
        ix, iy = (idx2[0], idx2[1])
        all_scores = (sx[:, :, None] + sy[:, None, :]).reshape(n, TOP_K * TOP_K)
        all_idx = (ix[:, :, None] * NUM_KEYS + iy[:, None, :]).reshape(n, TOP_K * TOP_K)
        scores, pk = jax.lax.top_k(all_scores, TOP_K)
        indices = jnp.take_along_axis(all_idx, pk, axis=-1)
        de = down_embed[indices]
        ue = up_embed[indices]
        x = hidden_states.reshape(n, h)
        ew = jnp.einsum('nh,nkh->nk', x, de)
        ew = jax.nn.silu(ew) * jax.nn.softmax(scores, axis=-1)
        experts_states = jnp.einsum('nk,nkh->nh', ew, ue).reshape(b, s, h)
        mlp = jax.nn.silu(x @ gate_w) * (x @ up_w) @ down_w
        return mlp.reshape(b, s, h) + experts_states

    def _L1_attn_ref(x, Wq, Wk, Wv, Wo):
        import jax, jax.numpy as jnp
        import numpy as np
        D = 256
        q = jnp.einsum('bsd,ed->bse', x, Wq)
        k = jnp.einsum('bsd,ed->bse', x, Wk)
        v = jnp.einsum('bsd,ed->bse', x, Wv)
        seq = x.shape[-2]
        denom = jnp.sqrt(jnp.float32(x.shape[-1])) / seq
        kvt = jnp.cumsum(k * v, axis=-2) * denom
        vhat = q * kvt
        return jnp.einsum('bse,fe->bsf', vhat, Wo)

    def _L1_xattn_ref(x, cond, wq, bq, wkv, bkv, wp, bp):
        import jax, jax.numpy as jnp
        import numpy as np
        NUM_HEADS = 16

        def _qdq(x):
            s = jnp.maximum(jnp.max(jnp.abs(x), axis=-1, keepdims=True) / 127.0, 1e-08)
            return jnp.clip(jnp.round(x / s), -127.0, 127.0) * s
        B, N, C = x.shape
        M = cond.shape[1]
        H = NUM_HEADS
        Dh = C // H
        q = _qdq(x) @ _qdq(wq).T + bq
        kv = cond @ wkv.T + bkv
        k, v = jnp.split(kv, 2, axis=-1)
        q = q.reshape(B, N, H, Dh)
        k = k.reshape(B, M, H, Dh)
        v = v.reshape(B, M, H, Dh)
        scale = 1.0 / np.sqrt(Dh)
        attn = jax.nn.softmax(jnp.einsum('bnhd,bmhd->bhnm', q, k) * scale, axis=-1)
        o = jnp.einsum('bhnm,bmhd->bnhd', attn, v).reshape(B, N, C)
        out = _qdq(o) @ _qdq(wp).T + bp
        return out

    def _L1_ffn_ref(x, gate_w, w_gate, w_up, w_down, sw_gate, sw_up, sw_down, expert_bias):
        import jax, jax.numpy as jnp
        import numpy as np
        E = 16
        K = 2
        D = 256
        F = 176
        B, S = (4, 256)

        def _swiglu(x, wg, wu, wd):
            return jax.nn.silu(x @ wg.T) * (x @ wu.T) @ wd.T
        b, s, d = x.shape
        flat = x.reshape(-1, d)
        logits = flat @ gate_w.T
        probs = jax.nn.softmax(logits, axis=-1)
        biased = logits + expert_bias
        _, top_idx = jax.lax.top_k(biased, K)
        top_w = jnp.take_along_axis(probs, top_idx, axis=-1)
        top_w = top_w / jnp.sum(top_w, axis=-1, keepdims=True)
        combine = jnp.sum(jax.nn.one_hot(top_idx, E, dtype=flat.dtype) * top_w[..., None], axis=1)
        out = jnp.zeros_like(flat)
        for e in range(E):
            out = out + combine[:, e:e + 1] * _swiglu(flat, w_gate[e], w_up[e], w_down[e])
        out = out + _swiglu(flat, sw_gate, sw_up, sw_down)
        return out.reshape(b, s, d)
    x = _layernorm(x + _L0_attn_ref(x, L0_attn_wq, L0_attn_bq, L0_attn_wk, L0_attn_bk, L0_attn_wv, L0_attn_bv, L0_attn_wo, L0_attn_bo), axis=-1)
    x = _layernorm(x + _L0_xattn_ref(x, mask_BxSx4224_bf0, ctx_2048, ctx_2048, L0_xattn_wq, L0_xattn_wk, L0_xattn_wv, L0_xattn_wo), axis=-1)
    x = _layernorm(x + _L0_ffn_ref(x, L0_ffn_W_q, L0_ffn_keys, L0_ffn_down_embed, L0_ffn_up_embed, L0_ffn_gate_w, L0_ffn_up_w, L0_ffn_down_w), axis=-1)
    x = _layernorm(x + _L1_attn_ref(x, L1_attn_Wq, L1_attn_Wk, L1_attn_Wv, L1_attn_Wo), axis=-1)
    x = _layernorm(x + _L1_xattn_ref(x, ctx_2048, L1_xattn_wq, L1_xattn_bq, L1_xattn_wkv, L1_xattn_bkv, L1_xattn_wp, L1_xattn_bp), axis=-1)
    x = _layernorm(x + _L1_ffn_ref(x, L1_ffn_gate_w, L1_ffn_w_gate, L1_ffn_w_up, L1_ffn_w_down, L1_ffn_sw_gate, L1_ffn_sw_up, L1_ffn_sw_down, L1_ffn_expert_bias), axis=-1)
    return x

_drawn_inputs = setup_inputs


def setup_inputs(seed=0):
    import zlib

    import numpy as np

    out = dict(_drawn_inputs(seed))
    spreads = {'L0_attn_bq': (0.0, 0.8),
     'L0_attn_bk': (0.0, 0.8),
     'L0_attn_bv': (0.0, 0.1),
     'L0_attn_bo': (0.0, 0.1),
     'L1_ffn_expert_bias': (0.0, 0.8)}
    factors = {'L0_attn_wq': 8.0,
     'L0_attn_wk': 8.0,
     'L0_attn_wv': 3.783,
     'L0_ffn_W_q': 8.0,
     'L0_ffn_keys': 8.0,
     'L0_ffn_down_embed': 8.0,
     'L0_ffn_up_embed': 8.0,
     'L1_xattn_wq': 8.0,
     'L1_xattn_bq': 8.0,
     'L1_xattn_bkv': 8.0,
     'L1_xattn_bp': 2.787,
     'L1_ffn_gate_w': 6.161,
     'L1_ffn_w_gate': 5.703,
     'L1_ffn_w_up': 5.645,
     'L1_ffn_w_down': 5.636,
     'L1_ffn_sw_gate': 4.138,
     'L1_ffn_sw_up': 4.069,
     'L1_ffn_sw_down': 4.093}
    for name, (base, spread) in spreads.items():
        noise = np.random.default_rng([zlib.crc32(name.encode()), seed]).standard_normal(out[name].shape)
        drawn = base * np.exp(spread * noise) if base else spread * noise
        out[name] = jnp.asarray(drawn.astype(out[name].dtype))
    for name, factor in factors.items():
        out[name] = (out[name] * factor).astype(out[name].dtype)
    return out
```

```python
from contextlib import ExitStack

import numpy as np
import concourse.bass as bass
from concourse import mybir

P = 128
B, S, D = 8, 256, 256
DC = D // P
TILES = B * S // P
H, HD = 16, 16
CTX = 64
EPS = 1e-5

ALU = mybir.AluOpType
ACT = mybir.ActivationFunctionType
AX = mybir.AxisListType
F32 = mybir.dt.float32
BF16 = mybir.dt.bfloat16
U32 = mybir.dt.uint32


class Lap:

    def __init__(self, n, half, low, looped):
        self.n, self.half, self.low, self.looped, self.par = n, half, low, looped, low % 2

    def back(self, k):
        return Lap(self.n - k, self.half + (self.low - k) // 2 - self.low // 2, self.low - k, self.looped)

    def past(self, k):
        assert self.low >= k or not self.looped, "peel more rounds"
        return self.low >= k

    def count(self, per, k):
        return per * self.n + k

    def landed(self, dmas):
        return 16 * dmas * self.half + 16 * dmas


def laps(eng, steps, start, count=B):
    last = max(max(lags) for _, lags in steps)
    assert (count - start) % 2 == 0 and start >= last

    def one_round(r, lap_of):
        for step, lags in steps:
            args = [lap_of(r - lag) if 0 <= r - lag and (r < start or r - lag < count) else None for lag in lags]
            if any(args):
                step(*args)

    for r in range(start):
        one_round(r, lambda n: Lap(n, n // 2, n, False))
    if count > start:
        with eng.Fori(0, (count - start) // 2) as i:
            for r in (start, start + 1):
                one_round(r, lambda n: Lap(2 * i + n, i + n // 2, n, True))
    for r in range(count, count + last):
        one_round(r, lambda n: Lap(n, n // 2, n, False) if n < count else None)


def apart(c, eng):
    eng.nop(nofuse=True)


class Count:

    def __init__(self, per):
        self.per, self.lap, self.k = per, 0, 0

    def begin(self, lap):
        self.lap, self.k = lap.n, 0

    def one(self):
        self.k += 1
        return 1

    def so_far(self):
        return self.per * self.lap + self.k

    def end(self):
        assert self.k == self.per, (self.k, self.per)


class Chip:

    def __init__(self, nc):
        self.nc = nc
        self.whole = ExitStack()
        self.stack = self.whole

    def sb(self, name, shape, dt=F32):
        return self.stack.enter_context(self.nc.sbuf_tensor(name, shape, dt))

    def psum(self, name, shape=(P, 512), dt=F32):
        return self.stack.enter_context(self.nc.psum_tensor(name, list(shape), dt))

    def sem(self, name):
        return self.whole.enter_context(self.nc.semaphore(name))

    def sems(self, name):
        return [self.sem(f"{name}_even"), self.sem(f"{name}_odd")]


class Norm:
    SUMMED, NORMED, PER = 1, 7, 7
    SCALED, KEPT, POOL_PER = 2, 3, 3

    def __init__(self, c, name, y_bank, y_done, t_bank, residual=None):
        self.c, self.residual = c, residual
        self.y, self.y_done, self.t = y_bank, y_done, t_bank
        self.dve_norm = c.sem(name + "_dve_norm")
        self.pool_scale = c.sem(name + "_pool_scale")
        self.pe_turned = c.sem(name + "_pe_turned")
        self.act_turned = c.sem(name + "_act_turned")
        self.sum = c.sb(name + "_sum", [P, 2, D])
        self.stats = c.sb(name + "_stats", [P, 2, 6])
        self.moments = c.sb(name + "_moments", [P, 2, 2, 2])
        self.spread = c.sb(name + "_spread", [P, 2])
        self.rstd = c.sb(name + "_rstd", [P, 2, 2])
        self.rows = [c.sb(name + f"_rows{p}", [P, 2, D]) for p in range(2)]

    def dve(self, eng):
        chain = Count(self.PER)

        def sum_up(b):
            chain.begin(b)
            mom = self.moments[:, b.par]
            self.y_done(eng, b)
            if b.past(1):
                eng.wait_ge(self.dve_norm, b.back(1).count(self.PER, self.NORMED))
            if self.residual:
                x, ready = self.residual
                ready(eng, b)
            else:
                x = self.c.X[:, bass.ds(2 * D * b.n, 2 * D)].rearrange("p (t d) -> p t d", t=2)
            eng.tensor_tensor(self.sum[:, :, :], self.y, x, ALU.add).then_inc(self.dve_norm, chain.one())
            eng.wait_ge(self.dve_norm, chain.so_far())
            for t in range(2):
                eng.bn_stats(self.stats[:, t, :], self.sum[:, t, :]).then_inc(self.dve_norm, chain.one())
            eng.wait_ge(self.dve_norm, chain.so_far())
            if b.past(2):
                eng.wait_ge(self.pool_scale, b.back(2).count(self.POOL_PER, self.SCALED))
            apart(self.c, eng)
            for t in range(2):
                eng.bn_aggr(mom[:, t, :], self.stats[:, t, :]).then_inc(self.dve_norm, chain.one())
            eng.wait_ge(self.dve_norm, chain.so_far())

        def normalise(b):
            eng.wait_ge(self.pool_scale, b.count(self.POOL_PER, self.SCALED))
            mom = self.moments[:, b.par]
            if b.past(2):
                eng.wait_ge(self.pool_scale, b.back(2).count(self.POOL_PER, self.KEPT))
            if b.past(2):
                eng.wait_ge(self.pe_turned, b.back(2).count(1, 1))
            for t in range(2):
                eng.tensor_scalar(self.rows[b.par][:, t, :], self.sum[:, t, :], mom[:, t, 0:1],
                                  self.rstd[:, b.par, t:t + 1], ALU.subtract, ALU.mult).then_inc(self.dve_norm, chain.one())
            chain.end()
        return sum_up, normalise

    def pool(self, eng):
        chain = Count(self.POOL_PER)

        def step(b):
            chain.begin(b)
            eng.wait_ge(self.dve_norm, b.count(self.PER, 5))
            if b.past(1):
                eng.wait_ge(self.pool_scale, b.back(1).count(self.POOL_PER, self.SCALED))
            apart(self.c, eng)
            eng.tensor_scalar(self.spread[:, :], self.moments[:, b.par, :, 1], EPS, None, ALU.add).then_inc(self.pool_scale, chain.one())
            eng.wait_ge(self.pool_scale, chain.so_far())
            if b.past(2):
                eng.wait_ge(self.dve_norm, b.back(2).count(self.PER, self.NORMED))
            eng.tensor_tensor(self.rstd[:, b.par, :], self.spread[:, :], self.c.minus_half[:, :], ALU.pow).then_inc(self.pool_scale, chain.one())
            eng.wait_ge(self.dve_norm, b.count(self.PER, self.NORMED))
            apart(self.c, eng)
            eng.tensor_copy(self.c.X[:, bass.ds(2 * D * b.n, 2 * D)],
                            self.rows[b.par][:, :, :].rearrange("p t d -> p (t d)")).then_inc(self.pool_scale, chain.one())
            chain.end()
        return step

    def pe(self, eng, bank_free=None):
        def step(b):
            eng.wait_ge(self.dve_norm, b.count(self.PER, self.NORMED))
            if b.past(1):
                eng.wait_ge(self.act_turned, b.back(1).count(1, 1))
            if bank_free:
                bank_free(eng, b)
            for t in range(2):
                for j in range(DC):
                    last = eng.transpose(self.t[:, (2 * j + t) * P:(2 * j + t + 1) * P],
                                         self.rows[b.par][:, t, j * P:(j + 1) * P], self.c.ident[:, :])
            last.then_inc(self.pe_turned, 1)
        return step

    def act(self, eng):
        def step(b):
            eng.wait_ge(self.pe_turned, b.count(1, 1))
            for j in range(DC):
                last = eng.activation(self.c.XT[:, bass.ds(j * B * S + S * b.n, S)], self.t[:, j * S:(j + 1) * S],
                                      ACT.Copy)
            last.then_inc(self.act_turned, 1)
        return step


class Fetch:

    def __init__(self, c, name, readers_done):
        self.c, self.readers_done = c, readers_done
        self.tile = [c.sb(name + f"_x{p}", [P, DC, S]) for p in range(2)]
        self.pool_x = c.sem(name + "_pool_x")

    def pool(self, eng):
        def step(b):
            if b.past(2):
                self.readers_done(eng, b.back(2))
            x = self.c.XT[:, :].rearrange("p (j t) -> p j t", j=DC)[:, :, bass.ds(S * b.n, S)]
            apart(self.c, eng)
            eng.tensor_copy(self.tile[b.par][:, :, :], x).then_inc(self.pool_x, 1)
        return step

    def ready(self, eng, b):
        eng.wait_ge(self.pool_x, b.count(1, 1))




SLOTS = 6
Q_PARTS = (0, 0, 1, 1, 0, 2)
K_PARTS = (0, 1, 0, 1, 2, 0)
MAX_ROW = SLOTS * HD
G = 4
GROUPS = H // G
UNITS = 2 * GROUPS


def load_parts(c, eng, b):
    for dst, src, arrived, slots in ((c.qs, c.d_parts[0], c.q_in, Q_PARTS), (c.ks, c.d_parts[1], c.k_in, K_PARTS)):
        for s, part in enumerate(slots):
            eng.dma_start(dst[b.par][HD * s:HD * s + HD, :, :],
                          src[bass.ds(b.n, 1), part, :, :].rearrange("o (h d) t -> d (o h) t", d=HD)
                          ).then_inc(arrived[b.par], 16)


def project_heads(c):
    nc = c.nc
    with ExitStack() as stack:
        c.stack = stack
        banks = [[c.psum(f"ph_{w}{p}", (P, DC, S)) for p in range(2)] for w in "qk"]
        full = [[c.sb(f"ph_full_{w}{p}", [P, DC, S]) for p in range(2)] for w in "qk"]
        parts = [[c.sb(f"ph_parts_{w}{p}", [P, 3, DC, S], BF16) for p in range(2)] for w in "qk"]
        rest = [c.sb(f"ph_rest_{w}", [P, DC, S]) for w in "qk"]
        pe_proj = c.sem("ph_pe_proj")
        act_full = c.sem("ph_act_full")
        split = [c.sem("ph_dve_split_q"), c.sem("ph_dve_split_k")]
        stored = [c.sems("ph_stored_q"), c.sems("ph_stored_k")]

        with nc.Block() as block:
            @block.tensor
            def _(eng):
                eng.wait_ge(c.in_first, 16 * 2)
                def project(b):
                    for w in range(2):
                        if b.past(2):
                            eng.wait_ge(act_full, b.back(2).count(4, 2 * w + 2))
                        for j in range(DC):
                            for k in range(DC):
                                last = eng.matmul(banks[w][b.par][:, j, :], c.w_qk[w][:, k, j * P:(j + 1) * P],
                                                  c.XT[:, bass.ds(k * B * S + S * b.n, S)],
                                                  start=k == 0, stop=k == DC - 1)
                        last.then_inc(pe_proj, 1)
                laps(eng, [(project, (0,))], 2)

            @block.scalar
            def _(eng):
                def add_bias(b):
                    for w in range(2):
                        eng.wait_ge(pe_proj, b.count(2, w + 1))
                        if b.past(2):
                            eng.wait_ge(split[w], b.back(2).count(4, 4))
                        for j in range(DC):
                            eng.activation(full[w][b.par][:, j, :], banks[w][b.par][:, j, :], ACT.Identity,
                                           bias=c.b_qk[w][:, j:j + 1]).then_inc(act_full, 1)
                laps(eng, [(add_bias, (0,))], 2)

            def splitter(eng, w):
                chain = Count(4)

                def step(b):
                    chain.begin(b)
                    eng.wait_ge(act_full, b.count(4, 2 * w + 2))
                    if b.past(2):
                        eng.wait_ge(stored[w][b.back(2).par], b.back(2).landed(1))
                    if b.past(1):
                        eng.wait_ge(split[w], b.back(1).count(4, 4))
                    src, dst, left = full[w][b.par][:, :, :], parts[w][b.par], rest[w][:, :, :]
                    apart(c, eng)
                    eng.tensor_copy(dst[:, 0], src).then_inc(split[w], chain.one())
                    eng.wait_ge(split[w], chain.so_far())
                    eng.tensor_tensor(left, src, dst[:, 0], ALU.subtract).then_inc(split[w], chain.one())
                    eng.wait_ge(split[w], chain.so_far())
                    apart(c, eng)
                    eng.tensor_copy(dst[:, 1], left).then_inc(split[w], chain.one())
                    eng.wait_ge(split[w], chain.so_far())
                    eng.tensor_tensor(dst[:, 2], left, dst[:, 1], ALU.subtract).then_inc(split[w], chain.one())
                    chain.end()
                return step

            @block.vector
            def _(eng):
                laps(eng, [(splitter(eng, 0), (0,)), (splitter(eng, 1), (0,))], 2)

            @block.gpsimd
            def _(eng):
                fills = [fill for p in range(2) for fill in (
                    (c.qs[p][MAX_ROW:P, :, :], 0.0), (c.ks[p][MAX_ROW:P, :, :], 0.0), (c.ks[p][MAX_ROW:MAX_ROW + 2, :, :], 1.0),
                    (c.v[p][:, :, :, HD:HD + 1], 1.0), (c.v[p][:, :, :, HD + 1:], 0.0))]
                for n, (place, value) in enumerate(fills):
                    eng.memset(place, value).then_inc(c.operands_init, 1)
                    eng.wait_ge(c.operands_init, n + 1)

            @block.sync
            def _(eng):
                def store(b):
                    for w in range(2):
                        eng.wait_ge(split[w], b.count(4, 4))
                        eng.dma_start(c.d_parts[w][bass.ds(b.n, 1)].rearrange("o c (j p) t -> p (o c j) t", p=P),
                                      parts[w][b.par][:, :, :, :].rearrange("p c j t -> p (c j) t")
                                      ).then_inc(stored[w][b.par], 16)
                for b in range(2):
                    store(Lap(b, 0, b, False))
                eng.wait_ge(c.operands_init, 10)
                for b in range(2):
                    for w in range(2):
                        eng.wait_ge(stored[w][b], 16)
                    load_parts(c, eng, Lap(b, 0, b, False))
                laps(eng, [(lambda b: b.past(2) and store(b), (0,))], 2)
                for w in range(2):
                    for p in range(2):
                        eng.wait_ge(stored[w][p], 16 * (B // 2))


def attention(c):
    nc = c.nc
    with ExitStack() as stack:
        c.stack = stack
        bank_row = c.psum("at_row", (P, G, S))
        bank_col = c.psum("at_col", (P, G, S))
        bank_a = c.psum("at_a")
        bank_b = c.psum("at_b")
        bank_o = c.psum("at_o", (P, 2, S))
        bank_y = c.psum("at_y", (P, 2, D))
        turned_max_ps = bank_b[:, 0:P].bitcast(BF16)
        qs, ks, v = c.qs, c.ks, c.v
        probs = [c.sb(f"at_probs{p}", [P, 2, G, S]) for p in range(2)]
        neg_max = c.sb("at_neg_max", [P, 2, H])
        max_parts = c.sb("at_max_parts", [P, 2, 2, H], BF16)
        turned_max = c.sb("at_turned_max", [2 * H, S], BF16)
        o_raw = [c.sb(f"at_o_raw{p}", [P, 2, S]) for p in range(2)]
        squares, divided = c.sb("at_squares", [P, 2 * S]), c.sb("at_divided", [P, 2 * S])
        recip = c.sb("at_recip", [P, S // HD])
        o_t = c.sb("at_o_t", [P, GROUPS, S])

        q_in, k_in = c.q_in, c.k_in
        max_in = c.sems("at_max_in")
        pe_v, dve_v = c.sem("at_pe_v"), c.sem("at_dve_v")
        MAX_PER = UNITS + 2
        pe_row, dve_max = c.sem("at_pe_row"), c.sem("at_dve_max")
        pe_max, act_max = c.sem("at_pe_max"), c.sem("at_act_max")
        pe_col, act_exp = c.sem("at_pe_col"), c.sem("at_act_exp")
        pe_pv, act_o = c.sem("at_pe_pv"), c.sem("at_act_o")
        dve_div, DIV = c.sem("at_dve_div"), 8
        pe_y = c.sem("at_pe_y")
        norm = Norm(c, "n1", bank_y[:, :, :], lambda eng, b: eng.wait_ge(pe_y, b.count(1, 1)), bank_a)
        fetch = Fetch(c, "at", lambda eng, b: eng.wait_ge(pe_v, b.count(1, 1)))

        with nc.Block() as block:
            @block.tensor
            def _(eng):
                def rows_unit(b, u):
                    g, t = divmod(u, 2)
                    if u == 0:
                        eng.wait_ge(q_in[b.par], b.landed(SLOTS))
                        eng.wait_ge(k_in[b.par], b.landed(SLOTS))
                        if b.past(1):
                            eng.wait_ge(dve_max, b.back(1).count(MAX_PER, UNITS))
                    else:
                        eng.wait_ge(dve_max, b.count(MAX_PER, u))
                    for i in range(G):
                        h = G * g + i
                        last = eng.matmul(bank_row[:, i, :], qs[b.par][0:MAX_ROW, h, t * P:(t + 1) * P],
                                          ks[b.par][0:MAX_ROW, h, :], start=True, stop=True)
                    last.then_inc(pe_row, 1)

                def cols_unit(b, u):
                    g, t = divmod(u, 2)
                    if u == 0:
                        eng.wait_ge(max_in[b.par], b.landed(2))
                        if b.past(1):
                            eng.wait_ge(act_exp, b.back(1).count(UNITS, UNITS))
                    else:
                        eng.wait_ge(act_exp, b.count(UNITS, u))
                    for i in range(G):
                        h = G * g + i
                        last = eng.matmul(bank_col[:, i, :], ks[b.par][:, h, t * P:(t + 1) * P],
                                          qs[b.par][:, h, :], start=True, stop=True)
                    last.then_inc(pe_col, 1)

                def pv(b, g):
                    eng.wait_ge(act_exp, b.count(UNITS, 2 * g + 2))
                    if g == 0:
                        eng.wait_ge(dve_v, b.count(1, 1))
                        if b.past(1):
                            eng.wait_ge(act_o, b.back(1).count(2, 2))
                    elif g == 2:
                        eng.wait_ge(act_o, b.count(2, 1))
                    for t in range(2):
                        for i in range(G):
                            last = eng.matmul(bank_o[32 * i:32 * i + 32, g % 2, :], v[b.par][:, t, G * g + i, :],
                                              probs[g % 2][:, t, i, :], start=t == 0, stop=t == 1)
                    last.then_inc(pe_pv, 1)

                def scores(a, b):
                    for u in range(UNITS):
                        if a:
                            rows_unit(a, u)
                        if b:
                            cols_unit(b, u)
                            if u in (2, 4, 6):
                                pv(b, u // 2 - 1)
                    if b:
                        pv(b, GROUPS - 1)

                def project_v(b):
                    fetch.ready(eng, b)
                    if b.past(1):
                        eng.wait_ge(dve_v, b.back(1).count(1, 1))
                    if b.past(3):
                        eng.wait_ge(norm.act_turned, b.back(3).count(1, 1))
                    for t in range(2):
                        for k in range(DC):
                            last = eng.matmul(bank_a[:, t * D:(t + 1) * D], fetch.tile[b.par][:, k, t * P:(t + 1) * P],
                                              c.w_v[:, k, :], start=k == 0, stop=k == DC - 1)
                    last.then_inc(pe_v, 1)

                def turn_max(b):
                    eng.wait_ge(dve_max, b.count(MAX_PER, MAX_PER))
                    if b.past(1):
                        eng.wait_ge(act_max, b.back(1).count(1, 1))
                    for t in range(2):
                        last = eng.transpose(turned_max_ps[0:2 * H, t * P:(t + 1) * P],
                                             max_parts[:, t, :, :].rearrange("p c h -> p (c h)"), c.ident_b[:, :])
                    last.then_inc(pe_max, 1)

                def out(b):
                    eng.wait_ge(dve_div, b.count(DIV, DIV))
                    if b.past(1):
                        eng.wait_ge(norm.dve_norm, b.back(1).count(norm.PER, norm.SUMMED))
                    for t in range(2):
                        for g in range(GROUPS):
                            last = eng.matmul(bank_y[:, t, :], o_t[:, g, t * P:(t + 1) * P], c.w_o[:, g, :],
                                              start=g == 0, stop=g == GROUPS - 1)
                    last.then_inc(pe_y, 1)

                def turn(a, b):
                    if b:
                        if a:
                            eng.wait_ge(dve_v, a.count(1, 1))
                        turn_rows(b)
                turn_rows = norm.pe(eng)
                laps(eng, [(scores, (0, 1)), (turn_max, (0,)), (project_v, (0,)), (out, (1,)), (turn, (0, 2))], 4)

            @block.scalar
            def _(eng):
                def exps_and_o(b):
                    for u in range(UNITS):
                        g, t = divmod(u, 2)
                        eng.wait_ge(pe_col, b.count(UNITS, u + 1))
                        if g < 2:
                            if b.past(1):
                                eng.wait_ge(pe_pv, b.back(1).count(GROUPS, g + 3))
                        else:
                            eng.wait_ge(pe_pv, b.count(GROUPS, g - 1))
                        eng.activation(probs[g % 2][:, t, :, :].rearrange("p g t -> p (g t)"),
                                       bank_col[:, :, :].rearrange("p g t -> p (g t)"), ACT.Exp,
                                       scale=HD ** -0.5).then_inc(act_exp, 1)
                        if u == 4:
                            evacuate_o(b, 0)
                    evacuate_o(b, 1)

                def evacuate_o(b, half):
                    eng.wait_ge(pe_pv, b.count(GROUPS, 2 * half + 2))
                    if b.past(1):
                        eng.wait_ge(dve_div, b.back(1).count(DIV, 4 * half + 1))
                    eng.activation(o_raw[half][:, :, :], bank_o[:, :, :], ACT.Copy).then_inc(act_o, 1)

                def keep_max(b):
                    eng.wait_ge(pe_max, b.count(1, 1))
                    if b.past(1):
                        eng.wait_ge(max_in[b.back(1).par], b.back(1).landed(2))
                    eng.activation(turned_max[:, :], turned_max_ps[0:2 * H, 0:S], ACT.Copy).then_inc(act_max, 1)

                laps(eng, [(exps_and_o, (1,)), (keep_max, (0,)), (norm.act(eng), (2,))], 4)

            @block.vector
            def _(eng):
                chain = Count(DIV)

                def max_unit(b, u):
                    g, t = divmod(u, 2)
                    eng.wait_ge(pe_row, b.count(UNITS, u + 1))
                    if u == 0:
                        if b.past(1):
                            eng.wait_ge(dve_max, b.back(1).count(MAX_PER, MAX_PER))
                    eng.tensor_reduce(neg_max[:, t, G * g:G * g + G], bank_row[:, :, :], AX.X, ALU.max,
                                      negate=True).then_inc(dve_max, 1)

                def max_in_parts(b):
                    eng.wait_ge(dve_max, b.count(MAX_PER, UNITS))
                    if b.past(1):
                        eng.wait_ge(pe_max, b.back(1).count(1, 1))
                    eng.tensor_copy(max_parts[:, :, 0, :], neg_max[:, :, :]).then_inc(dve_max, 1)
                    eng.wait_ge(dve_max, b.count(MAX_PER, UNITS + 1))
                    eng.tensor_tensor(max_parts[:, :, 1, :], neg_max[:, :, :], max_parts[:, :, 0, :],
                                      ALU.subtract).then_inc(dve_max, 1)

                def divide(b, half):
                    if half == 0:
                        chain.begin(b)
                    eng.wait_ge(act_o, b.count(2, half + 1))
                    if half:
                        eng.wait_ge(dve_div, chain.so_far())
                    elif b.past(1):
                        eng.wait_ge(dve_div, b.back(1).count(DIV, DIV))
                    apart(c, eng)
                    eng.transpose(squares[:, :], o_raw[half][:, :, :].rearrange("p g t -> p (g t)")
                                  ).then_inc(dve_div, chain.one())
                    eng.wait_ge(dve_div, chain.so_far())
                    rows = squares[:, :].rearrange("p (q d) -> p q d", d=2 * HD)
                    apart(c, eng)
                    eng.reciprocal(recip[:, :], rows[:, :, HD]).then_inc(dve_div, chain.one())
                    eng.wait_ge(dve_div, chain.so_far())
                    eng.tensor_tensor(divided[:, :].rearrange("p (q d) -> p q d", d=2 * HD), rows,
                                      recip[:, :].unsqueeze(2).broadcast_to([P, 2 * S // (2 * HD), 2 * HD]),
                                      ALU.mult).then_inc(dve_div, chain.one())
                    eng.wait_ge(dve_div, chain.so_far())
                    if half == 0:
                        if b.past(1):
                            eng.wait_ge(pe_y, b.back(1).count(1, 1))
                    apart(c, eng)
                    eng.transpose(o_t[:, 2 * half:2 * half + 2, :].rearrange("p g t -> p (g t)"), divided[:, :]
                                  ).then_inc(dve_div, chain.one())
                    if half == 1:
                        chain.end()

                sum_up, normalise = norm.dve(eng)

                def main(a, b, z):
                    for u in range(UNITS):
                        if a:
                            max_unit(a, u)
                        if z and u == 1:
                            sum_up(z)
                        if z and u == 4:
                            normalise(z)
                        if b and u == 6:
                            divide(b, 0)
                    if a:
                        max_in_parts(a)
                    if b:
                        divide(b, 1)

                def add_bias_v(b):
                    eng.wait_ge(pe_v, b.count(1, 1))
                    if b.past(2):
                        eng.wait_ge(pe_pv, b.back(2).count(GROUPS, GROUPS))
                    eng.tensor_tensor(v[b.par][:, :, :, 0:HD].rearrange("p t h d -> p (t h) d"),
                                      bank_a[:, :].rearrange("p (q d) -> p q d", d=HD),
                                      c.bv_twice[:, :].rearrange("p (q d) -> p q d", d=HD),
                                      ALU.add).then_inc(dve_v, 1)

                laps(eng, [(main, (0, 1, 2)), (add_bias_v, (0,))], 4)

            @block.gpsimd
            def _(eng):
                laps(eng, [(fetch.pool(eng), (0,)), (norm.pool(eng), (2,))], 4)

            @block.sync
            def _(eng):
                eng.wait_ge(c.in_x, 16 * 3)
                c.load_packs(eng)

                def load(b):
                    if b.past(2):
                        eng.wait_ge(pe_col, b.back(2).count(UNITS, UNITS))
                    load_parts(c, eng, b)

                def load_max(b):
                    eng.wait_ge(act_max, b.count(1, 1))
                    for part in range(2):
                        eng.dma_start(qs[b.par][MAX_ROW + part:MAX_ROW + part + 1, :, :],
                                      turned_max[H * part:H * part + H, :]).then_inc(max_in[b.par], 16)

                laps(eng, [(lambda b: b.past(2) and load(b), (0,)), (load_max, (0,))], 4)
                eng.wait_ge(c.in_packs, 16 * 4)




def context_attention(c):
    nc = c.nc
    KEYS = S + CTX
    with ExitStack() as stack:
        c.stack = stack
        bank_q, bank_k = c.psum("ca_q", (P, DC, S)), c.psum("ca_k", (P, DC, S))
        bank_vo = c.psum("ca_vo", (P, 2, D))
        bank_s = [c.psum(f"ca_s{t}") for t in range(2)]
        bank_t = [c.psum(f"ca_t{t}") for t in range(2)]
        bank_y = c.psum("ca_y", (P, 2, D))
        q = [c.sb(f"ca_qT{p}", [P, DC, S]) for p in range(2)]
        k = [c.sb(f"ca_kT{p}", [P, DC, KEYS]) for p in range(2)]
        v = [c.sb(f"ca_v{p}", [P, 2, D]) for p in range(2)]
        v_ctx = [c.sb(f"ca_vctx{p}", [CTX, D]) for p in range(2)]
        probs = [c.sb(f"ca_probs{p}", [P, 2, KEYS]) for p in range(2)]
        neg_max, bias = c.sb("ca_neg_max", [P, 2]), c.sb("ca_bias", [P, 2])
        total, recip = c.sb("ca_total", [P, 2]), c.sb("ca_recip", [P, 2])
        probs_t = c.sb("ca_probs_t", [P, 3, S])
        o_t = c.sb("ca_o_t", [P, DC, S])

        pe_proj, act_qk, dve_v = c.sem("ca_pe_proj"), c.sem("ca_act_qk"), c.sem("ca_dve_v")
        k_ctx_in, v_ctx_in = c.sems("ca_k_ctx_in"), c.sems("ca_v_ctx_in")
        pe_scores, act_exp = c.sem("ca_pe_scores"), c.sem("ca_act_exp")
        SOFT_PER = 6
        dve_soft = c.sem("ca_dve_soft")
        pe_turn_p, act_turn_p = c.sem("ca_pe_turn_p"), c.sem("ca_act_turn_p")
        pe_pv, act_o, pe_y = c.sem("ca_pe_pv"), c.sem("ca_act_o"), c.sem("ca_pe_y")
        norm = Norm(c, "n2", bank_y[:, :, :], lambda eng, b: eng.wait_ge(pe_y, b.count(1, 1)),
                    bank_q[:, :, :].rearrange("p j t -> p (j t)"))
        fetch = Fetch(c, "ca", lambda eng, b: eng.wait_ge(pe_proj, b.count(3, 3)))

        with nc.Block() as block:
            @block.tensor
            def _(eng):
                def project(b):
                    x = fetch.tile[b.par]
                    fetch.ready(eng, b)
                    for w, bank, weights in ((0, bank_q, c.x0_q), (1, bank_k, c.x0_k)):
                        if w == 0:
                            if b.past(3):
                                eng.wait_ge(norm.act_turned, b.back(3).count(1, 1))
                        if b.past(1):
                            eng.wait_ge(act_qk, b.back(1).count(2, w + 1))
                        for j in range(DC):
                            for i in range(DC):
                                last = eng.matmul(bank[:, j, :], weights[:, i, j * P:(j + 1) * P], x[:, i, :],
                                                  start=i == 0, stop=i == DC - 1)
                        last.then_inc(pe_proj, 1)
                    if b.past(2):
                        eng.wait_ge(act_o, b.back(2).count(1, 1))
                    if b.past(1):
                        eng.wait_ge(dve_v, b.back(1).count(1, 1))
                    for t in range(2):
                        for i in range(DC):
                            last = eng.matmul(bank_vo[:, t, :], x[:, i, t * P:(t + 1) * P], c.x0_v[:, i, :],
                                              start=i == 0, stop=i == DC - 1)
                    last.then_inc(pe_proj, 1)

                def turn_probs(b):
                    for t in range(2):
                        eng.wait_ge(dve_soft, b.count(SOFT_PER, 5 + t))
                        if b.past(1):
                            eng.wait_ge(act_turn_p, b.back(1).count(2, t + 1))
                        for i, n in enumerate((P, P, CTX)):
                            last = eng.transpose(bank_t[t][0:n, i * P:(i + 1) * P],
                                                 probs[b.par][:, t, i * P:i * P + n], c.ident[:, :])
                        last.then_inc(pe_turn_p, 1)

                def score(b):
                    eng.wait_ge(act_qk, b.count(2, 2))
                    eng.wait_ge(k_ctx_in[b.par], b.landed(1))
                    for t in range(2):
                        if b.past(1):
                            eng.wait_ge(act_exp, b.back(1).count(2, t + 1))
                        for i in range(DC):
                            last = eng.matmul(bank_s[t][:, 0:KEYS], q[b.par][:, i, t * P:(t + 1) * P],
                                              k[b.par][:, i, :], start=i == 0, stop=i == DC - 1)
                        last.then_inc(pe_scores, 1)

                def pv(a, b):
                    if not b:
                        return
                    eng.wait_ge(dve_v, b.count(1, 1))
                    if a:
                        eng.wait_ge(dve_v, a.count(1, 1))
                    eng.wait_ge(v_ctx_in[b.par], b.landed(1))
                    eng.wait_ge(act_turn_p, b.count(2, 2))
                    for j in range(DC):
                        cols = slice(j * P, (j + 1) * P)
                        for i in range(2):
                            eng.matmul(bank_vo[:, j, :], v[b.par][:, i, cols], probs_t[:, i, :], start=i == 0, stop=False)
                        last = eng.matmul(bank_vo[:, j, :], v_ctx[b.par][:, cols], probs_t[0:CTX, 2, :],
                                          start=False, stop=True)
                    last.then_inc(pe_pv, 1)

                def turn(a, b):
                    if b:
                        if a:
                            eng.wait_ge(act_qk, a.count(2, 1))
                        turn_rows(b)
                turn_rows = norm.pe(eng)

                def out(b):
                    eng.wait_ge(act_o, b.count(1, 1))
                    if b.past(1):
                        eng.wait_ge(norm.dve_norm, b.back(1).count(norm.PER, norm.SUMMED))
                    for t in range(2):
                        for i in range(DC):
                            last = eng.matmul(bank_y[:, t, :], o_t[:, i, t * P:(t + 1) * P], c.x0_o[:, i, :],
                                              start=i == 0, stop=i == DC - 1)
                    last.then_inc(pe_y, 1)

                laps(eng, [(project, (0,)), (turn_probs, (1,)), (score, (0,)), (pv, (0, 1)), (turn, (0, 2)),
                           (out, (1,))], 4)

            @block.scalar
            def _(eng):
                def keep_qk(b):
                    for w, bank, dst in ((0, bank_q, q), (1, bank_k, k)):
                        eng.wait_ge(pe_proj, b.count(3, w + 1))
                        if b.past(2):
                            eng.wait_ge(pe_scores, b.back(2).count(2, 2))
                        eng.activation(dst[b.par][:, :, 0:S], bank[:, :, :], ACT.Copy).then_inc(act_qk, 1)

                def keep_probs(b):
                    for t in range(2):
                        eng.wait_ge(pe_turn_p, b.count(2, t + 1))
                        if b.past(1):
                            eng.wait_ge(pe_pv, b.back(1).count(1, 1))
                        cols = slice(t * P, (t + 1) * P)
                        eng.activation(probs_t[:, 0:2, cols], bank_t[t][:, 0:2 * P].rearrange("p (i t) -> p i t", i=2),
                                       ACT.Copy)
                        eng.activation(probs_t[0:CTX, 2, cols], bank_t[t][0:CTX, 2 * P:3 * P],
                                       ACT.Copy).then_inc(act_turn_p, 1)

                def exps(b):
                    for t in range(2):
                        eng.wait_ge(dve_soft, b.count(SOFT_PER, 3))
                        if b.past(2):
                            eng.wait_ge(pe_turn_p, b.back(2).count(2, t + 1))
                        if b.past(1):
                            eng.wait_ge(dve_soft, b.back(1).count(SOFT_PER, 4))
                        eng.activation(probs[b.par][:, t, :], bank_s[t][:, 0:KEYS], ACT.Exp, bias=bias[:, t:t + 1],
                                       scale=D ** -0.5, accum_out=total[:, t:t + 1]).then_inc(act_exp, 1)

                def keep_o(b):
                    eng.wait_ge(pe_pv, b.count(1, 1))
                    if b.past(1):
                        eng.wait_ge(pe_y, b.back(1).count(1, 1))
                    eng.activation(o_t[:, :, :], bank_vo[:, :, :], ACT.Copy).then_inc(act_o, 1)

                laps(eng, [(keep_qk, (0,)), (keep_probs, (1,)), (exps, (0,)), (keep_o, (1,)),
                           (norm.act(eng), (2,))], 4)

            @block.vector
            def _(eng):
                chain = Count(SOFT_PER)

                def keep_v(b):
                    eng.wait_ge(pe_proj, b.count(3, 3))
                    if b.past(2):
                        eng.wait_ge(pe_pv, b.back(2).count(1, 1))
                    eng.tensor_copy(v[b.par][:, :, :], bank_vo[:, :, :]).then_inc(dve_v, 1)

                def soften(b):
                    chain.begin(b)
                    if b.past(1):
                        eng.wait_ge(dve_soft, b.back(1).count(SOFT_PER, SOFT_PER))
                    for t in range(2):
                        eng.wait_ge(pe_scores, b.count(2, t + 1))
                        eng.tensor_reduce(neg_max[:, t:t + 1], bank_s[t][:, 0:KEYS], AX.X, ALU.max,
                                          negate=True).then_inc(dve_soft, chain.one())
                    eng.wait_ge(dve_soft, chain.so_far())
                    if b.past(1):
                        eng.wait_ge(act_exp, b.back(1).count(2, 2))
                    eng.tensor_scalar(bias[:, :], neg_max[:, :], D ** -0.5, None, ALU.mult).then_inc(dve_soft, chain.one())
                    eng.wait_ge(act_exp, b.count(2, 2))
                    eng.reciprocal(recip[:, :], total[:, :]).then_inc(dve_soft, chain.one())
                    eng.wait_ge(dve_soft, chain.so_far())
                    for t in range(2):
                        eng.tensor_scalar(probs[b.par][:, t, :], probs[b.par][:, t, :], recip[:, t:t + 1],
                                          None, ALU.mult).then_inc(dve_soft, chain.one())
                    chain.end()

                laps(eng, [(keep_v, (0,)), (soften, (0,)), *((step, (1,)) for step in norm.dve(eng))], 4)

            @block.gpsimd
            def _(eng):
                laps(eng, [(fetch.pool(eng), (0,)), (norm.pool(eng), (2,))], 4)

            @block.sync
            def _(eng):
                def load(b):
                    if b.past(2):
                        eng.wait_ge(pe_scores, b.back(2).count(2, 2))
                    eng.dma_start(k[b.par][:, :, S:KEYS], c.d_ctx_t[bass.ds(b.n, 1)].rearrange("o p j k -> p (o j) k")
                                  ).then_inc(k_ctx_in[b.par], 16)
                    if b.past(2):
                        eng.wait_ge(pe_pv, b.back(2).count(1, 1))
                    eng.dma_start(v_ctx[b.par][:, :], c.d_ctx[bass.ds(b.n, 1)].rearrange("o k d -> k (o d)")
                                  ).then_inc(v_ctx_in[b.par], 16)
                laps(eng, [(load, (0,))], 2)




TOP = 8
EXPERTS = 512
NKEYS = 64
RETR = 128
INTER = 1024
EB = EXPERTS // P
FB = INTER // P
LOWEST = -3.0e38


def route_scores(c):
    nc = c.nc
    with ExitStack() as stack:
        c.stack = stack
        bank_q = [c.psum(f"rt_q{p}", (P, S)) for p in range(2)]
        bank_r = [c.psum(f"rt_r{p}", (P, 2, P)) for p in range(2)]
        q = [c.sb(f"rt_q_sb{p}", [P, S]) for p in range(2)]
        with nc.Block() as block:
            sems = [[c.sem(f"rt_{n}{t}") for n in ("pe_q", "act_q", "pe_r", "dve_r")] for t in range(2)]

            @block.tensor
            def _(eng):
                for table in range(2):
                    pe_q, act_q, pe_r, dve_r = sems[table]

                    def queries(b):
                        if b.past(2):
                            eng.wait_ge(act_q, b.back(2).count(1, 1))
                        for i in range(DC):
                            last = eng.matmul(bank_q[b.par][:, :], c.w_query[:, i, :],
                                              c.XT[:, bass.ds(i * B * S + S * b.n + table * (B // 2) * S, S)],
                                              start=i == 0, stop=i == DC - 1)
                        last.then_inc(pe_q, 1)

                    def scores(b):
                        eng.wait_ge(act_q, b.count(1, 1))
                        if b.past(2):
                            eng.wait_ge(dve_r, b.back(2).count(1, 1))
                        for t in range(2):
                            last = eng.matmul(bank_r[b.par][:, t, :], q[b.par][:, t * P:(t + 1) * P],
                                              c.keys[:, table, :], start=True, stop=True)
                        last.then_inc(pe_r, 1)
                    if table:
                        eng.wait_ge(sems[0][1], B // 2)
                        eng.wait_ge(sems[0][3], B // 2)
                    laps(eng, [(queries, (0,)), (scores, (1,))], 4, B // 2)

            @block.scalar
            def _(eng):
                for table in range(2):
                    pe_q, act_q, pe_r, dve_r = sems[table]

                    def keep(b):
                        eng.wait_ge(pe_q, b.count(1, 1))
                        if b.past(2):
                            eng.wait_ge(pe_r, b.back(2).count(1, 1))
                        if table:
                            eng.wait_ge(sems[0][2], B // 2)
                        eng.activation(q[b.par][:, :], bank_q[b.par][:, :], ACT.Copy).then_inc(act_q, 1)
                    laps(eng, [(keep, (0,))], 4, B // 2)

            @block.vector
            def _(eng):
                for table in range(2):
                    pe_q, act_q, pe_r, dve_r = sems[table]

                    def keep(b):
                        eng.wait_ge(pe_r, b.count(1, 1))
                        eng.tensor_copy(c.R[:, bass.ds(2 * P * b.n + table * B * P, 2 * P)],
                                        bank_r[b.par][:, :, :].rearrange("p t k -> p (t k)")).then_inc(dve_r, 1)
                    laps(eng, [(keep, (0,))], 4, B // 2)


def feed_forward(c):
    nc = c.nc
    with ExitStack() as stack:
        c.stack = stack
        bank_u = [c.psum(f"ff_u{p}", (P, 2, S)) for p in range(2)]
        bank_w = [c.psum(f"ff_w{p}", (P, 2, 2, P)) for p in range(2)]
        bank_y, bank_t = c.psum("ff_y", (P, 2, D)), c.psum("ff_t")
        rt = [c.sb(f"ff_rt{p}", [P, 2, 2, NKEYS]) for p in range(2)]
        best, best_i = c.sb("ff_best", [P, 2, 2, TOP]), c.sb("ff_best_i", [P, 2, 2, TOP], U32)
        best_f = c.sb("ff_best_f", [P, 2, 2, TOP])
        neg_best = c.sb("ff_neg_best", [P, 2, 2])
        sums, left = c.sb("ff_sums", [P, 2, TOP, TOP]), c.sb("ff_left", [P, 2, TOP, TOP])
        top, neg_top = c.sb("ff_top", [P, 2, TOP]), c.sb("ff_neg_top", [P, 2])
        taken, count = c.sb("ff_taken", [P, 2, TOP, TOP]), c.sb("ff_count", [P, 2, TOP])
        stairs, stair = c.sb("ff_stairs", [P, 2, TOP, TOP]), c.sb("ff_stair", [P, 2, TOP])
        places, rank = c.sb("ff_places", [P, 2, NKEYS, TOP]), c.sb("ff_rank", [P, 2, NKEYS])
        e_first, e_second = c.sb("ff_e_first", [P, 2, TOP]), c.sb("ff_e_second", [P, 2, NKEYS])
        e_top, total, r_total = c.sb("ff_e_top", [P, TOP]), c.sb("ff_total", [P, 2]), c.sb("ff_r_total", [P, 2])
        scaled = c.sb("ff_scaled", [P, 2, TOP])
        chosen = c.sb("ff_chosen", [P, 2, TOP, NKEYS])
        weight = [c.sb(f"ff_weight{p}", [P, 2, EXPERTS]) for p in range(2)]
        inside, outside = c.sb("ff_inside", [P, 2]), c.sb("ff_outside", [P, 2])
        act = [c.sb(f"ff_act{p}", [P, 2, S]) for p in range(2)]
        hidden = c.sb("ff_hidden", [P, FB + EB, S])

        UNITS_F = EB // 2 + FB
        pool_rt = c.sem("ff_pool_rt")
        BEST, TOP_SUMS, CHOSEN, SCALED, WEIGHT = 10, 16, 26, 28, 30
        dve_route, act_route = c.sem("ff_dve_route"), c.sem("ff_act_route")
        pool_weight = c.sem("ff_pool_weight")
        pe_w, pe_u, act_u, dve_u = c.sem("ff_pe_w"), c.sem("ff_pe_u"), c.sem("ff_act_u"), c.sem("ff_dve_u")
        pe_y = c.sem("ff_pe_y")
        norm = Norm(c, "n3", bank_y[:, :, :], lambda eng, b: eng.wait_ge(pe_y, b.count(1, 1)), bank_t)

        with nc.Block() as block:
            @block.tensor
            def _(eng):
                def turn_weights(b):
                    eng.wait_ge(dve_route, b.count(WEIGHT, WEIGHT))
                    if b.past(1):
                        eng.wait_ge(dve_u, b.back(1).count(UNITS_F, UNITS_F))
                    for e in range(EB):
                        for j in range(2):
                            last = eng.transpose(bank_w[e // 2][:, e % 2, j, :],
                                                 weight[b.par][:, j, e * P:(e + 1) * P], c.ident[:, :])
                    last.then_inc(pe_w, 1)

                def units(b):
                    for u in range(UNITS_F):
                        if u < 2:
                            if b.past(1):
                                eng.wait_ge(dve_u, b.back(1).count(UNITS_F, UNITS_F - 1 + u))
                        else:
                            eng.wait_ge(dve_u, b.count(UNITS_F, u - 1))
                        for w in range(2):
                            if u < FB:
                                weights, col = (c.f_gate, c.f_up)[w], u * P
                            else:
                                weights, col = c.w_down_embed, (2 * (u - FB) + w) * P
                            for i in range(DC):
                                last = eng.matmul(bank_u[u % 2][:, w, :], weights[:, i, col:col + P],
                                                  c.XT[:, bass.ds(i * B * S + S * b.n, S)],
                                                  start=i == 0, stop=i == DC - 1)
                        last.then_inc(pe_u, 1)
                        if u == FB - 2:
                            turn_weights(b)

                def down(b):
                    if b.past(1):
                        eng.wait_ge(norm.dve_norm, b.back(1).count(norm.PER, norm.SUMMED))
                    for t in range(2):
                        for k in range(FB + EB):
                            if t == 0:
                                eng.wait_ge(dve_u, b.count(UNITS_F, k + 1 if k < FB else FB + (k - FB) // 2 + 1))
                            weights = c.f_down[:, k, :] if k < FB else c.w_up_embed[:, k - FB, :]
                            last = eng.matmul(bank_y[:, t, :], hidden[:, k, t * P:(t + 1) * P], weights,
                                              start=k == 0, stop=k == FB + EB - 1)
                    last.then_inc(pe_y, 1)

                laps(eng, [(units, (1,)), (norm.pe(eng), (2,)), (down, (1,))], 4)

            @block.scalar
            def _(eng):
                def exps(b):
                    eng.wait_ge(dve_route, b.count(WEIGHT, BEST))
                    for j in range(2):
                        if b.past(1):
                            eng.wait_ge(dve_route, b.back(1).count(WEIGHT, SCALED))
                        eng.activation(e_first[:, j, :], rt[b.par][:, 0, j, 0:TOP], ACT.Exp,
                                       bias=neg_best[:, 0, j:j + 1]).then_inc(act_route, 1)
                        if b.past(1):
                            eng.wait_ge(pool_weight, b.back(1).count(2, 1))
                        eng.activation(e_second[:, j, :], rt[b.par][:, 1, j, :], ACT.Exp,
                                       bias=neg_best[:, 1, j:j + 1]).then_inc(act_route, 1)
                    eng.wait_ge(dve_route, b.count(WEIGHT, TOP_SUMS))
                    for j in range(2):
                        eng.wait_ge(act_route, b.count(6, 4 + j))
                        eng.activation(e_top[:, :], top[:, j, :], ACT.Exp, bias=neg_top[:, j:j + 1],
                                       accum_out=total[:, j:j + 1]).then_inc(act_route, 1)

                def silu(b, u):
                    eng.wait_ge(pe_u, b.count(UNITS_F, u + 1))
                    if u < 2:
                        if b.past(1):
                            eng.wait_ge(dve_u, b.back(1).count(UNITS_F, UNITS_F - 1 + u))
                    else:
                        eng.wait_ge(dve_u, b.count(UNITS_F, u - 1))
                    n = 1 if u < FB else 2
                    eng.activation(act[u % 2][:, 0:n, :], bank_u[u % 2][:, 0:n, :], ACT.Silu).then_inc(act_u, 1)

                def main(a, b):
                    for u in range(UNITS_F):
                        if b:
                            silu(b, u)
                        if a and u == 5:
                            exps(a)
                laps(eng, [(main, (0, 1)), (norm.act(eng), (2,))], 4)

            @block.vector
            def _(eng):
                chain = Count(WEIGHT)
                half_keys = [P, 2, TOP, TOP]

                def best_scores(b):
                    chain.begin(b)
                    eng.wait_ge(pool_rt, b.count(2, 2))
                    if b.past(1):
                        eng.wait_ge(dve_route, b.back(1).count(WEIGHT, WEIGHT))
                    apart(c, eng)
                    for table in range(2):
                        for j in range(2):
                            eng.max(best[:, table, j, :], rt[b.par][:, table, j, :]).then_inc(dve_route, chain.one())

                def best_keys(b):
                    eng.wait_ge(dve_route, chain.so_far())
                    apart(c, eng)
                    for table in range(2):
                        for j in range(2):
                            eng.max_index(best_i[:, table, j, :], best[:, table, j, :], rt[b.par][:, table, j, :]).then_inc(dve_route, chain.one())
                    eng.wait_ge(dve_route, chain.so_far())
                    eng.tensor_copy(best_f[:, :, :, :], best_i[:, :, :, :]).then_inc(dve_route, chain.one())
                    if b.past(1):
                        eng.wait_ge(act_route, b.back(1).count(6, 4))
                    eng.tensor_scalar(neg_best[:, :, :], best[:, :, :, 0], -1.0, None, ALU.mult).then_inc(dve_route, chain.one())
                    assert chain.k == BEST

                def best_sums(b):
                    eng.tensor_tensor(sums[:, :, :, :], best[:, 0, :, :].unsqueeze(3).broadcast_to(half_keys),
                                      best[:, 1, :, :].unsqueeze(2).broadcast_to(half_keys), ALU.add).then_inc(dve_route, chain.one())
                    eng.wait_ge(dve_route, chain.so_far())
                    if b.past(1):
                        eng.wait_ge(act_route, b.back(1).count(6, 6))
                    apart(c, eng)
                    for j in range(2):
                        eng.max(top[:, j, :], sums[:, j, :, :].rearrange("p a b -> p (a b)")).then_inc(dve_route, chain.one())
                    eng.wait_ge(dve_route, chain.so_far())
                    apart(c, eng)
                    for j in range(2):
                        eng.match_replace(left[:, j, :, :].rearrange("p a b -> p (a b)"), top[:, j, :],
                                          sums[:, j, :, :].rearrange("p a b -> p (a b)"), LOWEST).then_inc(dve_route, chain.one())
                    eng.tensor_scalar(neg_top[:, :], top[:, :, 0], -1.0, None, ALU.mult).then_inc(dve_route, chain.one())
                    assert chain.k == TOP_SUMS

                def staircase(b):
                    eng.wait_ge(dve_route, chain.so_far())
                    eng.tensor_tensor(taken[:, :, :, :], left[:, :, :, :], sums[:, :, :, :], ALU.not_equal).then_inc(dve_route, chain.one())
                    eng.wait_ge(dve_route, chain.so_far())
                    eng.tensor_reduce(count[:, :, :], taken[:, :, :, :], AX.X, ALU.add).then_inc(dve_route, chain.one())
                    eng.tensor_tensor(stairs[:, :, :, :],
                                      c.iota[:, 0:TOP].unsqueeze(1).unsqueeze(3).broadcast_to(half_keys),
                                      best_f[:, 0, :, :].unsqueeze(2).broadcast_to(half_keys), ALU.is_equal).then_inc(dve_route, chain.one())
                    eng.wait_ge(dve_route, chain.so_far())
                    eng.tensor_tensor(stairs[:, :, :, :], stairs[:, :, :, :],
                                      count[:, :, :].unsqueeze(2).broadcast_to(half_keys), ALU.mult).then_inc(dve_route, chain.one())
                    eng.wait_ge(dve_route, chain.so_far())
                    eng.tensor_reduce(stair[:, :, :], stairs[:, :, :, :], AX.X, ALU.add).then_inc(dve_route, chain.one())
                    eng.wait_ge(dve_route, chain.so_far())
                    eng.tensor_scalar(stair[:, :, :], stair[:, :, :], -float(TOP), None, ALU.add).then_inc(dve_route, chain.one())

                key_ranks = [P, 2, NKEYS, TOP]

                def find_ranks(b):
                    eng.tensor_tensor(places[:, :, :, :],
                                      c.iota[:, 0:NKEYS].unsqueeze(1).unsqueeze(3).broadcast_to(key_ranks),
                                      best_f[:, 1, :, :].unsqueeze(2).broadcast_to(key_ranks), ALU.is_equal).then_inc(dve_route, chain.one())

                def scale_ranks(b):
                    eng.wait_ge(dve_route, chain.so_far())
                    eng.tensor_tensor(places[:, :, :, :], places[:, :, :, :],
                                      c.rank[:, 0:TOP].unsqueeze(1).unsqueeze(2).broadcast_to(key_ranks), ALU.mult).then_inc(dve_route, chain.one())

                def rank_keys(b):
                    eng.wait_ge(dve_route, chain.so_far())
                    eng.tensor_reduce(rank[:, :, :], places[:, :, :, :], AX.X, ALU.add).then_inc(dve_route, chain.one())

                def choose(b):
                    eng.wait_ge(dve_route, chain.so_far())
                    if b.past(1):
                        eng.wait_ge(pool_weight, b.back(1).count(2, 2))
                    shape = [P, 2, TOP, NKEYS]
                    eng.tensor_tensor(chosen[:, :, :, :], rank[:, :, :].unsqueeze(2).broadcast_to(shape),
                                      stair[:, :, :].unsqueeze(3).broadcast_to(shape), ALU.is_lt).then_inc(dve_route, chain.one())
                    assert chain.k == CHOSEN

                def scale_first(b):
                    eng.wait_ge(act_route, b.count(6, 6))
                    eng.reciprocal(r_total[:, :], total[:, :]).then_inc(dve_route, chain.one())
                    eng.wait_ge(dve_route, chain.so_far())
                    eng.tensor_tensor(scaled[:, :, :], e_first[:, :, :],
                                      r_total[:, :].unsqueeze(2).broadcast_to([P, 2, TOP]), ALU.mult).then_inc(dve_route, chain.one())
                    assert chain.k == SCALED

                def weigh_last(b):
                    eng.wait_ge(pool_weight, b.count(2, 2))
                    eng.tensor_reduce(inside[:, :], weight[b.par][:, :, 0:EXPERTS - 1], AX.X, ALU.add).then_inc(dve_route, chain.one())
                    eng.wait_ge(dve_route, chain.so_far())
                    eng.tensor_scalar(weight[b.par][:, :, EXPERTS - 1], inside[:, :], -1.0, 1.0,
                                      ALU.mult, ALU.add).then_inc(dve_route, chain.one())
                    chain.end()

                routing = (best_scores, best_keys, best_sums, staircase, find_ranks, scale_ranks, rank_keys, choose,
                           scale_first)

                def hide(b, u):
                    eng.wait_ge(act_u, b.count(UNITS_F, u + 1))
                    if b.past(1):
                        eng.wait_ge(pe_y, b.back(1).count(1, 1))
                    if u < FB:
                        eng.tensor_tensor(hidden[:, u, :], act[u % 2][:, 0, :], bank_u[u % 2][:, 1, :],
                                          ALU.mult).then_inc(dve_u, 1)
                    else:
                        eng.wait_ge(pe_w, b.count(1, 1))
                        e = u - FB
                        dst, src = (x.rearrange("p w (i j) -> p w j i", j=2)
                                    for x in (hidden[:, FB + 2 * e:FB + 2 * e + 2, :], act[u % 2][:, :, :]))
                        eng.tensor_tensor(dst, src, bank_w[e][:, :, :, :], ALU.mult).then_inc(dve_u, 1)

                sum_up, normalise = norm.dve(eng)

                def main(a, b, z):
                    for u in range(UNITS_F):
                        if b:
                            hide(b, u)
                        if z and u == 1:
                            sum_up(z)
                        if z and u == 3:
                            normalise(z)
                        if a and u < len(routing):
                            routing[u](a)

                laps(eng, [(main, (0, 1, 2)), (weigh_last, (0,))], 4)

            @block.gpsimd
            def _(eng):
                def fetch_scores(b):
                    for table in range(2):
                        if b.past(2):
                            eng.wait_ge(dve_route, b.back(2).count(WEIGHT, BEST))
                        if b.past(2):
                            eng.wait_ge(act_route, b.back(2).count(6, 4))
                        apart(c, eng)
                        eng.tensor_copy(rt[b.par][:, table, :, :].rearrange("p j k -> p (j k)"),
                                        c.R[:, bass.ds(P * b.n + table * B * P, P)]).then_inc(pool_rt, 1)

                def weigh(b):
                    eng.wait_ge(dve_route, b.count(WEIGHT, CHOSEN))
                    eng.wait_ge(act_route, b.count(6, 4))
                    shape = [P, 2, TOP, NKEYS]
                    eng.tensor_tensor(chosen[:, :, :, :], chosen[:, :, :, :],
                                      e_second[:, :, :].unsqueeze(2).broadcast_to(shape), ALU.mult).then_inc(pool_weight, 1)
                    eng.wait_ge(pool_weight, b.count(2, 1))
                    eng.wait_ge(dve_route, b.count(WEIGHT, SCALED))
                    if b.past(2):
                        eng.wait_ge(pe_w, b.back(2).count(1, 1))
                    eng.tensor_tensor(weight[b.par][:, :, :].rearrange("p j (a b) -> p j a b", b=NKEYS), chosen[:, :, :, :],
                                      scaled[:, :, :].unsqueeze(3).broadcast_to(shape), ALU.mult).then_inc(pool_weight, 1)
                laps(eng, [(fetch_scores, (0,)), (norm.pool(eng), (2,)), (weigh, (0,))], 4)




def running_sum(c):
    nc = c.nc
    with ExitStack() as stack:
        c.stack = stack
        bank_kv = [c.psum(f"rs_kv{t}") for t in range(2)]
        bank_q, bank_c = c.psum("rs_q", (P, DC, S)), c.psum("rs_c", (P, DC, S))
        bank_y, bank_t = c.psum("rs_y", (P, 2, D)), c.psum("rs_t")
        k = c.sb("rs_k", [P, 2, D])
        kv = [c.sb(f"rs_kv_sb{p}", [P, 2, D]) for p in range(2)]
        q = [c.sb(f"rs_q_sb{p}", [P, DC, S]) for p in range(2)]
        o_t = [c.sb(f"rs_o_t{p}", [P, DC, S]) for p in range(2)]
        pe_kv, act_k, dve_kv = c.sem("rs_pe_kv"), c.sem("rs_act_k"), c.sem("rs_dve_kv")
        pe_q, act_q, pe_c = c.sem("rs_pe_q"), c.sem("rs_act_q"), c.sem("rs_pe_c")
        dve_o, pe_y = c.sem("rs_dve_o"), c.sem("rs_pe_y")
        norm = Norm(c, "n4", bank_y[:, :, :], lambda eng, b: eng.wait_ge(pe_y, b.count(1, 1)), bank_t)
        fetch = Fetch(c, "rs", lambda eng, b: eng.wait_ge(pe_q, b.count(1, 1)))

        with nc.Block() as block:
            @block.sync
            def _(eng):
                c.load_mixture(eng)

            @block.tensor
            def _(eng):
                def project(b):
                    x = fetch.tile[b.par]
                    fetch.ready(eng, b)
                    for t in range(2):
                        if b.past(1):
                            eng.wait_ge(dve_kv, b.back(1).count(2, t + 1))
                        for i in range(DC):
                            last = eng.matmul(bank_kv[t][:, :], x[:, i, t * P:(t + 1) * P], c.r_kv[:, i, :],
                                              start=i == 0, stop=i == DC - 1)
                        last.then_inc(pe_kv, 1)
                    if b.past(1):
                        eng.wait_ge(act_q, b.back(1).count(1, 1))
                    for j in range(DC):
                        for i in range(DC):
                            last = eng.matmul(bank_q[:, j, :], c.r_q[:, i, j * P:(j + 1) * P], x[:, i, :],
                                              start=i == 0, stop=i == DC - 1)
                    last.then_inc(pe_q, 1)

                def out(b):
                    eng.wait_ge(dve_o, b.count(1, 1))
                    if b.past(1):
                        eng.wait_ge(norm.dve_norm, b.back(1).count(norm.PER, norm.SUMMED))
                    for t in range(2):
                        for i in range(DC):
                            last = eng.matmul(bank_y[:, t, :], o_t[b.par][:, i, t * P:(t + 1) * P], c.r_o[:, i, :],
                                              start=i == 0, stop=i == DC - 1)
                    last.then_inc(pe_y, 1)

                def add_up(b):
                    eng.wait_ge(dve_kv, b.count(2, 2))
                    if b.past(1):
                        eng.wait_ge(dve_o, b.back(1).count(1, 1))
                    for j in range(DC):
                        cols = slice(j * P, (j + 1) * P)
                        eng.matmul(bank_c[:, j, :], kv[b.par][:, 0, cols], c.tri[:, :], start=True, stop=False)
                        last = eng.matmul(bank_c[:, j, P:], kv[b.par][:, 1, cols], c.tri[:, 0:P], start=False, stop=True)
                    last.then_inc(pe_c, 1)

                laps(eng, [(project, (0,)), (out, (1,)), (add_up, (0,)), (norm.pe(eng), (2,))], 4)

            @block.scalar
            def _(eng):
                def keep(b):
                    for t in range(2):
                        eng.wait_ge(pe_kv, b.count(2, t + 1))
                        if b.past(1):
                            eng.wait_ge(dve_kv, b.back(1).count(2, t + 1))
                        eng.activation(k[:, t, :], bank_kv[t][:, 0:D], ACT.Copy).then_inc(act_k, 1)
                    eng.wait_ge(pe_q, b.count(1, 1))
                    if b.past(2):
                        eng.wait_ge(dve_o, b.back(2).count(1, 1))
                    eng.activation(q[b.par][:, :, :], bank_q[:, :, :], ACT.Copy).then_inc(act_q, 1)
                laps(eng, [(keep, (0,)), (norm.act(eng), (2,))], 4)

            @block.vector
            def _(eng):
                def products(b):
                    for t in range(2):
                        eng.wait_ge(act_k, b.count(2, t + 1))
                        if b.past(2):
                            eng.wait_ge(pe_c, b.back(2).count(1, 1))
                        eng.tensor_tensor(kv[b.par][:, t, :], bank_kv[t][:, D:], k[:, t, :], ALU.mult).then_inc(dve_kv, 1)

                def gate(b):
                    eng.wait_ge(pe_c, b.count(1, 1))
                    eng.wait_ge(act_q, b.count(1, 1))
                    if b.past(2):
                        eng.wait_ge(pe_y, b.back(2).count(1, 1))
                    eng.tensor_tensor(o_t[b.par][:, :, :], bank_c[:, :, :], q[b.par][:, :, :],
                                      ALU.mult).then_inc(dve_o, 1)
                laps(eng, [(products, (0,)), *((step, (1,)) for step in norm.dve(eng)), (gate, (0,))], 4)

            @block.gpsimd
            def _(eng):
                laps(eng, [(fetch.pool(eng), (0,)), (norm.pool(eng), (2,))], 4)




ROUND = 1.5 * 2.0 ** 23
INT8 = 127.0
HB = H // 2
SCORES = HB * CTX


class Rounding:
    PER = 8

    def __init__(self, c, name):
        self.c = c
        self.dve_done = c.sem(name + "_dve_rounded")
        self.peak, self.step, self.inv = (c.sb(name + n, [P, 2]) for n in ("_peak", "_step", "_inv"))
        self.whole = c.sb(name + "_whole", [P, 2, D])

    def run(self, eng, b, src, dst):
        chain = Count(self.PER)
        chain.begin(b)
        if b.past(1):
            eng.wait_ge(self.dve_done, b.back(1).count(self.PER, self.PER))
        apart(self.c, eng)
        eng.tensor_reduce(self.peak[:, :], src, AX.X, ALU.max, apply_absolute_value=True).then_inc(self.dve_done, chain.one())
        eng.wait_ge(self.dve_done, chain.so_far())
        eng.tensor_scalar(self.step[:, :], self.peak[:, :], 1 / INT8, 1e-8, ALU.mult, ALU.max).then_inc(self.dve_done, chain.one())
        eng.wait_ge(self.dve_done, chain.so_far())
        eng.reciprocal(self.inv[:, :], self.step[:, :]).then_inc(self.dve_done, chain.one())
        eng.wait_ge(self.dve_done, chain.so_far())
        for t in range(2):
            eng.tensor_scalar(self.whole[:, t, :], src[:, t, :], self.inv[:, t:t + 1], INT8, ALU.mult, ALU.min).then_inc(self.dve_done, chain.one())
        eng.wait_ge(self.dve_done, chain.so_far())
        eng.tensor_scalar(self.whole[:, :, :], self.whole[:, :, :], -INT8, ROUND, ALU.max, ALU.add).then_inc(self.dve_done, chain.one())
        eng.wait_ge(self.dve_done, chain.so_far())
        for t in range(2):
            eng.tensor_scalar(dst[:, t, :], self.whole[:, t, :], ROUND, self.step[:, t:t + 1],
                              ALU.subtract, ALU.mult).then_inc(self.dve_done, chain.one())
        chain.end()


def rounded_attention(c):
    nc = c.nc
    with ExitStack() as stack:
        c.stack = stack
        bank_s = c.psum("ra_s", (P, 2, SCORES))
        bank_p = c.psum("ra_p", (P, HB, P))
        bank_a, bank_q = c.psum("ra_a", (P, 2, S)), c.psum("ra_q", (P, DC, S))
        bank_o, bank_y = c.psum("ra_o", (P, 2, S)), c.psum("ra_y", (P, 2, D))
        weight = [c.sb(f"ra_weight_{n}", [P, DC, D]) for n in "qp"]
        k_all = c.sb("ra_k_all", [P, DC * B * CTX])
        v_all = c.sb("ra_v_all", [P, B * D])
        rounded_w = [c.sb(f"ra_rounded_{n}", [P, DC, D]) for n in "qp"]
        k_diag = [c.sb(f"ra_k_diag{p}", [P, DC, HB, CTX]) for p in range(2)]
        v_diag = [c.sb(f"ra_v_diag{p}", [P, HB, 2 * HD]) for p in range(2)]
        x_round = [c.sb(f"ra_x_round{p}", [P, 2, D]) for p in range(2)]
        x_t, q_t = c.sb("ra_x_t", [P, DC, S]), c.sb("ra_q_t", [P, DC, S])
        probs = c.sb("ra_probs", [P, 2, H, CTX])
        peak = c.sb("ra_peak_s", [P, 2, H])
        total = c.sb("ra_total", [P, 2, H])
        recip = [c.sb(f"ra_recip{p}", [P, 2, H]) for p in range(2)]
        probs_t = c.sb("ra_probs_t", [P, HB, S])
        o_t, o_rows = c.sb("ra_o_t", [P, 2, S]), c.sb("ra_o_rows", [P, 2, D])
        o_round, o_round_t = c.sb("ra_o_round", [P, 2, D]), c.sb("ra_o_round_t", [P, DC, S])
        residual = c.sb("ra_residual", [P, 2, D])

        w_round, x_rounding, o_rounding = Rounding(c, "ra_w"), Rounding(c, "ra_x"), Rounding(c, "ra_o")
        pe_setup, act_setup, dve_setup = c.sem("ra_pe_setup"), c.sem("ra_act_setup"), c.sem("ra_dve_setup")
        pool_diag = c.sem("ra_pool_diag")
        pool_res = c.sem("ra_pool_res")
        pe_x, act_x, pe_q, act_q = (c.sem("ra_" + n) for n in ("pe_x", "act_x", "pe_q", "act_q"))
        pe_s, act_exp = c.sem("ra_pe_s"), c.sem("ra_act_exp")
        SOFT = 7
        dve_soft = c.sem("ra_dve_soft")
        pe_p, act_p = c.sem("ra_pe_p"), c.sem("ra_act_p")
        pe_pv, act_o, pe_rows, dve_rows = (c.sem("ra_" + n) for n in ("pe_pv", "act_o", "pe_rows", "dve_rows"))
        pe_or, act_or, pe_y = c.sem("ra_pe_or"), c.sem("ra_act_or"), c.sem("ra_pe_y")
        norm = Norm(c, "n5", bank_y[:, :, :], lambda eng, b: eng.wait_ge(pe_y, b.count(1, 1)),
                    bank_a[:, :, :].rearrange("p j t -> p (j t)"),
                    residual=(residual[:, :, :], lambda eng, b: eng.wait_ge(pool_res, b.count(1, 1))))

        def turn_tiles(eng, bank, src):
            for t in range(2):
                for j in range(DC):
                    last = eng.transpose(bank[:, j, t * P:(t + 1) * P], src[:, t, j * P:(j + 1) * P], c.ident[:, :])
            return last

        with nc.Block() as block:
            @block.tensor
            def _(eng):
                for w in range(2):
                    eng.wait_ge(w_round.dve_done, w_round.PER * (w + 1))
                    turn_tiles(eng, (bank_a, bank_q)[w], rounded_w[w]).then_inc(pe_setup, 1)
                for j in range(DC):
                    for i in range(DC):
                        last = eng.matmul(bank_s[:, j, :], c.a_k[:, i, j * P:(j + 1) * P], c.ctx_all[:, i, :],
                                          start=i == 0, stop=i == DC - 1)
                    last.then_inc(pe_setup, 1)
                for b in range(B):
                    if b >= 2:
                        eng.wait_ge(dve_setup, b - 1)
                    for i in range(DC):
                        last = eng.matmul((bank_o, bank_y)[b % 2][:, 0, :], c.ctx_twice[:, i, b * P:(b + 1) * P],
                                          c.a_v[:, i, :], start=i == 0, stop=i == DC - 1)
                    last.then_inc(pe_setup, 1)
                eng.wait_ge(act_setup, 2 + DC)
                eng.wait_ge(dve_setup, B)

                def turn_x(a):
                    eng.wait_ge(x_rounding.dve_done, a.count(Rounding.PER, Rounding.PER))
                    if a.past(1):
                        eng.wait_ge(act_x, a.back(1).count(1, 1))
                    if a.past(2):
                        eng.wait_ge(dve_rows, a.back(2).count(1, 1))
                    if a.past(3):
                        eng.wait_ge(act_or, a.back(3).count(1, 1))
                    if a.past(3):
                        eng.wait_ge(norm.act_turned, a.back(3).count(1, 1))
                    turn_tiles(eng, bank_a, x_round[a.par]).then_inc(pe_x, 1)

                def project_q(a):
                    eng.wait_ge(act_x, a.count(1, 1))
                    if a.past(1):
                        eng.wait_ge(act_q, a.back(1).count(1, 1))
                    for j in range(DC):
                        for i in range(DC):
                            last = eng.matmul(bank_q[:, j, :], weight[0][:, i, j * P:(j + 1) * P], x_t[:, i, :],
                                              start=i == 0, stop=i == DC - 1)
                    last.then_inc(pe_q, 1)

                def score(a, t):
                    eng.wait_ge(act_q, a.count(1, 1))
                    eng.wait_ge(pool_diag, a.count(3, 2))
                    if t:
                        eng.wait_ge(dve_soft, a.count(SOFT, 2))
                    else:
                        if a.past(1):
                            eng.wait_ge(dve_soft, a.back(1).count(SOFT, 4))
                    for j in range(DC):
                        last = eng.matmul(bank_s[:, j, :], q_t[:, j, t * P:(t + 1) * P],
                                          k_diag[a.par][:, j, :, :].rearrange("p h k -> p (h k)"), start=True, stop=True)
                    last.then_inc(pe_s, 1)

                def turn_probs(b, t):
                    eng.wait_ge(act_exp, b.count(2, t + 1))
                    if t:
                        eng.wait_ge(act_p, b.count(2, 1))
                    else:
                        if b.past(1):
                            eng.wait_ge(act_p, b.back(1).count(2, 2))
                    for h in range(HB):
                        last = eng.transpose(bank_p[:, h, :],
                                             probs[:, t, 2 * h:2 * h + 2, :].rearrange("p h k -> p (h k)"), c.ident[:, :])
                    last.then_inc(pe_p, 1)

                def pv(b):
                    eng.wait_ge(act_p, b.count(2, 2))
                    eng.wait_ge(pool_diag, b.count(3, 3))
                    if b.past(1):
                        eng.wait_ge(act_o, b.back(1).count(1, 1))
                    for h in range(HB):
                        at = 32 * (h % 4)
                        last = eng.matmul(bank_o[at:at + 32, h // 4, :], v_diag[b.par][:, h, :], probs_t[:, h, :],
                                          start=True, stop=True)
                    last.then_inc(pe_pv, 1)

                def turn_o(a, b, z):
                    eng.wait_ge(act_o, b.count(1, 1))
                    if z:
                        eng.wait_ge(act_or, z.count(1, 1))
                    elif a:
                        eng.wait_ge(act_x, a.count(1, 1))
                    turn_tiles(eng, bank_a, o_t).then_inc(pe_rows, 1)

                def turn_rounded(a, z):
                    eng.wait_ge(o_rounding.dve_done, z.count(Rounding.PER, Rounding.PER))
                    if a:
                        eng.wait_ge(act_x, a.count(1, 1))
                    elif z.past(1):
                        eng.wait_ge(norm.act_turned, z.back(1).count(1, 1))
                    turn_tiles(eng, bank_a, o_round).then_inc(pe_or, 1)

                def out(b):
                    eng.wait_ge(act_or, b.count(1, 1))
                    if b.past(1):
                        eng.wait_ge(norm.dve_norm, b.back(1).count(norm.PER, norm.SUMMED))
                    for t in range(2):
                        for i in range(DC):
                            last = eng.matmul(bank_y[:, t, :], o_round_t[:, i, t * P:(t + 1) * P], weight[1][:, i, :],
                                              start=i == 0, stop=i == DC - 1)
                    last.then_inc(pe_y, 1)

                turn_rows = norm.pe(eng)

                def main(a, b, z):
                    if a:
                        turn_x(a)
                    if b:
                        turn_probs(b, 0)
                    if a:
                        project_q(a)
                    if z:
                        turn_rounded(a, z)
                    if b:
                        turn_probs(b, 1)
                    if z:
                        out(z)
                    if a:
                        score(a, 0)
                    if b:
                        pv(b)
                    if a:
                        score(a, 1)
                    if b:
                        turn_o(a, b, z)
                    if z:
                        if b:
                            eng.wait_ge(dve_rows, b.count(1, 1))
                        turn_rows(z)
                laps(eng, [(main, (1, 2, 3))], 4)

            @block.scalar
            def _(eng):
                for w in range(2):
                    eng.wait_ge(pe_setup, w + 1)
                    eng.activation(weight[w][:, :, :], (bank_a, bank_q)[w][:, :, :], ACT.Copy).then_inc(act_setup, 1)
                for j in range(DC):
                    eng.wait_ge(pe_setup, 3 + j)
                    eng.activation(k_all[:, j * B * CTX:(j + 1) * B * CTX], bank_s[:, j, :], ACT.Identity,
                                   bias=c.a_bk[:, j:j + 1]).then_inc(act_setup, 1)

                def keep_x(a):
                    eng.wait_ge(pe_x, a.count(1, 1))
                    if a.past(1):
                        eng.wait_ge(pe_q, a.back(1).count(1, 1))
                    eng.activation(x_t[:, :, :], bank_a[:, :, :], ACT.Copy).then_inc(act_x, 1)

                def keep_probs(b, t):
                    eng.wait_ge(pe_p, b.count(2, t + 1))
                    if b.past(1):
                        eng.wait_ge(pe_pv, b.back(1).count(1, 1))
                    eng.activation(probs_t[:, :, t * P:(t + 1) * P], bank_p[:, :, :], ACT.Copy).then_inc(act_p, 1)

                def keep_q(a):
                    eng.wait_ge(pe_q, a.count(1, 1))
                    if a.past(1):
                        eng.wait_ge(pe_s, a.back(1).count(2, 2))
                    for j in range(DC):
                        last = eng.activation(q_t[:, j, :], bank_q[:, j, :], ACT.Identity, bias=c.a_bq[:, j:j + 1])
                    last.then_inc(act_q, 1)

                def exps(a, t):
                    eng.wait_ge(dve_soft, a.count(SOFT, 2 * t + 2))
                    eng.activation(probs[:, t, :, :], probs[:, t, :, :], ACT.Exp, scale=HD ** -0.5).then_inc(act_exp, 1)

                def keep_o(b):
                    eng.wait_ge(pe_pv, b.count(1, 1))
                    if b.past(1):
                        eng.wait_ge(pe_rows, b.back(1).count(1, 1))
                    eng.activation(o_t[:, :, :], bank_o[:, :, :], ACT.Copy).then_inc(act_o, 1)

                def keep_rounded(b):
                    eng.wait_ge(pe_or, b.count(1, 1))
                    if b.past(1):
                        eng.wait_ge(pe_y, b.back(1).count(1, 1))
                    eng.activation(o_round_t[:, :, :], bank_a[:, :, :], ACT.Copy).then_inc(act_or, 1)

                turned = norm.act(eng)

                def main(a, b, z):
                    if a:
                        keep_x(a)
                    if b:
                        keep_probs(b, 0)
                    if a:
                        keep_q(a)
                    if z:
                        keep_rounded(z)
                    if b:
                        keep_probs(b, 1)
                    if a:
                        exps(a, 0)
                    if b:
                        keep_o(b)
                    if a:
                        exps(a, 1)
                    if z:
                        turned(z)
                laps(eng, [(main, (1, 2, 3))], 4)

            @block.vector
            def _(eng):
                for w in range(2):
                    w_round.run(eng, Lap(w, 0, w, False), (c.a_q, c.a_p)[w], rounded_w[w])
                for b in range(B):
                    eng.wait_ge(pe_setup, 2 + DC + b + 1)
                    eng.tensor_tensor(v_all[:, b * D:(b + 1) * D], (bank_o, bank_y)[b % 2][:, 0, :], c.a_bv[:, :],
                                      ALU.add).then_inc(dve_setup, 1)

                chain = Count(SOFT)

                def less_peak(a, t):
                    if t == 0:
                        chain.begin(a)
                        if a.past(1):
                            eng.wait_ge(dve_soft, a.back(1).count(SOFT, 6))
                    eng.wait_ge(pe_s, a.count(2, t + 1))
                    scores = bank_s[:, :, :].rearrange("p j (h k) -> p (j h) k", k=CTX)
                    eng.tensor_reduce(peak[:, t, :], scores, AX.X, ALU.max).then_inc(dve_soft, chain.one())
                    eng.wait_ge(dve_soft, chain.so_far())
                    if a.past(1):
                        eng.wait_ge(pe_p, a.back(1).count(2, t + 1))
                    eng.tensor_tensor(probs[:, t, :, :], scores,
                                      peak[:, t, :].unsqueeze(2).broadcast_to([P, H, CTX]), ALU.subtract).then_inc(dve_soft, chain.one())

                def add_up(a):
                    if a.past(1):
                        eng.wait_ge(dve_soft, a.back(1).count(SOFT, SOFT))
                    for t in range(2):
                        eng.wait_ge(act_exp, a.count(2, t + 1))
                        eng.tensor_reduce(total[:, t, :], probs[:, t, :, :], AX.X, ALU.add).then_inc(dve_soft, chain.one())
                    eng.wait_ge(dve_soft, chain.so_far())
                    if a.past(2):
                        eng.wait_ge(dve_rows, a.back(2).count(1, 1))
                    eng.reciprocal(recip[a.par][:, :, :], total[:, :, :]).then_inc(dve_soft, chain.one())
                    chain.end()

                def divide(b):
                    eng.wait_ge(pe_rows, b.count(1, 1))
                    eng.wait_ge(dve_soft, b.count(SOFT, SOFT))
                    if b.past(1):
                        eng.wait_ge(o_rounding.dve_done, b.back(1).count(Rounding.PER, Rounding.PER))
                    eng.tensor_tensor(o_rows[:, :, :].rearrange("p t (h d) -> p (t h) d", d=HD),
                                      bank_a[:, :, :].rearrange("p t (h d) -> p (t h) d", d=HD),
                                      recip[b.par][:, :, :].rearrange("p t h -> p (t h)").unsqueeze(2).broadcast_to(
                                          [P, 2 * H, HD]), ALU.mult).then_inc(dve_rows, 1)

                def round_o(b):
                    eng.wait_ge(dve_rows, b.count(1, 1))
                    if b.past(1):
                        eng.wait_ge(pe_or, b.back(1).count(1, 1))
                    o_rounding.run(eng, b, o_rows[:, :, :], o_round)

                def round_x(n):
                    x = c.X[:, bass.ds(2 * D * n.n, 2 * D)].rearrange("p (t d) -> p t d", t=2)
                    if n.past(2):
                        eng.wait_ge(pe_x, n.back(2).count(1, 1))
                    x_rounding.run(eng, n, x, x_round[n.par])

                sum_up, normalise = norm.dve(eng)

                def main(n, a, b, z):
                    if z:
                        round_o(z)
                    if n:
                        round_x(n)
                    if a:
                        less_peak(a, 0)
                    if z:
                        sum_up(z)
                    if a:
                        less_peak(a, 1)
                    if z:
                        normalise(z)
                    if b:
                        divide(b)
                    if a:
                        add_up(a)
                laps(eng, [(main, (0, 1, 2, 3))], 6)

            @block.gpsimd
            def _(eng):
                eng.wait_ge(act_setup, 2 + DC)
                eng.wait_ge(dve_setup, B)

                def diagonals(n):
                    for j in range(DC):
                        if n.past(2):
                            eng.wait_ge(pe_s, n.back(2).count(2, 2))
                        apart(c, eng)
                        eng.tensor_tensor(k_diag[n.par][:, j, :, :],
                                          k_all[:, bass.ds(j * B * CTX + CTX * n.n, CTX)].unsqueeze(1).broadcast_to(
                                              [P, HB, CTX]),
                                          c.head_of[:, :].unsqueeze(2).broadcast_to([P, HB, CTX]),
                                          ALU.mult).then_inc(pool_diag, 1)
                    if n.past(2):
                        eng.wait_ge(pe_pv, n.back(2).count(1, 1))
                    apart(c, eng)
                    eng.tensor_tensor(v_diag[n.par][:, :, :],
                                      v_all[:, bass.ds(D * n.n, D)].rearrange("p (h d) -> p h d", h=HB),
                                      c.half_of[:, :].unsqueeze(1).broadcast_to([P, HB, 2 * HD]),
                                      ALU.mult).then_inc(pool_diag, 1)

                def add_bias(b):
                    if b.past(1):
                        eng.wait_ge(norm.dve_norm, b.back(1).count(norm.PER, norm.SUMMED))
                    apart(c, eng)
                    eng.tensor_tensor(residual[:, :, :],
                                      c.X[:, bass.ds(2 * D * b.n, 2 * D)].rearrange("p (t d) -> p t d", t=2),
                                      c.a_bp[:, :].rearrange("p (t d) -> p t d", t=2), ALU.add).then_inc(pool_res, 1)

                laps(eng, [(diagonals, (0,)), (add_bias, (3,)), (norm.pool(eng), (3,))], 6)




E = 16
KE = 2
F = 176
FP = 2 * P
SLOTS_E = TILES * KE
MTILES = B * S * KE // P + E
I32 = mybir.dt.int32


def route_experts(c):
    nc = c.nc
    with ExitStack() as stack:
        c.stack = stack
        bank_l, bank_r, bank_n = c.psum("re_l", (P, TILES, E)), c.psum("re_r", (P, TILES, E)), c.psum("re_n", (P, E))
        biased = c.sb("re_biased", [P, TILES, E])
        best, best_i = c.sb("re_best", [P, TILES, TOP]), c.sb("re_best_i", [P, TILES, TOP], U32)
        best_f = c.sb("re_best_f", [P, TILES, KE])
        peak, less = c.sb("re_peak", [P, TILES]), c.sb("re_less", [P, TILES, E])
        exps = c.sb("re_exps", [P, TILES, E])
        chosen, picked = c.sb("re_chosen", [P, TILES, KE, E]), c.sb("re_picked", [P, TILES, KE, E])
        both = c.sb("re_both", [P, 2 * TILES, E], BF16)
        w, w_sum, w_inv = c.sb("re_w", [P, TILES, KE]), c.sb("re_w_sum", [P, TILES]), c.sb("re_w_inv", [P, TILES])
        ranks = c.sb("re_ranks", [P, SLOTS_E])
        counts, tiles_of = c.sb("re_counts", [P, E]), c.sb("re_tiles", [P, E])
        before, start, end = c.sb("re_before", [P, E, E]), c.sb("re_start", [P, E]), c.sb("re_end", [P, E])
        starts = c.sb("re_starts", [P, SLOTS_E])
        done, expert = c.sb("re_done", [P, MTILES, E]), c.sb("re_expert", [P, MTILES])
        place = c.sb("re_place", [P, SLOTS_E])
        pe_logits, act_exps, dve_route, pe_ranks = (c.sem("re_" + n) for n in ("pe_logits", "act_exps", "dve", "pe_ranks"))
        EXP_READY, BOTH_READY = [0], [0]

        with nc.Block() as block:
            @block.sync
            def _(eng):
                c.load_down(eng)

            @block.vector
            def _(eng):
                chain = Count(0)
                eng.memset(both[:, 0:TILES, :], 0.0).then_inc(dve_route, chain.one())
                eng.wait_ge(pe_logits, 1)
                eng.tensor_tensor(biased[:, :, :], bank_l[:, :, :],
                                  c.m_bias[:, :].unsqueeze(1).broadcast_to([P, TILES, E]), ALU.add).then_inc(dve_route, chain.one())
                eng.tensor_reduce(peak[:, :], bank_l[:, :, :], AX.X, ALU.max).then_inc(dve_route, chain.one())
                eng.wait_ge(dve_route, chain.so_far())
                eng.tensor_tensor(less[:, :, :], bank_l[:, :, :],
                                  peak[:, :].unsqueeze(2).broadcast_to([P, TILES, E]), ALU.subtract).then_inc(dve_route, chain.one())
                EXP_READY[0] = chain.k
                for t in range(TILES):
                    eng.max(best[:, t, :], biased[:, t, :]).then_inc(dve_route, chain.one())
                eng.wait_ge(dve_route, chain.so_far())
                for t in range(TILES):
                    eng.max_index(best_i[:, t, :], best[:, t, :], biased[:, t, :]).then_inc(dve_route, chain.one())
                eng.wait_ge(dve_route, chain.so_far())
                eng.tensor_copy(best_f[:, :, :], best_i[:, :, 0:KE]).then_inc(dve_route, chain.one())
                eng.wait_ge(dve_route, chain.so_far())
                shape = [P, SLOTS_E, E]
                flat = "p t k e -> p (t k) e"
                eng.tensor_tensor(chosen[:, :, :, :].rearrange(flat), c.iota[:, 0:E].unsqueeze(1).broadcast_to(shape),
                                  best_f[:, :, :].rearrange("p t k -> p (t k)").unsqueeze(2).broadcast_to(shape),
                                  ALU.is_equal).then_inc(dve_route, chain.one())
                eng.wait_ge(dve_route, chain.so_far())
                eng.tensor_tensor(both[:, TILES:, :], chosen[:, :, 0, :], chosen[:, :, 1, :], ALU.add).then_inc(dve_route, chain.one())
                BOTH_READY[0] = chain.k
                eng.wait_ge(act_exps, 1)
                eng.tensor_tensor(picked[:, :, :, :], chosen[:, :, :, :],
                                  exps[:, :, :].unsqueeze(2).broadcast_to([P, TILES, KE, E]), ALU.mult).then_inc(dve_route, chain.one())
                eng.wait_ge(dve_route, chain.so_far())
                eng.tensor_reduce(w[:, :, :], picked[:, :, :, :], AX.X, ALU.add).then_inc(dve_route, chain.one())
                eng.wait_ge(dve_route, chain.so_far())
                eng.tensor_reduce(w_sum[:, :], w[:, :, :], AX.X, ALU.add).then_inc(dve_route, chain.one())
                eng.wait_ge(dve_route, chain.so_far())
                eng.reciprocal(w_inv[:, :], w_sum[:, :]).then_inc(dve_route, chain.one())
                eng.wait_ge(dve_route, chain.so_far())
                eng.tensor_tensor(c.row_weights[:, :].rearrange("p (t k) -> p t k", k=KE), w[:, :, :],
                                  w_inv[:, :].unsqueeze(2).broadcast_to([P, TILES, KE]), ALU.mult).then_inc(dve_route, chain.one())
                eng.wait_ge(pe_ranks, 1)
                eng.tensor_tensor(picked[:, :, :, :], chosen[:, :, :, :],
                                  bank_r[:, :, :].unsqueeze(2).broadcast_to([P, TILES, KE, E]), ALU.mult).then_inc(dve_route, chain.one())
                eng.wait_ge(dve_route, chain.so_far())
                eng.tensor_reduce(ranks[:, :], picked[:, :, :, :].rearrange(flat), AX.X, ALU.add).then_inc(dve_route, chain.one())
                eng.tensor_scalar(counts[:, :], bank_n[:, :], 1 / P, (P - 1) / P - 0.5 + 0.25 / P, ALU.mult, ALU.add).then_inc(dve_route, chain.one())
                eng.wait_ge(dve_route, chain.so_far())
                eng.tensor_scalar(counts[:, :], counts[:, :], ROUND, None, ALU.add).then_inc(dve_route, chain.one())
                eng.wait_ge(dve_route, chain.so_far())
                eng.tensor_scalar(tiles_of[:, :], counts[:, :], ROUND, None, ALU.subtract).then_inc(dve_route, chain.one())
                eng.wait_ge(dve_route, chain.so_far())
                eng.tensor_tensor(before[:, :, :], tiles_of[:, :].unsqueeze(1).broadcast_to([P, E, E]),
                                  c.earlier[:, :].rearrange("p (e f) -> p e f", e=E), ALU.mult).then_inc(dve_route, chain.one())
                eng.wait_ge(dve_route, chain.so_far())
                eng.tensor_reduce(start[:, :], before[:, :, :], AX.X, ALU.add).then_inc(dve_route, chain.one())
                eng.wait_ge(dve_route, chain.so_far())
                eng.tensor_tensor(end[:, :], start[:, :], tiles_of[:, :], ALU.add).then_inc(dve_route, chain.one())
                eng.tensor_tensor(picked[:, :, :, :].rearrange(flat), chosen[:, :, :, :].rearrange(flat),
                                  start[:, :].unsqueeze(1).broadcast_to(shape), ALU.mult).then_inc(dve_route, chain.one())
                eng.wait_ge(dve_route, chain.so_far())
                eng.tensor_reduce(starts[:, :], picked[:, :, :, :].rearrange(flat), AX.X, ALU.add).then_inc(dve_route, chain.one())
                eng.wait_ge(dve_route, chain.so_far())
                eng.scalar_tensor_tensor(place[:, :], starts[:, :], float(P), ranks[:, :], ALU.mult, ALU.add).then_inc(dve_route, chain.one())
                eng.wait_ge(dve_route, chain.so_far())
                eng.tensor_copy(c.places[:, :], place[:, :]).then_inc(dve_route, chain.one())
                eng.tensor_tensor(done[:, :, :], end[:, :].unsqueeze(1).broadcast_to([P, MTILES, E]),
                                  c.iota[:, 0:MTILES].unsqueeze(2).broadcast_to([P, MTILES, E]), ALU.is_le).then_inc(dve_route, chain.one())
                eng.wait_ge(dve_route, chain.so_far())
                eng.tensor_reduce(expert[:, :], done[:, :, :], AX.X, ALU.add).then_inc(dve_route, chain.one())
                eng.wait_ge(dve_route, chain.so_far())
                eng.tensor_scalar(c.tile_expert[:, :], expert[:, :], float(E - 1), None, ALU.min).then_inc(dve_route, chain.one())
                eng.wait_ge(dve_route, chain.so_far())

            @block.tensor
            def _(eng):
                eng.wait_ge(c.in_w6, 16)
                for t in range(TILES):
                    for i in range(DC):
                        last = eng.matmul(bank_l[:, t, :], c.XT[:, i * B * S + t * P:i * B * S + (t + 1) * P],
                                          c.m_router[:, i, :], start=i == 0, stop=i == DC - 1)
                last.then_inc(pe_logits, 1)
                eng.wait_ge(dve_route, BOTH_READY[0])
                eng.matmul(bank_r[:, :, :], c.below_b[:, :], both[:, TILES:, :], start=True, stop=False)
                for back in range(1, TILES):
                    eng.matmul(bank_r[:, :, :], c.ones_b[:, :], both[:, TILES - back:2 * TILES - back, :],
                               start=False, stop=back == TILES - 1)
                for t in range(TILES):
                    last = eng.matmul(bank_n[:, :], c.ones_b[:, :], both[:, TILES + t, :], start=t == 0, stop=t == TILES - 1)
                last.then_inc(pe_ranks, 1)

            @block.scalar
            def _(eng):
                eng.wait_ge(dve_route, EXP_READY[0])
                eng.activation(exps[:, :, :], less[:, :, :], ACT.Exp).then_inc(act_exps, 1)


def shared_expert(c):
    nc = c.nc
    with ExitStack() as stack:
        c.stack = stack
        bank_u = [c.psum(f"se_u{p}", (P, 2, S)) for p in range(2)]
        bank_y = [c.psum(f"se_y{p}", (P, 2, D)) for p in range(2)]
        act = [c.sb(f"se_act{k}", [P, S]) for k in range(2)]
        hidden = [c.sb(f"se_hidden{p}", [P, 2, S]) for p in range(2)]
        pe_u, act_u, dve_u, pe_y, dve_y = (c.sem("se_" + n) for n in ("pe_u", "act_u", "dve_u", "pe_y", "dve_y"))
        sent = c.sem("se_rows_sent")
        with nc.Block() as block:
            @block.gpsimd
            def _(eng):
                eng.wait_ge(c.sorted_cleared, 16)
                for s in range(SLOTS_E):
                    t = s // KE
                    eng.indirect_dma_start(c.d_sorted, bass.IndirectOffsetOnAxis(ap=c.places[:, s:s + 1], axis=0),
                                           c.X[:, t * D:(t + 1) * D], None).then_inc(sent, 16)
                eng.wait_ge(sent, 16 * SLOTS_E)

            @block.tensor
            def _(eng):
                def up(b):
                    for k in range(2):
                        if b.past(1):
                            eng.wait_ge(dve_u, b.back(1).count(2, k + 1))
                        for w in range(2):
                            for i in range(DC):
                                last = eng.matmul(bank_u[k][:, w, :], (c.s_gate, c.s_up)[w][:, i, k * P:(k + 1) * P],
                                                  c.XT[:, bass.ds(i * B * S + S * b.n, S)], start=i == 0, stop=i == DC - 1)
                        last.then_inc(pe_u, 1)

                def down(b):
                    eng.wait_ge(dve_u, b.count(2, 2))
                    if b.past(2):
                        eng.wait_ge(dve_y, b.back(2).count(1, 1))
                    for t in range(2):
                        for k in range(2):
                            last = eng.matmul(bank_y[b.par][:, t, :], hidden[b.par][:, k, t * P:(t + 1) * P],
                                              c.s_down[:, k, :], start=k == 0, stop=k == 1)
                    last.then_inc(pe_y, 1)
                laps(eng, [(up, (0,)), (down, (1,))], 4)

            @block.scalar
            def _(eng):
                def silu(b):
                    for k in range(2):
                        eng.wait_ge(pe_u, b.count(2, k + 1))
                        if b.past(1):
                            eng.wait_ge(dve_u, b.back(1).count(2, k + 1))
                        eng.activation(act[k][:, :], bank_u[k][:, 0, :], ACT.Silu).then_inc(act_u, 1)
                laps(eng, [(silu, (0,))], 2)

            @block.vector
            def _(eng):
                def hide(b):
                    for k in range(2):
                        eng.wait_ge(act_u, b.count(2, k + 1))
                        if b.past(2):
                            eng.wait_ge(pe_y, b.back(2).count(1, 1))
                        eng.tensor_tensor(hidden[b.par][:, k, :], act[k][:, :], bank_u[k][:, 1, :],
                                          ALU.mult).then_inc(dve_u, 1)

                def keep(b):
                    eng.wait_ge(pe_y, b.count(1, 1))
                    at = bass.ds(2 * D * b.n, 2 * D)
                    eng.tensor_tensor(c.with_shared[:, at].rearrange("p (t d) -> p t d", t=2), bank_y[b.par][:, :, :],
                                      c.X[:, at].rearrange("p (t d) -> p t d", t=2), ALU.add).then_inc(dve_y, 1)
                laps(eng, [(hide, (0,)), (keep, (1,))], 4)


def experts(c):
    nc = c.nc
    with ExitStack() as stack:
        c.stack = stack
        bank_x = [c.psum(f"ex_x{p}", (P, DC, P)) for p in range(2)]
        bank_u = [c.psum(f"ex_u{p}", (P, 2 * F)) for p in range(2)]
        bank_h = [c.psum(f"ex_h{p}", (P, 2, P)) for p in range(2)]
        bank_y = [c.psum(f"ex_y{p}", (P, D)) for p in range(2)]
        rows = [c.sb(f"ex_rows{p}", [P, D]) for p in range(2)]
        x_t = [c.sb(f"ex_x_t{p}", [P, DC, P]) for p in range(2)]
        act = [c.sb(f"ex_act{p}", [P, F]) for p in range(2)]
        hidden = [c.sb(f"ex_hidden{p}", [P, FP]) for p in range(2)]
        hidden_t = [c.sb(f"ex_hidden_t{p}", [P, 2, P]) for p in range(2)]
        y = [c.sb(f"ex_y_sb{p}", [P, D]) for p in range(2)]
        loaded, kept = c.sems("ex_loaded"), c.sems("ex_kept")
        pe_x, act_x, pe_u, act_u, dve_h = (c.sem("ex_" + n) for n in ("pe_x", "act_x", "pe_u", "act_u", "dve_h"))
        pe_h, dve_ht, pe_y, act_y = (c.sem("ex_" + n) for n in ("pe_h", "dve_ht", "pe_y", "act_y"))
        dve_init = c.sem("ex_dve_init")
        with nc.Block() as block:
            @block.sync
            def _(eng):
                def load(n):
                    if n.past(2):
                        eng.wait_ge(pe_x, n.back(2).count(1, 1))
                    eng.dma_start(rows[n.par][:, :], c.d_sorted[bass.ds(P * n.n, P), :]).then_inc(loaded[n.par], 16)

                def store(n):
                    eng.wait_ge(act_y, n.count(1, 1))
                    eng.dma_start(c.d_expert_out[bass.ds(P * n.n, P), :], y[n.par][:, :]).then_inc(kept[n.par], 16)
                laps(eng, [(load, (0,)), (store, (2,))], 4, MTILES)
                for p in range(2):
                    eng.wait_ge(kept[p], 16 * (MTILES // 2))

            @block.tensor
            def _(eng):
                eng.wait_ge(dve_init, 2)
                eng.wait_ge(c.in_w7, 16)

                def turn_x(n):
                    eng.wait_ge(loaded[n.par], n.landed(1))
                    if n.past(2):
                        eng.wait_ge(act_x, n.back(2).count(1, 1))
                    for i in range(DC):
                        last = eng.transpose(bank_x[n.par][:, i, :], rows[n.par][:, i * P:(i + 1) * P], c.ident[:, :])
                    last.then_inc(pe_x, 1)

                def turn_hidden(n):
                    eng.wait_ge(dve_h, n.count(1, 1))
                    if n.past(2):
                        eng.wait_ge(dve_ht, n.back(2).count(1, 1))
                    for k in range(2):
                        last = eng.transpose(bank_h[n.par][:, k, :], hidden[n.par][:, k * P:(k + 1) * P], c.ident[:, :])
                    last.then_inc(pe_h, 1)

                def up(n):
                    expert = eng.value_load(c.tile_expert[0:1, bass.ds(n.n, 1)], min_val=0, max_val=E - 1)
                    eng.wait_ge(act_x, n.count(1, 1))
                    if n.past(2):
                        eng.wait_ge(dve_h, n.back(2).count(1, 1))
                    for i in range(DC):
                        last = eng.matmul(bank_u[n.par][:, :], x_t[n.par][:, i, :],
                                          c.m_up[:, bass.ds(expert * (2 * F) + i * E * 2 * F, 2 * F)],
                                          start=i == 0, stop=i == DC - 1)
                    last.then_inc(pe_u, 1)

                def down(n):
                    expert = eng.value_load(c.tile_expert[0:1, bass.ds(n.n, 1)], min_val=0, max_val=E - 1)
                    eng.wait_ge(dve_ht, n.count(1, 1))
                    if n.past(2):
                        eng.wait_ge(act_y, n.back(2).count(1, 1))
                    for k in range(2):
                        last = eng.matmul(bank_y[n.par][:, :], hidden_t[n.par][:, k, :],
                                          c.m_down[:, bass.ds(expert * D + k * E * D, D)], start=k == 0, stop=k == 1)
                    last.then_inc(pe_y, 1)
                laps(eng, [(turn_x, (1,)), (turn_hidden, (2,)), (up, (1,)), (down, (2,))], 4, MTILES)

            @block.scalar
            def _(eng):
                def keep_x(n):
                    eng.wait_ge(pe_x, n.count(1, 1))
                    if n.past(2):
                        eng.wait_ge(pe_u, n.back(2).count(1, 1))
                    eng.activation(x_t[n.par][:, :, :], bank_x[n.par][:, :, :], ACT.Copy).then_inc(act_x, 1)

                def silu(n):
                    eng.wait_ge(pe_u, n.count(1, 1))
                    if n.past(2):
                        eng.wait_ge(dve_h, n.back(2).count(1, 1))
                    eng.activation(act[n.par][:, :], bank_u[n.par][:, 0:F], ACT.Silu).then_inc(act_u, 1)

                def keep_y(n):
                    eng.wait_ge(pe_y, n.count(1, 1))
                    if n.past(2):
                        eng.wait_ge(kept[n.back(2).par], n.back(2).landed(1))
                    eng.activation(y[n.par][:, :], bank_y[n.par][:, :], ACT.Copy).then_inc(act_y, 1)
                laps(eng, [(keep_x, (1,)), (silu, (1,)), (keep_y, (2,))], 4, MTILES)

            @block.vector
            def _(eng):
                for p in range(2):
                    eng.memset(hidden[p][:, F:FP], 0.0).then_inc(dve_init, 1)

                def turn(n):
                    eng.wait_ge(pe_h, n.count(1, 1))
                    if n.past(2):
                        eng.wait_ge(pe_y, n.back(2).count(1, 1))
                    eng.tensor_copy(hidden_t[n.par][:, :, :], bank_h[n.par][:, :, :]).then_inc(dve_ht, 1)

                def hide(n):
                    eng.wait_ge(act_u, n.count(1, 1))
                    if n.past(2):
                        eng.wait_ge(pe_h, n.back(2).count(1, 1))
                    eng.tensor_tensor(hidden[n.par][:, 0:F], act[n.par][:, :], bank_u[n.par][:, F:], ALU.mult).then_inc(dve_h, 1)
                laps(eng, [(turn, (2,)), (hide, (1,))], 4, MTILES)


def combine(c, out):
    nc = c.nc
    with ExitStack() as stack:
        c.stack = stack
        got = [c.sb(f"co_got{p}", [P, 2, KE, D]) for p in range(2)]
        total = [c.sb(f"co_total{p}", [P, 2, D]) for p in range(2)]
        stats, moments = c.sb("co_stats", [P, 2, 6]), [c.sb(f"co_moments{p}", [P, 2, 2]) for p in range(2)]
        spread, rstd = c.sb("co_spread", [P, 2]), [c.sb(f"co_rstd{p}", [P, 2]) for p in range(2)]
        rows = [c.sb(f"co_rows{p}", [P, 2, D]) for p in range(2)]
        fetched, stored = c.sems("co_fetched"), c.sems("co_stored")
        SUMMED, MOMENTS, NORMED, SCALED = 2 * KE, 2 * KE + 4, 2, 2
        dve_sum, dve_norm, pool_rstd = c.sem("co_dve_sum"), c.sem("co_dve_norm"), c.sem("co_pool_rstd")
        dst = out.rearrange("b (t p) d -> b p t d", p=P)
        with nc.Block() as block:
            @block.gpsimd
            def _(eng):
                def fetch(b):
                    if b.past(2):
                        eng.wait_ge(dve_sum, b.back(2).count(MOMENTS, SUMMED))
                    for t in range(2):
                        for k in range(KE):
                            s = (2 * b.n + t) * KE + k
                            eng.indirect_dma_start(got[b.par][:, t, k, :], None, c.d_expert_out,
                                                   bass.IndirectOffsetOnAxis(ap=c.places[:, s:s + 1], axis=0)
                                                   ).then_inc(fetched[b.par], 16)

                def scale(b):
                    eng.wait_ge(dve_sum, b.count(MOMENTS, MOMENTS))
                    if b.past(1):
                        eng.wait_ge(pool_rstd, b.back(1).count(SCALED, SCALED))
                    eng.tensor_scalar(spread[:, :], moments[b.par][:, :, 1], EPS, None, ALU.add).then_inc(pool_rstd, 1)
                    eng.wait_ge(pool_rstd, b.count(SCALED, 1))
                    if b.past(2):
                        eng.wait_ge(dve_norm, b.back(2).count(NORMED, NORMED))
                    eng.tensor_tensor(rstd[b.par][:, :], spread[:, :], c.minus_half[:, :], ALU.pow).then_inc(pool_rstd, 1)
                laps(eng, [(fetch, (0,)), (scale, (1,))], B)

            @block.vector
            def _(eng):
                sums = Count(MOMENTS)

                def add_up(b):
                    sums.begin(b)
                    eng.wait_ge(fetched[b.par], b.landed(2 * KE))
                    if b.past(2):
                        eng.wait_ge(dve_norm, b.back(2).count(NORMED, NORMED))
                    for k in range(KE):
                        for t in range(2):
                            s = (2 * b.n + t) * KE + k
                            before = (total[b.par][:, t, :] if k else
                                      c.with_shared[:, (2 * b.n + t) * D:(2 * b.n + t + 1) * D])
                            eng.scalar_tensor_tensor(total[b.par][:, t, :], got[b.par][:, t, k, :],
                                                     c.row_weights[:, s:s + 1], before, ALU.mult, ALU.add).then_inc(dve_sum, sums.one())
                        eng.wait_ge(dve_sum, sums.so_far())
                    for t in range(2):
                        eng.bn_stats(stats[:, t, :], total[b.par][:, t, :]).then_inc(dve_sum, sums.one())
                    eng.wait_ge(dve_sum, sums.so_far())
                    if b.past(2):
                        eng.wait_ge(pool_rstd, b.back(2).count(SCALED, 1))
                    for t in range(2):
                        eng.bn_aggr(moments[b.par][:, t, :], stats[:, t, :]).then_inc(dve_sum, sums.one())
                    eng.wait_ge(dve_sum, sums.so_far())
                    sums.end()

                def normalise(b):
                    eng.wait_ge(pool_rstd, b.count(SCALED, SCALED))
                    if b.past(2):
                        eng.wait_ge(stored[b.back(2).par], b.back(2).landed(1))
                    for t in range(2):
                        eng.tensor_scalar(rows[b.par][:, t, :], total[b.par][:, t, :], moments[b.par][:, t, 0:1],
                                          rstd[b.par][:, t:t + 1], ALU.subtract, ALU.mult).then_inc(dve_norm, 1)
                laps(eng, [(add_up, (0,)), (normalise, (1,))], B)

            @block.sync
            def _(eng):
                def store(b):
                    eng.wait_ge(dve_norm, b.count(NORMED, NORMED))
                    eng.dma_start(dst[b.n], rows[b.par][:, :, :]).then_inc(stored[b.par], 16)
                laps(eng, [(store, (0,))], B)
                for p in range(2):
                    eng.wait_ge(stored[p], 16 * (B // 2))




CONST = {"ident": P, "iota": NKEYS, "rank": TOP, "tri": S, "earlier": E * E}
CONST_B = {"ident": P, "below": P, "ones": P}
PACK2 = {"q": DC * D, "k": DC * D, "v": DC * D, "o": DC * D}
PACK3 = {"query": DC * RETR, "keys": 2 * P, "down_embed": DC * EXPERTS, "up_embed": EB * D, "gate": DC * INTER,
         "up": DC * INTER, "down": FB * D}
PACK4 = {"kv": DC * 2 * D, "q": DC * D, "o": DC * D}
PACK5 = {"q": DC * D, "p": DC * D, "k": DC * D, "v": DC * D, "ctx_all": DC * B * CTX, "ctx_twice": DC * B * P,
         "bq": DC, "bk": DC, "bv": D, "bp": 2 * D, "head_of": HB, "half_of": 2 * HD}
PACK6 = {"router": DC * E, "bias": E, "s_gate": DC * FP, "s_up": DC * FP, "s_down": DC * D, "up": DC * E * 2 * F}
PACK1 = {"w_q": DC * D, "w_k": DC * D, "w_v": DC * D, "w_o": GROUPS * D, "b_q": DC, "b_k": DC, "bv_twice": 2 * D}


def views(tile, widths):
    at, out = 0, {}
    for name, n in widths.items():
        out[name] = tile[:, at:at + n]
        at += n
    return out


def blocks(view, n):
    return view.rearrange("p (k n) -> p k n", k=n)


def decoder(nc, x, xt, const, const_b, pack1, pack2, pack3, pack4, pack5, pack6, pack7, ctx, ctx_t, out):
    c = Chip(nc)
    with c.whole:
        c.X = c.sb("X", [P, TILES * D])
        c.XT = c.sb("XT", [P, DC * B * S])
        c.minus_half = c.sb("minus_half", [P, 2])
        const_sb = c.sb("const", [P, sum(CONST.values())])
        c.ident, c.iota, c.rank, c.tri, c.earlier = views(const_sb, CONST).values()
        const_b_sb = c.sb("const_b", [P, sum(CONST_B.values())], BF16)
        c.ident_b, c.below_b, c.ones_b = views(const_b_sb, CONST_B).values()
        c.pool_const = c.sem("pool_const")
        c.in_first, c.in_x, c.in_packs, c.in_w6, c.in_w7 = (c.sem("in_" + n) for n in ("first", "x", "packs", "w6", "w7"))
        c.d_parts = [nc.dram_tensor(f"parts_{w}", [B, 3, D, S], BF16, kind="Internal").ap() for w in "qk"]
        c.d_sorted = nc.dram_tensor("sorted_rows", [MTILES * P, D], F32, kind="Internal").ap()
        c.d_expert_out = nc.dram_tensor("expert_out", [MTILES * P, D], F32, kind="Internal").ap()
        c.d_ctx, c.d_ctx_t = ctx, ctx_t
        c.sorted_cleared = c.sem("sorted_cleared")
        zeros = c.sb("zeros", [P, D])
        w4, w5 = c.sb("pack4", [P, sum(PACK4.values())]), c.sb("pack5", [P, sum(PACK5.values())])
        v4, v5 = views(w4, PACK4), views(w5, PACK5)
        c.r_kv, c.r_q, c.r_o = (blocks(v4[n], DC) for n in ("kv", "q", "o"))
        c.a_q, c.a_p, c.a_k, c.a_v, c.ctx_all, c.ctx_twice = (
            blocks(v5[n], DC) for n in ("q", "p", "k", "v", "ctx_all", "ctx_twice"))
        c.a_bq, c.a_bk, c.a_bv, c.a_bp, c.head_of, c.half_of = (
            v5[n] for n in ("bq", "bk", "bv", "bp", "head_of", "half_of"))
        with ExitStack() as first_layer:
            c.stack = first_layer
            w1, w2, w3 = (c.sb(n, [P, sum(pack.values())])
                          for n, pack in (("pack1", PACK1), ("pack2", PACK2), ("pack3", PACK3)))
            v1, v2, v3 = views(w1, PACK1), views(w2, PACK2), views(w3, PACK3)
            c.w_qk, c.b_qk = [blocks(v1["w_q"], DC), blocks(v1["w_k"], DC)], [v1["b_q"], v1["b_k"]]
            c.w_v, c.w_o, c.bv_twice = blocks(v1["w_v"], DC), blocks(v1["w_o"], GROUPS), v1["bv_twice"]
            c.x0_q, c.x0_k, c.x0_v, c.x0_o = (blocks(v2[n], DC) for n in "qkvo")
            c.w_query, c.keys, c.w_down_embed = (
                blocks(v3["query"], DC), blocks(v3["keys"], 2), blocks(v3["down_embed"], DC))
            c.w_up_embed, c.f_gate, c.f_up = blocks(v3["up_embed"], EB), blocks(v3["gate"], DC), blocks(v3["up"], DC)
            c.f_down = blocks(v3["down"], FB)
            attention_operands = first_layer.enter_context(ExitStack())
            c.stack = attention_operands
            c.qs = [c.sb(f"qs{p}", [P, H, S], BF16) for p in range(2)]
            c.ks = [c.sb(f"ks{p}", [P, H, S], BF16) for p in range(2)]
            c.v = [c.sb(f"v{p}", [P, 2, H, 2 * HD]) for p in range(2)]
            def load_packs(eng):
                for tile, pack in ((w2, pack2), (w3, pack3), (w4, pack4), (w5, pack5)):
                    eng.dma_start(tile[:, :], pack).then_inc(c.in_packs, 16)
            c.load_packs = load_packs
            c.operands_init, c.q_in, c.k_in = c.sem("operands_init"), c.sems("q_in"), c.sems("k_in")
            with nc.Block() as block:
                @block.sync
                def _(eng):
                    eng.dma_start(c.XT[:, :], xt).then_inc(c.in_first, 16)
                    eng.dma_start(w1[:, :], pack1).then_inc(c.in_first, 16)
                    eng.dma_start(c.X[:, :], x).then_inc(c.in_x, 16)
                    eng.dma_start(const_sb[:, :], const).then_inc(c.in_x, 16)
                    eng.dma_start(const_b_sb[:, :], const_b).then_inc(c.in_x, 16)

                @block.gpsimd
                def _(eng):
                    eng.memset(zeros[:, :], 0.0).then_inc(c.pool_const, 1)
                    eng.memset(c.minus_half[:, :], -0.5).then_inc(c.pool_const, 1)
            project_heads(c)
            attention(c)
            attention_operands.close()
            c.stack = first_layer
            c.R = c.sb("R", [P, TILES * P])
            context_attention(c)
            route_scores(c)
            feed_forward(c)
        with ExitStack() as mixture:
            c.stack = mixture
            w6 = c.sb("pack6", [P, sum(PACK6.values())])
            v6 = views(w6, PACK6)
            c.m_router, c.s_gate, c.s_up, c.s_down = (blocks(v6[n], DC) for n in ("router", "s_gate", "s_up", "s_down"))
            c.m_bias, c.m_up = v6["bias"], v6["up"]
            def load_mixture(eng):
                eng.dma_start(w6[:, :], pack6).then_inc(c.in_w6, 16)
                eng.dma_start(c.d_sorted.rearrange("(n p) d -> p n d", p=P),
                              zeros[:, :].unsqueeze(1).broadcast_to([P, MTILES, D])).then_inc(c.sorted_cleared, 16)
            c.load_mixture = load_mixture
            running_sum(c)
            rounded_attention(c)
            c.stack = mixture
            c.with_shared = c.sb("with_shared", [P, TILES * D])
            c.row_weights, c.places = c.sb("row_weights", [P, SLOTS_E]), c.sb("places", [P, SLOTS_E], U32)
            c.tile_expert = c.sb("tile_expert", [P, MTILES], I32)
            c.m_down = c.sb("m_down", [P, DC * E * D])
            c.load_down = lambda eng: eng.dma_start(c.m_down[:, :], pack7).then_inc(c.in_w7, 16)
            route_experts(c)
            shared_expert(c)
            experts(c)
            combine(c, out)


def k_major(w):
    k, n = w.shape
    return np.ascontiguousarray(w.reshape(k // P, P, n).transpose(1, 0, 2)).reshape(P, -1)


def padded_out_weight(wo, bo):
    w = np.zeros((GROUPS, G, 2 * HD, D), np.float32)
    w[:, :, :HD] = wo.reshape(GROUPS, G, HD, D)
    w[0, 0, HD] = bo
    return np.ascontiguousarray(w.transpose(1, 2, 0, 3)).reshape(P, -1)


def kernel(**inputs):
    import concourse.bacc as bacc
    from concourse.bass_utils import run_bass_kernel_spmd

    a = {k: np.asarray(v) for k, v in inputs.items()}
    x = a["x"].reshape(B * S, D)
    ident = np.eye(P, dtype=np.float32)
    pack1 = np.concatenate([
        k_major(a["L0_attn_wq"]), k_major(a["L0_attn_wk"]), k_major(a["L0_attn_wv"]),
        padded_out_weight(a["L0_attn_wo"], a["L0_attn_bo"]),
        a["L0_attn_bq"].reshape(DC, P).T, a["L0_attn_bk"].reshape(DC, P).T,
        np.tile(a["L0_attn_bv"][None, :], (P, 2))], axis=1)
    keys = np.zeros((2, P, P), np.float32)
    for half in range(2):
        keys[:, half * NKEYS:(half + 1) * NKEYS, half * NKEYS:(half + 1) * NKEYS] = a["L0_ffn_keys"]
    pack2 = np.concatenate([k_major(a["L0_xattn_w" + n].T) for n in "qkvo"], axis=1)
    pack3 = np.concatenate([k_major(a["L0_ffn_W_q"]), k_major(keys.reshape(2 * P, P)), k_major(a["L0_ffn_down_embed"].T),
                            k_major(a["L0_ffn_up_embed"]), k_major(a["L0_ffn_gate_w"]), k_major(a["L0_ffn_up_w"]),
                            k_major(a["L0_ffn_down_w"])], axis=1)
    pack4 = np.concatenate([k_major(np.concatenate([a["L1_attn_Wk"].T, a["L1_attn_Wv"].T], axis=1)),
                            k_major(a["L1_attn_Wq"].T), k_major(a["L1_attn_Wo"].T)], axis=1)
    ctx = a["ctx_2048"]
    ctx_t_all = np.ascontiguousarray(ctx.reshape(B * CTX, D).T)
    part = np.arange(P)[:, None]
    pack5 = np.concatenate([
        k_major(a["L1_xattn_wq"]), k_major(a["L1_xattn_wp"]), k_major(a["L1_xattn_wkv"][:D].T),
        k_major(a["L1_xattn_wkv"][D:].T), k_major(ctx_t_all),
        k_major(np.repeat(ctx_t_all.reshape(D, B, 1, CTX), 2, axis=2).reshape(D, B * P)),
        a["L1_xattn_bq"].reshape(DC, P).T, a["L1_xattn_bkv"][:D].reshape(DC, P).T,
        np.tile(a["L1_xattn_bkv"][None, D:], (P, 1)), np.tile(a["L1_xattn_bp"][None, :], (P, 2)),
        (part // HD == np.arange(HB)).astype(np.float32),
        (part // CTX == np.arange(2 * HD) // HD).astype(np.float32)], axis=1)
    up = np.concatenate([a["L1_ffn_w_gate"], a["L1_ffn_w_up"]], axis=1)
    down = np.pad(a["L1_ffn_w_down"].transpose(2, 0, 1), ((0, FP - F), (0, 0), (0, 0)))
    pad = ((0, 0), (0, FP - F))
    pack6 = np.concatenate([
        k_major(a["L1_ffn_gate_w"].T), np.tile(a["L1_ffn_expert_bias"][None, :], (P, 1)),
        k_major(np.pad(a["L1_ffn_sw_gate"].T, pad)), k_major(np.pad(a["L1_ffn_sw_up"].T, pad)),
        k_major(np.pad(a["L1_ffn_sw_down"].T, pad[::-1])), k_major(up.transpose(2, 0, 1).reshape(D, -1))],
        axis=1)
    earlier = np.tile(np.tri(E, E, -1, dtype=np.float32).reshape(1, -1), (P, 1))
    iota = np.tile(np.arange(NKEYS, dtype=np.float32), (P, 1))
    tri = np.triu(np.full((P, S), D ** 0.5 / S, np.float32))
    arrays = {
        "x": k_major(x), "xt": k_major(np.ascontiguousarray(x.T)),
        "const": np.concatenate([ident, iota, iota[:, :TOP] - TOP, tri, earlier], axis=1),
        "const_b": np.concatenate([ident, np.triu(np.ones((P, P)), 1), np.ones((P, P))], axis=1).astype(np_bf16()),
        "pack1": pack1, "pack2": pack2, "pack3": pack3, "pack4": pack4, "pack5": pack5, "pack6": pack6, "pack7": k_major(down.reshape(FP, -1)), "ctx": ctx,
        "ctx_t": np.ascontiguousarray(ctx.transpose(0, 2, 1).reshape(B, DC, P, CTX).transpose(0, 2, 1, 3))}
    nc = bacc.Bacc("TRN2", target_bir_lowering=False, num_devices=1)
    args = [nc.dram_tensor("in_" + n, v.shape, mybir.dt.from_np(v.dtype), kind="ExternalInput").ap()
            for n, v in arrays.items()]
    out = nc.dram_tensor("out", [B, S, D], F32, kind="ExternalOutput").ap()
    decoder(nc, *args, out)
    r = run_bass_kernel_spmd(nc, [{"in_" + n: v for n, v in arrays.items()}], core_ids=[0])
    return r.results[0]["out"]


def np_bf16():
    return mybir.dt.np(BF16)
```

```python
from contextlib import ExitStack

import numpy as np
import concourse.bass as bass
from concourse import mybir

P = 128
B, S, D = 8, 256, 256
DC = D // P
TILES = B * S // P
H, HD = 16, 16
CTX = 64
EPS = 1e-5

ALU = mybir.AluOpType
ACT = mybir.ActivationFunctionType
AX = mybir.AxisListType
F32 = mybir.dt.float32
BF16 = mybir.dt.bfloat16
U32 = mybir.dt.uint32


class Lap:

    def __init__(self, low, i=None, unroll=2):
        self.low, self.i, self.unroll = low, i, unroll
        self.n, self.par, self.looped = self.rounds(1), low % 2, i is not None

    def rounds(self, buffers):
        assert self.unroll % buffers == 0
        return self.low // buffers if self.i is None else self.unroll // buffers * self.i + self.low // buffers

    def back(self, k):
        return Lap(self.low - k, self.i, self.unroll)

    def past(self, k):
        assert self.low >= k or not self.looped, "peel more rounds"
        return self.low >= k

    def count(self, per, k):
        return per * self.n + k

    def landed(self, dmas, buffers=2):
        return 16 * dmas * self.rounds(buffers) + 16 * dmas


def laps(eng, steps, start, count=B, unroll=2, begin=0):
    last = max(max(lags) for _, lags in steps)
    assert (count - start) % unroll == start % 2 == unroll % 2 == 0 and (start >= last or start == count)

    def one_round(r, lap_of):
        for step, lags in steps:
            args = [lap_of(r - lag) if begin <= r - lag and (r < start or r - lag < count) else None for lag in lags]
            if any(args):
                step(*args)

    def peeled(n):
        return Lap(n, None, unroll) if n < count else None

    for r in range(begin, start):
        one_round(r, peeled)
    if count > start:
        with eng.Fori(0, (count - start) // unroll) as i:
            for r in range(start, start + unroll):
                one_round(r, lambda n: Lap(n, i, unroll))
    for r in range(count, count + last):
        one_round(r, peeled)


def apart(c, eng):
    eng.nop(nofuse=True)


class Count:

    def __init__(self, per):
        self.per, self.lap, self.k = per, 0, 0

    def begin(self, lap):
        self.lap, self.k = lap.n, 0

    def one(self):
        self.k += 1
        return 1

    def so_far(self):
        return self.per * self.lap + self.k

    def end(self):
        assert self.k == self.per, (self.k, self.per)


class Chip:

    def __init__(self, nc):
        self.nc = nc
        self.whole = ExitStack()
        self.stack = self.whole

    def sb(self, name, shape, dt=F32):
        return self.stack.enter_context(self.nc.sbuf_tensor(name, shape, dt))

    def psum(self, name, shape=(P, 512), dt=F32):
        return self.stack.enter_context(self.nc.psum_tensor(name, list(shape), dt))

    def sem(self, name):
        return self.whole.enter_context(self.nc.semaphore(name))

    def sems(self, name):
        return [self.sem(f"{name}_even"), self.sem(f"{name}_odd")]


class Norm:
    SUMMED, NORMED, PER = 1, 7, 7
    SCALED, KEPT, POOL_PER = 2, 3, 3

    def __init__(self, c, name, y_bank, y_done, t_bank, residual=None):
        self.c, self.residual = c, residual
        self.y, self.y_done, self.t = y_bank, y_done, t_bank
        self.dve_norm = c.sem(name + "_dve_norm")
        self.pool_scale = c.sem(name + "_pool_scale")
        self.pe_turned = c.sem(name + "_pe_turned")
        self.act_turned = c.sem(name + "_act_turned")
        self.sum = c.sb(name + "_sum", [P, 2, D])
        self.stats = c.sb(name + "_stats", [P, 2, 6])
        self.moments = c.sb(name + "_moments", [P, 2, 2, 2])
        self.spread = c.sb(name + "_spread", [P, 2])
        self.rstd = c.sb(name + "_rstd", [P, 2, 2])
        self.rows = [c.sb(name + f"_rows{p}", [P, 2, D]) for p in range(2)]

    def dve(self, eng):
        chain = Count(self.PER)

        def sum_up(b):
            chain.begin(b)
            mom = self.moments[:, b.par]
            self.y_done(eng, b)
            if b.past(1):
                eng.wait_ge(self.dve_norm, b.back(1).count(self.PER, self.NORMED))
            if self.residual:
                x, ready = self.residual
                ready(eng, b)
            else:
                x = self.c.X[:, bass.ds(2 * D * b.n, 2 * D)].rearrange("p (t d) -> p t d", t=2)
            eng.tensor_tensor(self.sum[:, :, :], self.y, x, ALU.add).then_inc(self.dve_norm, chain.one())
            eng.wait_ge(self.dve_norm, chain.so_far())
            for t in range(2):
                eng.bn_stats(self.stats[:, t, :], self.sum[:, t, :]).then_inc(self.dve_norm, chain.one())
            eng.wait_ge(self.dve_norm, chain.so_far())
            if b.past(2):
                eng.wait_ge(self.pool_scale, b.back(2).count(self.POOL_PER, self.SCALED))
            apart(self.c, eng)
            for t in range(2):
                eng.bn_aggr(mom[:, t, :], self.stats[:, t, :]).then_inc(self.dve_norm, chain.one())
            eng.wait_ge(self.dve_norm, chain.so_far())

        def normalise(b):
            eng.wait_ge(self.pool_scale, b.count(self.POOL_PER, self.SCALED))
            mom = self.moments[:, b.par]
            if b.past(2):
                eng.wait_ge(self.pool_scale, b.back(2).count(self.POOL_PER, self.KEPT))
            if b.past(2):
                eng.wait_ge(self.pe_turned, b.back(2).count(1, 1))
            for t in range(2):
                eng.tensor_scalar(self.rows[b.par][:, t, :], self.sum[:, t, :], mom[:, t, 0:1],
                                  self.rstd[:, b.par, t:t + 1], ALU.subtract, ALU.mult).then_inc(self.dve_norm, chain.one())
            chain.end()
        return sum_up, normalise

    def pool(self, eng):
        chain = Count(self.POOL_PER)

        def step(b):
            chain.begin(b)
            eng.wait_ge(self.dve_norm, b.count(self.PER, 5))
            if b.past(1):
                eng.wait_ge(self.pool_scale, b.back(1).count(self.POOL_PER, self.SCALED))
            apart(self.c, eng)
            eng.tensor_scalar(self.spread[:, :], self.moments[:, b.par, :, 1], EPS, None, ALU.add).then_inc(self.pool_scale, chain.one())
            eng.wait_ge(self.pool_scale, chain.so_far())
            if b.past(2):
                eng.wait_ge(self.dve_norm, b.back(2).count(self.PER, self.NORMED))
            eng.tensor_tensor(self.rstd[:, b.par, :], self.spread[:, :], self.c.minus_half[:, :], ALU.pow).then_inc(self.pool_scale, chain.one())
            eng.wait_ge(self.dve_norm, b.count(self.PER, self.NORMED))
            apart(self.c, eng)
            eng.tensor_copy(self.c.X[:, bass.ds(2 * D * b.n, 2 * D)],
                            self.rows[b.par][:, :, :].rearrange("p t d -> p (t d)")).then_inc(self.pool_scale, chain.one())
            chain.end()
        return step

    def pe(self, eng, bank_free=None):
        def step(b):
            eng.wait_ge(self.dve_norm, b.count(self.PER, self.NORMED))
            if b.past(1):
                eng.wait_ge(self.act_turned, b.back(1).count(1, 1))
            if bank_free:
                bank_free(eng, b)
            for t in range(2):
                for j in range(DC):
                    last = eng.transpose(self.t[:, (2 * j + t) * P:(2 * j + t + 1) * P],
                                         self.rows[b.par][:, t, j * P:(j + 1) * P], self.c.ident[:, :])
            last.then_inc(self.pe_turned, 1)
        return step

    def act(self, eng):
        def step(b):
            eng.wait_ge(self.pe_turned, b.count(1, 1))
            for j in range(DC):
                last = eng.activation(self.c.XT[:, bass.ds(j * B * S + S * b.n, S)], self.t[:, j * S:(j + 1) * S],
                                      ACT.Copy)
            last.then_inc(self.act_turned, 1)
        return step


class Fetch:

    def __init__(self, c, name, readers_done):
        self.c, self.readers_done = c, readers_done
        self.tile = [c.sb(name + f"_x{p}", [P, DC, S]) for p in range(2)]
        self.pool_x = c.sem(name + "_pool_x")

    def pool(self, eng):
        def step(b):
            if b.past(2):
                self.readers_done(eng, b.back(2))
            x = self.c.XT[:, :].rearrange("p (j t) -> p j t", j=DC)[:, :, bass.ds(S * b.n, S)]
            apart(self.c, eng)
            eng.tensor_copy(self.tile[b.par][:, :, :], x).then_inc(self.pool_x, 1)
        return step

    def ready(self, eng, b):
        eng.wait_ge(self.pool_x, b.count(1, 1))




SLOTS = 6
RUNS = ((0, 3), (3, 2), (5, 1))
MAX_ROW = SLOTS * HD
G = 4
GROUPS = H // G
UNITS = 2 * GROUPS


def load_parts(c, eng, b, half):
    heads = slice(half * H // 2, (half + 1) * H // 2)
    for run, (slot, length) in enumerate(RUNS):
        for dst, parts in ((c.qs, c.d_parts[0][bass.ds(b.n, 1), run:run + 1]), (c.ks, c.d_parts[1][bass.ds(b.n, 1), 0:length])):
            src = parts.rearrange("o c (d h) t -> (o c) d h t", h=H)[:, :, heads, :].broadcast_to([length, HD, H // 2, S])
            eng.dma_start(dst[b.par][HD * slot:HD * (slot + length), heads, :].rearrange("p h t -> p (h t)"),
                          src.rearrange("c d h t -> c d (h t)")).then_inc(c.parts_in[half][b.par], 16)


def project_heads(c):
    nc = c.nc
    with ExitStack() as stack:
        c.stack = stack
        banks = [[c.psum(f"ph_{w}{p}", (P, DC, S)) for p in range(2)] for w in "qk"]
        full = [[c.sb(f"ph_full_{w}{p}", [P, DC, S]) for p in range(2)] for w in "qk"]
        parts = [[c.sb(f"ph_parts_{w}{p}", [P, 3, DC, S], BF16) for p in range(2)] for w in "qk"]
        rest = [c.sb(f"ph_rest_{w}", [P, DC, S]) for w in "qk"]
        pe_proj = c.sem("ph_pe_proj")
        act_full = c.sem("ph_act_full")
        split = [c.sem("ph_dve_split_q"), c.sem("ph_dve_split_k")]
        stored = [c.sems("ph_stored_q"), c.sems("ph_stored_k")]

        with nc.Block() as block:
            @block.tensor
            def _(eng):
                eng.wait_ge(c.in_first, 16 * 2)

                def project(b):
                    if b.past(2):
                        eng.wait_ge(c.in_xt, 16)
                    for w in range(2):
                        if b.past(2):
                            eng.wait_ge(act_full, b.back(2).count(6, 2 * w + 2))
                        for j in range(DC):
                            for k in range(DC):
                                last = eng.matmul(banks[w][b.par][:, j, :], c.w_qk[w][:, k, j * P:(j + 1) * P],
                                                  c.XT[:, bass.ds(k * B * S + S * b.n, S)],
                                                  start=k == 0, stop=k == DC - 1)
                        last.then_inc(pe_proj, 1)
                laps(eng, [(project, (0,))], 2)

            @block.scalar
            def _(eng):
                def add_bias(b):
                    for w in range(2):
                        eng.wait_ge(pe_proj, b.count(2, w + 1))
                        if b.past(2):
                            eng.wait_ge(split[w], b.back(2).count(3, 1))
                        for j in range(DC):
                            eng.activation(full[w][b.par][:, j, :], banks[w][b.par][:, j, :], ACT.Identity,
                                           bias=c.b_qk[w][:, j:j + 1]).then_inc(act_full, 1)
                    for w in range(2):
                        eng.wait_ge(act_full, b.count(6, 2 * w + 2))
                        if b.past(2):
                            eng.wait_ge(stored[w][b.back(2).par], b.back(2).landed(1))
                        eng.activation(parts[w][b.par][:, 0], full[w][b.par][:, :, :], ACT.Copy).then_inc(act_full, 1)
                laps(eng, [(add_bias, (0,))], 2)

            @block.vector
            def _(eng):
                chains = Count(3), Count(3)

                def split_up(b):
                    for w in range(2):
                        chains[w].begin(b)
                        eng.wait_ge(act_full, b.count(6, 5 + w))
                        eng.wait_ge(split[w], chains[w].so_far())
                        eng.tensor_tensor(rest[w][:, :, :], full[w][b.par][:, :, :], parts[w][b.par][:, 0],
                                          ALU.subtract).then_inc(split[w], chains[w].one())
                    for w in range(2):
                        eng.wait_ge(split[w], chains[w].so_far())
                        if b.past(2):
                            eng.wait_ge(stored[w][b.back(2).par], b.back(2).landed(1))
                        apart(c, eng)
                        eng.tensor_copy(parts[w][b.par][:, 1], rest[w][:, :, :]).then_inc(split[w], chains[w].one())
                    for w in range(2):
                        eng.wait_ge(split[w], chains[w].so_far())
                        eng.tensor_tensor(parts[w][b.par][:, 2], rest[w][:, :, :], parts[w][b.par][:, 1],
                                          ALU.subtract).then_inc(split[w], chains[w].one())
                        chains[w].end()
                laps(eng, [(split_up, (0,))], 2)

            @block.gpsimd
            def _(eng):
                fills = [fill for p in range(2) for fill in (
                    (c.qs[p][MAX_ROW:P, :, :], 0.0), (c.ks[p][MAX_ROW:P, :, :], 0.0), (c.ks[p][MAX_ROW:MAX_ROW + 2, :, :], 1.0),
                    (c.v[p][:, :, :, HD:HD + 1], 1.0), (c.v[p][:, :, :, HD + 1:], 0.0))]
                for n, (place, value) in enumerate(fills):
                    eng.memset(place, value).then_inc(c.operands_init, 1)
                    eng.wait_ge(c.operands_init, n + 1)

            @block.sync
            def _(eng):
                def store(b):
                    for w in range(2):
                        eng.wait_ge(act_full, b.count(6, 5 + w))
                        eng.wait_ge(split[w], b.count(3, 3))
                        eng.dma_start(c.d_parts[w][bass.ds(b.n, 1)].rearrange("o c (j p) t -> p (o c j) t", p=P),
                                      parts[w][b.par][:, :, :, :].rearrange("p c j t -> p (c j) t")
                                      ).then_inc(stored[w][b.par], 16)

                def load_first(b):
                    if b.low == 3 and not b.looped:
                        eng.wait_ge(c.operands_init, 10)
                        for w in range(2):
                            eng.wait_ge(stored[w][0], 16)
                        load_parts(c, eng, Lap(0), 0)
                laps(eng, [(store, (0,)), (load_first, (0,))], 4)
                for w in range(2):
                    for p in range(2):
                        eng.wait_ge(stored[w][p], 16 * (B // 2))


def attention(c):
    nc = c.nc
    with ExitStack() as stack:
        c.stack = stack
        bank_row = c.psum("at_row", (P, G, S))
        bank_col = c.psum("at_col", (P, G, S))
        bank_a = c.psum("at_a")
        bank_b = c.psum("at_b")
        bank_o = c.psum("at_o", (P, 2, S))
        bank_y = c.psum("at_y", (P, 2, D))
        turned_max_ps = bank_b[:, 0:P].bitcast(BF16)
        qs, ks, v = c.qs, c.ks, c.v
        probs = [c.sb(f"at_probs{p}", [P, 2, G, S]) for p in range(2)]
        neg_max = c.sb("at_neg_max", [P, 2, H])
        max_parts = c.sb("at_max_parts", [P, 2, 2, H], BF16)
        turned_max = c.sb("at_turned_max", [2 * H, S], BF16)
        o_raw = [c.sb(f"at_o_raw{p}", [P, 2, S]) for p in range(2)]
        squares, divided = c.sb("at_squares", [P, 2 * S]), c.sb("at_divided", [P, 2 * S])
        recip = c.sb("at_recip", [P, S // HD])
        o_t = c.sb("at_o_t", [P, GROUPS, S])

        max_in = c.sems("at_max_in")
        pe_v, dve_v = c.sem("at_pe_v"), c.sem("at_dve_v")
        ROWS = 2 * UNITS
        MAX_PER = ROWS + 2
        pe_row, dve_max = c.sem("at_pe_row"), c.sem("at_dve_max")
        pe_max, act_max = c.sem("at_pe_max"), c.sem("at_act_max")
        pe_col, act_exp = c.sem("at_pe_col"), c.sem("at_act_exp")
        pe_pv, act_o = c.sem("at_pe_pv"), c.sem("at_act_o")
        dve_div, DIV = c.sem("at_dve_div"), 8
        pe_y = c.sem("at_pe_y")
        norm = Norm(c, "n1", bank_y[:, :, :], lambda eng, b: eng.wait_ge(pe_y, b.count(1, 1)), bank_a)
        fetch = Fetch(c, "at", lambda eng, b: eng.wait_ge(pe_v, b.count(1, 1)))

        with nc.Block() as block:
            @block.tensor
            def _(eng):
                def rows_bank(b, r):
                    g, t, pair = r // 4, r // 2 % 2, r % 2
                    if r % (ROWS // 2) == 0:
                        half = 2 * r // ROWS
                        eng.wait_ge(c.parts_in[half][b.par], b.landed(2 * len(RUNS)))
                    if r >= 2:
                        eng.wait_ge(dve_max, b.count(MAX_PER, r - 1))
                    elif b.past(1):
                        eng.wait_ge(dve_max, b.back(1).count(MAX_PER, ROWS - 1 + r))
                    for i in (2 * pair, 2 * pair + 1):
                        h = G * g + i
                        last = eng.matmul(bank_row[:, i, :], qs[b.par][0:MAX_ROW, h, t * P:(t + 1) * P],
                                          ks[b.par][0:MAX_ROW, h, :], start=True, stop=True)
                    last.then_inc(pe_row, 1)

                def cols_unit(b, u):
                    g, t = divmod(u, 2)
                    if u == 0:
                        eng.wait_ge(max_in[b.par], b.landed(2))
                        if b.past(1):
                            eng.wait_ge(act_exp, b.back(1).count(UNITS, UNITS))
                    else:
                        eng.wait_ge(act_exp, b.count(UNITS, u))
                    for i in range(G):
                        h = G * g + i
                        last = eng.matmul(bank_col[:, i, :], ks[b.par][:, h, t * P:(t + 1) * P],
                                          qs[b.par][:, h, :], start=True, stop=True)
                    last.then_inc(pe_col, 1)

                def pv(b, g):
                    eng.wait_ge(act_exp, b.count(UNITS, 2 * g + 2))
                    if g == 0:
                        eng.wait_ge(dve_v, b.count(1, 1))
                        if b.past(1):
                            eng.wait_ge(act_o, b.back(1).count(2, 2))
                    elif g == 2:
                        eng.wait_ge(act_o, b.count(2, 1))
                    for t in range(2):
                        for i in range(G):
                            last = eng.matmul(bank_o[32 * i:32 * i + 32, g % 2, :], v[b.par][:, t, G * g + i, :],
                                              probs[g % 2][:, t, i, :], start=t == 0, stop=t == 1)
                    last.then_inc(pe_pv, 1)

                def scores(a, b):
                    for u in range(UNITS):
                        if a:
                            rows_bank(a, 2 * u)
                            rows_bank(a, 2 * u + 1)
                        if b:
                            cols_unit(b, u)
                            if u in (2, 4, 6):
                                pv(b, u // 2 - 1)
                    if b:
                        pv(b, GROUPS - 1)

                def project_v(b):
                    fetch.ready(eng, b)
                    if b.past(1):
                        eng.wait_ge(dve_v, b.back(1).count(1, 1))
                    if b.past(3):
                        eng.wait_ge(norm.act_turned, b.back(3).count(1, 1))
                    for t in range(2):
                        for k in range(DC):
                            last = eng.matmul(bank_a[:, t * D:(t + 1) * D], fetch.tile[b.par][:, k, t * P:(t + 1) * P],
                                              c.w_v[:, k, :], start=k == 0, stop=k == DC - 1)
                    last.then_inc(pe_v, 1)

                def turn_max(b):
                    eng.wait_ge(dve_max, b.count(MAX_PER, MAX_PER))
                    if b.past(1):
                        eng.wait_ge(act_max, b.back(1).count(1, 1))
                    for t in range(2):
                        last = eng.transpose(turned_max_ps[0:2 * H, t * P:(t + 1) * P],
                                             max_parts[:, t, :, :].rearrange("p c h -> p (c h)"), c.ident_b[:, :])
                    last.then_inc(pe_max, 1)

                def out(b):
                    eng.wait_ge(dve_div, b.count(DIV, DIV))
                    if b.past(1):
                        eng.wait_ge(norm.dve_norm, b.back(1).count(norm.PER, norm.SUMMED))
                    for t in range(2):
                        for g in range(GROUPS):
                            last = eng.matmul(bank_y[:, t, :], o_t[:, g, t * P:(t + 1) * P], c.w_o[:, g, :],
                                              start=g == 0, stop=g == GROUPS - 1)
                    last.then_inc(pe_y, 1)

                def turn(a, b):
                    if b:
                        if a:
                            eng.wait_ge(dve_v, a.count(1, 1))
                        turn_rows(b)
                turn_rows = norm.pe(eng)
                laps(eng, [(scores, (0, 1)), (turn_max, (0,)), (project_v, (0,)), (out, (1,)), (turn, (0, 2))], 4)

            @block.scalar
            def _(eng):
                def exps_and_o(b):
                    for u in range(UNITS):
                        g, t = divmod(u, 2)
                        eng.wait_ge(pe_col, b.count(UNITS, u + 1))
                        if g < 2:
                            if b.past(1):
                                eng.wait_ge(pe_pv, b.back(1).count(GROUPS, g + 3))
                        else:
                            eng.wait_ge(pe_pv, b.count(GROUPS, g - 1))
                        eng.activation(probs[g % 2][:, t, :, :].rearrange("p g t -> p (g t)"),
                                       bank_col[:, :, :].rearrange("p g t -> p (g t)"), ACT.Exp,
                                       scale=HD ** -0.5).then_inc(act_exp, 1)
                        if u == 4:
                            evacuate_o(b, 0)
                    evacuate_o(b, 1)

                def evacuate_o(b, half):
                    eng.wait_ge(pe_pv, b.count(GROUPS, 2 * half + 2))
                    if b.past(1):
                        eng.wait_ge(dve_div, b.back(1).count(DIV, 4 * half + 1))
                    eng.activation(o_raw[half][:, :, :], bank_o[:, :, :], ACT.Copy).then_inc(act_o, 1)

                def keep_max(b):
                    eng.wait_ge(pe_max, b.count(1, 1))
                    if b.past(1):
                        eng.wait_ge(max_in[b.back(1).par], b.back(1).landed(2))
                    eng.activation(turned_max[:, :], turned_max_ps[0:2 * H, 0:S], ACT.Copy).then_inc(act_max, 1)

                laps(eng, [(exps_and_o, (1,)), (keep_max, (0,)), (norm.act(eng), (2,))], 4)

            @block.vector
            def _(eng):
                chain = Count(DIV)

                def max_bank(b, r):
                    g, t, pair = r // 4, r // 2 % 2, r % 2
                    eng.wait_ge(pe_row, b.count(ROWS, r + 1))
                    if r == 0:
                        if b.past(1):
                            eng.wait_ge(dve_max, b.back(1).count(MAX_PER, MAX_PER))
                    eng.tensor_reduce(neg_max[:, t, G * g + 2 * pair:G * g + 2 * pair + 2],
                                      bank_row[:, 2 * pair:2 * pair + 2, :], AX.X, ALU.max,
                                      negate=True).then_inc(dve_max, 1)

                def max_in_parts(b):
                    eng.wait_ge(dve_max, b.count(MAX_PER, ROWS))
                    if b.past(1):
                        eng.wait_ge(pe_max, b.back(1).count(1, 1))
                    eng.tensor_copy(max_parts[:, :, 0, :], neg_max[:, :, :]).then_inc(dve_max, 1)
                    eng.wait_ge(dve_max, b.count(MAX_PER, ROWS + 1))
                    eng.tensor_tensor(max_parts[:, :, 1, :], neg_max[:, :, :], max_parts[:, :, 0, :],
                                      ALU.subtract).then_inc(dve_max, 1)

                def divide(b, half):
                    if half == 0:
                        chain.begin(b)
                    eng.wait_ge(act_o, b.count(2, half + 1))
                    if half:
                        eng.wait_ge(dve_div, chain.so_far())
                    elif b.past(1):
                        eng.wait_ge(dve_div, b.back(1).count(DIV, DIV))
                    apart(c, eng)
                    eng.transpose(squares[:, :], o_raw[half][:, :, :].rearrange("p g t -> p (g t)")
                                  ).then_inc(dve_div, chain.one())
                    eng.wait_ge(dve_div, chain.so_far())
                    rows = squares[:, :].rearrange("p (q d) -> p q d", d=2 * HD)
                    apart(c, eng)
                    eng.reciprocal(recip[:, :], rows[:, :, HD]).then_inc(dve_div, chain.one())
                    eng.wait_ge(dve_div, chain.so_far())
                    eng.tensor_tensor(divided[:, :].rearrange("p (q d) -> p q d", d=2 * HD), rows,
                                      recip[:, :].unsqueeze(2).broadcast_to([P, 2 * S // (2 * HD), 2 * HD]),
                                      ALU.mult).then_inc(dve_div, chain.one())
                    eng.wait_ge(dve_div, chain.so_far())
                    if half == 0:
                        if b.past(1):
                            eng.wait_ge(pe_y, b.back(1).count(1, 1))
                    apart(c, eng)
                    eng.transpose(o_t[:, 2 * half:2 * half + 2, :].rearrange("p g t -> p (g t)"), divided[:, :]
                                  ).then_inc(dve_div, chain.one())
                    if half == 1:
                        chain.end()

                sum_up, normalise = norm.dve(eng)

                def main(a, b, z):
                    for u in range(UNITS):
                        if a:
                            max_bank(a, 2 * u)
                            max_bank(a, 2 * u + 1)
                        if z and u == 1:
                            sum_up(z)
                        if z and u == 4:
                            normalise(z)
                        if b and u == 6:
                            divide(b, 0)
                    if a:
                        max_in_parts(a)
                    if b:
                        divide(b, 1)

                def add_bias_v(b):
                    eng.wait_ge(pe_v, b.count(1, 1))
                    if b.past(2):
                        eng.wait_ge(pe_pv, b.back(2).count(GROUPS, GROUPS))
                    eng.tensor_tensor(v[b.par][:, :, :, 0:HD].rearrange("p t h d -> p (t h) d"),
                                      bank_a[:, :].rearrange("p (q d) -> p q d", d=HD),
                                      c.bv_twice[:, :].rearrange("p (q d) -> p q d", d=HD),
                                      ALU.add).then_inc(dve_v, 1)

                laps(eng, [(main, (0, 1, 2)), (add_bias_v, (0,))], 4)

            @block.gpsimd
            def _(eng):
                laps(eng, [(fetch.pool(eng), (0,)), (norm.pool(eng), (2,))], 4)

            @block.sync
            def _(eng):
                eng.wait_ge(c.in_x, 16 * 4)

                def load_pack(b):
                    if not b.looped and b.low < len(c.later_packs):
                        for tile, pack in c.later_packs[b.low]:
                            eng.dma_start(tile, pack).then_inc(c.in_packs, 16)

                def load(b, half):
                    if half or b.past(1):
                        if b.past(2):
                            eng.wait_ge(pe_col, b.back(2).count(UNITS, (half + 1) * UNITS // 2))
                        load_parts(c, eng, b, half)

                def load_max(b):
                    eng.wait_ge(act_max, b.count(1, 1))
                    for part in range(2):
                        eng.dma_start(qs[b.par][MAX_ROW + part:MAX_ROW + part + 1, :, :],
                                      turned_max[H * part:H * part + H, :]).then_inc(max_in[b.par], 16)

                laps(eng, [(lambda b: load(b, 0), (0,)), (load_max, (1,)), (lambda b: load(b, 1), (0,)),
                           (load_pack, (0,))], 4)
                eng.wait_ge(c.in_packs, 16 * sum(map(len, c.later_packs)))




def context_attention(c):
    nc = c.nc
    KEYS = S + CTX
    with ExitStack() as stack:
        c.stack = stack
        bank_q, bank_k = c.psum("ca_q", (P, DC, S)), c.psum("ca_k", (P, DC, S))
        bank_vo = c.psum("ca_vo", (P, 2, D))
        bank_s = [c.psum(f"ca_s{t}") for t in range(2)]
        bank_t = [c.psum(f"ca_t{t}") for t in range(2)]
        bank_y = c.psum("ca_y", (P, 2, D))
        q = [c.sb(f"ca_qT{p}", [P, DC, S]) for p in range(2)]
        k = [c.sb(f"ca_kT{p}", [P, DC, KEYS]) for p in range(2)]
        v = [c.sb(f"ca_v{p}", [P, 2, D]) for p in range(2)]
        v_ctx = [c.sb(f"ca_vctx{p}", [CTX, D]) for p in range(2)]
        probs = [c.sb(f"ca_probs{p}", [P, 2, KEYS]) for p in range(2)]
        neg_max, bias = c.sb("ca_neg_max", [P, 2]), c.sb("ca_bias", [P, 2])
        total, recip = c.sb("ca_total", [P, 2]), c.sb("ca_recip", [P, 2])
        probs_t = c.sb("ca_probs_t", [P, 3, S])
        o_t = c.sb("ca_o_t", [P, DC, S])

        pe_proj, act_qk, dve_v = c.sem("ca_pe_proj"), c.sem("ca_act_qk"), c.sem("ca_dve_v")
        k_ctx_in, v_ctx_in = c.sems("ca_k_ctx_in"), c.sems("ca_v_ctx_in")
        pe_scores, act_exp = c.sem("ca_pe_scores"), c.sem("ca_act_exp")
        SOFT_PER = 6
        dve_soft = c.sem("ca_dve_soft")
        pe_turn_p, act_turn_p = c.sem("ca_pe_turn_p"), c.sem("ca_act_turn_p")
        pe_pv, act_o, pe_y = c.sem("ca_pe_pv"), c.sem("ca_act_o"), c.sem("ca_pe_y")
        norm = Norm(c, "n2", bank_y[:, :, :], lambda eng, b: eng.wait_ge(pe_y, b.count(1, 1)),
                    bank_q[:, :, :].rearrange("p j t -> p (j t)"))
        fetch = Fetch(c, "ca", lambda eng, b: eng.wait_ge(pe_proj, b.count(3, 3)))

        with nc.Block() as block:
            @block.tensor
            def _(eng):
                def project(b):
                    x = fetch.tile[b.par]
                    fetch.ready(eng, b)
                    for w, bank, weights in ((0, bank_q, c.x0_q), (1, bank_k, c.x0_k)):
                        if w == 0:
                            if b.past(3):
                                eng.wait_ge(norm.act_turned, b.back(3).count(1, 1))
                        if b.past(1):
                            eng.wait_ge(act_qk, b.back(1).count(2, w + 1))
                        for j in range(DC):
                            for i in range(DC):
                                last = eng.matmul(bank[:, j, :], weights[:, i, j * P:(j + 1) * P], x[:, i, :],
                                                  start=i == 0, stop=i == DC - 1)
                        last.then_inc(pe_proj, 1)
                    if b.past(2):
                        eng.wait_ge(act_o, b.back(2).count(1, 1))
                    if b.past(1):
                        eng.wait_ge(dve_v, b.back(1).count(1, 1))
                    for t in range(2):
                        for i in range(DC):
                            last = eng.matmul(bank_vo[:, t, :], x[:, i, t * P:(t + 1) * P], c.x0_v[:, i, :],
                                              start=i == 0, stop=i == DC - 1)
                    last.then_inc(pe_proj, 1)

                def turn_probs(b):
                    for t in range(2):
                        eng.wait_ge(dve_soft, b.count(SOFT_PER, 5 + t))
                        if b.past(1):
                            eng.wait_ge(act_turn_p, b.back(1).count(2, t + 1))
                        for i, n in enumerate((P, P, CTX)):
                            last = eng.transpose(bank_t[t][0:n, i * P:(i + 1) * P],
                                                 probs[b.par][:, t, i * P:i * P + n], c.ident[:, :])
                        last.then_inc(pe_turn_p, 1)

                def score(b):
                    eng.wait_ge(act_qk, b.count(2, 2))
                    eng.wait_ge(k_ctx_in[b.par], b.landed(1))
                    for t in range(2):
                        if b.past(1):
                            eng.wait_ge(act_exp, b.back(1).count(2, t + 1))
                        for i in range(DC):
                            last = eng.matmul(bank_s[t][:, 0:KEYS], q[b.par][:, i, t * P:(t + 1) * P],
                                              k[b.par][:, i, :], start=i == 0, stop=i == DC - 1)
                        last.then_inc(pe_scores, 1)

                def pv(a, b):
                    if not b:
                        return
                    eng.wait_ge(dve_v, b.count(1, 1))
                    if a:
                        eng.wait_ge(dve_v, a.count(1, 1))
                    eng.wait_ge(v_ctx_in[b.par], b.landed(1))
                    eng.wait_ge(act_turn_p, b.count(2, 2))
                    for j in range(DC):
                        cols = slice(j * P, (j + 1) * P)
                        for i in range(2):
                            eng.matmul(bank_vo[:, j, :], v[b.par][:, i, cols], probs_t[:, i, :], start=i == 0, stop=False)
                        last = eng.matmul(bank_vo[:, j, :], v_ctx[b.par][:, cols], probs_t[0:CTX, 2, :],
                                          start=False, stop=True)
                    last.then_inc(pe_pv, 1)

                def turn(a, b):
                    if b:
                        if a:
                            eng.wait_ge(act_qk, a.count(2, 1))
                        turn_rows(b)
                turn_rows = norm.pe(eng)

                def out(b):
                    eng.wait_ge(act_o, b.count(1, 1))
                    if b.past(1):
                        eng.wait_ge(norm.dve_norm, b.back(1).count(norm.PER, norm.SUMMED))
                    for t in range(2):
                        for i in range(DC):
                            last = eng.matmul(bank_y[:, t, :], o_t[:, i, t * P:(t + 1) * P], c.x0_o[:, i, :],
                                              start=i == 0, stop=i == DC - 1)
                    last.then_inc(pe_y, 1)

                laps(eng, [(project, (0,)), (turn_probs, (1,)), (score, (0,)), (pv, (0, 1)), (turn, (0, 2)),
                           (out, (1,))], 4)

            @block.scalar
            def _(eng):
                def keep_qk(b):
                    for w, bank, dst in ((0, bank_q, q), (1, bank_k, k)):
                        eng.wait_ge(pe_proj, b.count(3, w + 1))
                        if b.past(2):
                            eng.wait_ge(pe_scores, b.back(2).count(2, 2))
                        eng.activation(dst[b.par][:, :, 0:S], bank[:, :, :], ACT.Copy).then_inc(act_qk, 1)

                def keep_probs(b):
                    for t in range(2):
                        eng.wait_ge(pe_turn_p, b.count(2, t + 1))
                        if b.past(1):
                            eng.wait_ge(pe_pv, b.back(1).count(1, 1))
                        cols = slice(t * P, (t + 1) * P)
                        eng.activation(probs_t[:, 0:2, cols], bank_t[t][:, 0:2 * P].rearrange("p (i t) -> p i t", i=2),
                                       ACT.Copy)
                        eng.activation(probs_t[0:CTX, 2, cols], bank_t[t][0:CTX, 2 * P:3 * P],
                                       ACT.Copy).then_inc(act_turn_p, 1)

                def exps(b):
                    for t in range(2):
                        eng.wait_ge(dve_soft, b.count(SOFT_PER, 3))
                        if b.past(2):
                            eng.wait_ge(pe_turn_p, b.back(2).count(2, t + 1))
                        if b.past(1):
                            eng.wait_ge(dve_soft, b.back(1).count(SOFT_PER, 4))
                        eng.activation(probs[b.par][:, t, :], bank_s[t][:, 0:KEYS], ACT.Exp, bias=bias[:, t:t + 1],
                                       scale=D ** -0.5, accum_out=total[:, t:t + 1]).then_inc(act_exp, 1)

                def keep_o(b):
                    eng.wait_ge(pe_pv, b.count(1, 1))
                    if b.past(1):
                        eng.wait_ge(pe_y, b.back(1).count(1, 1))
                    eng.activation(o_t[:, :, :], bank_vo[:, :, :], ACT.Copy).then_inc(act_o, 1)

                laps(eng, [(keep_qk, (0,)), (keep_probs, (1,)), (exps, (0,)), (keep_o, (1,)),
                           (norm.act(eng), (2,))], 4)

            @block.vector
            def _(eng):
                chain = Count(SOFT_PER)

                def keep_v(b):
                    eng.wait_ge(pe_proj, b.count(3, 3))
                    if b.past(2):
                        eng.wait_ge(pe_pv, b.back(2).count(1, 1))
                    eng.tensor_copy(v[b.par][:, :, :], bank_vo[:, :, :]).then_inc(dve_v, 1)

                def soften(b):
                    chain.begin(b)
                    if b.past(1):
                        eng.wait_ge(dve_soft, b.back(1).count(SOFT_PER, SOFT_PER))
                    for t in range(2):
                        eng.wait_ge(pe_scores, b.count(2, t + 1))
                        eng.tensor_reduce(neg_max[:, t:t + 1], bank_s[t][:, 0:KEYS], AX.X, ALU.max,
                                          negate=True).then_inc(dve_soft, chain.one())
                    eng.wait_ge(dve_soft, chain.so_far())
                    if b.past(1):
                        eng.wait_ge(act_exp, b.back(1).count(2, 2))
                    eng.tensor_scalar(bias[:, :], neg_max[:, :], D ** -0.5, None, ALU.mult).then_inc(dve_soft, chain.one())
                    eng.wait_ge(act_exp, b.count(2, 2))
                    eng.reciprocal(recip[:, :], total[:, :]).then_inc(dve_soft, chain.one())
                    eng.wait_ge(dve_soft, chain.so_far())
                    for t in range(2):
                        eng.tensor_scalar(probs[b.par][:, t, :], probs[b.par][:, t, :], recip[:, t:t + 1],
                                          None, ALU.mult).then_inc(dve_soft, chain.one())
                    chain.end()

                laps(eng, [(keep_v, (0,)), (soften, (0,)), *((step, (1,)) for step in norm.dve(eng))], 4)

            @block.gpsimd
            def _(eng):
                laps(eng, [(fetch.pool(eng), (0,)), (norm.pool(eng), (2,))], 4)

            @block.sync
            def _(eng):
                def load(b):
                    if b.past(2):
                        eng.wait_ge(pe_scores, b.back(2).count(2, 2))
                    eng.dma_start(k[b.par][:, :, S:KEYS], c.d_ctx_t[bass.ds(b.n, 1)].rearrange("o p j k -> p (o j) k")
                                  ).then_inc(k_ctx_in[b.par], 16)
                    if b.past(2):
                        eng.wait_ge(pe_pv, b.back(2).count(1, 1))
                    eng.dma_start(v_ctx[b.par][:, :], c.d_ctx[bass.ds(b.n, 1)].rearrange("o k d -> k (o d)")
                                  ).then_inc(v_ctx_in[b.par], 16)
                laps(eng, [(load, (0,))], 2)




TOP = 8
EXPERTS = 512
NKEYS = 64
RETR = 128
INTER = 1024
EB = EXPERTS // P
FB = INTER // P
LOWEST = -3.0e38


def route_scores(c):
    nc = c.nc
    with ExitStack() as stack:
        c.stack = stack
        bank_q = [c.psum(f"rt_q{p}", (P, S)) for p in range(2)]
        bank_r = [c.psum(f"rt_r{p}", (P, 2, P)) for p in range(2)]
        q = [c.sb(f"rt_q_sb{p}", [P, S]) for p in range(2)]
        with nc.Block() as block:
            sems = [[c.sem(f"rt_{n}{t}") for n in ("pe_q", "act_q", "pe_r", "dve_r")] for t in range(2)]

            @block.tensor
            def _(eng):
                for table in range(2):
                    pe_q, act_q, pe_r, dve_r = sems[table]

                    def queries(b):
                        if b.past(2):
                            eng.wait_ge(act_q, b.back(2).count(1, 1))
                        for i in range(DC):
                            last = eng.matmul(bank_q[b.par][:, :], c.w_query[:, i, :],
                                              c.XT[:, bass.ds(i * B * S + S * b.n + table * (B // 2) * S, S)],
                                              start=i == 0, stop=i == DC - 1)
                        last.then_inc(pe_q, 1)

                    def scores(b):
                        eng.wait_ge(act_q, b.count(1, 1))
                        if b.past(2):
                            eng.wait_ge(dve_r, b.back(2).count(1, 1))
                        for t in range(2):
                            last = eng.matmul(bank_r[b.par][:, t, :], q[b.par][:, t * P:(t + 1) * P],
                                              c.keys[:, table, :], start=True, stop=True)
                        last.then_inc(pe_r, 1)
                    if table:
                        eng.wait_ge(sems[0][1], B // 2)
                        eng.wait_ge(sems[0][3], B // 2)
                    laps(eng, [(queries, (0,)), (scores, (1,))], 4, B // 2)

            @block.scalar
            def _(eng):
                for table in range(2):
                    pe_q, act_q, pe_r, dve_r = sems[table]

                    def keep(b):
                        eng.wait_ge(pe_q, b.count(1, 1))
                        if b.past(2):
                            eng.wait_ge(pe_r, b.back(2).count(1, 1))
                        if table:
                            eng.wait_ge(sems[0][2], B // 2)
                        eng.activation(q[b.par][:, :], bank_q[b.par][:, :], ACT.Copy).then_inc(act_q, 1)
                    laps(eng, [(keep, (0,))], 4, B // 2)

            @block.vector
            def _(eng):
                for table in range(2):
                    pe_q, act_q, pe_r, dve_r = sems[table]

                    def keep(b):
                        eng.wait_ge(pe_r, b.count(1, 1))
                        eng.tensor_copy(c.R[:, bass.ds(2 * P * b.n + table * B * P, 2 * P)],
                                        bank_r[b.par][:, :, :].rearrange("p t k -> p (t k)")).then_inc(dve_r, 1)
                    laps(eng, [(keep, (0,))], 4, B // 2)


def feed_forward(c):
    nc = c.nc
    with ExitStack() as stack:
        c.stack = stack
        bank_u = [c.psum(f"ff_u{p}", (P, 2, S)) for p in range(2)]
        bank_w = [c.psum(f"ff_w{p}", (P, 2, 2, P)) for p in range(2)]
        bank_y, bank_t = c.psum("ff_y", (P, 2, D)), c.psum("ff_t")
        rt = [c.sb(f"ff_rt{p}", [P, 2, 2, NKEYS]) for p in range(2)]
        best, best_i = c.sb("ff_best", [P, 2, 2, TOP]), c.sb("ff_best_i", [P, 2, 2, TOP], U32)
        best_f = c.sb("ff_best_f", [P, 2, 2, TOP])
        neg_best = c.sb("ff_neg_best", [P, 2, 2])
        sums, left = c.sb("ff_sums", [P, 2, TOP, TOP]), c.sb("ff_left", [P, 2, TOP, TOP])
        top, neg_top = c.sb("ff_top", [P, 2, TOP]), c.sb("ff_neg_top", [P, 2])
        taken, count = c.sb("ff_taken", [P, 2, TOP, TOP]), c.sb("ff_count", [P, 2, TOP])
        stairs, stair = c.sb("ff_stairs", [P, 2, TOP, TOP]), c.sb("ff_stair", [P, 2, TOP])
        places, rank = c.sb("ff_places", [P, 2, NKEYS, TOP]), c.sb("ff_rank", [P, 2, NKEYS])
        e_first, e_second = c.sb("ff_e_first", [P, 2, TOP]), c.sb("ff_e_second", [P, 2, NKEYS])
        e_top, total, r_total = c.sb("ff_e_top", [P, TOP]), c.sb("ff_total", [P, 2]), c.sb("ff_r_total", [P, 2])
        scaled = c.sb("ff_scaled", [P, 2, TOP])
        chosen = c.sb("ff_chosen", [P, 2, TOP, NKEYS])
        weight = [c.sb(f"ff_weight{p}", [P, 2, EXPERTS]) for p in range(2)]
        inside, outside = c.sb("ff_inside", [P, 2]), c.sb("ff_outside", [P, 2])
        act = [c.sb(f"ff_act{p}", [P, 2, S]) for p in range(2)]
        hidden = c.sb("ff_hidden", [P, FB + EB, S])

        UNITS_F = EB // 2 + FB
        pool_rt = c.sem("ff_pool_rt")
        BEST, TOP_SUMS, CHOSEN, SCALED, WEIGHT = 10, 16, 26, 28, 30
        dve_route, act_route = c.sem("ff_dve_route"), c.sem("ff_act_route")
        pool_weight = c.sem("ff_pool_weight")
        pe_w, pe_u, act_u, dve_u = c.sem("ff_pe_w"), c.sem("ff_pe_u"), c.sem("ff_act_u"), c.sem("ff_dve_u")
        pe_y = c.sem("ff_pe_y")
        norm = Norm(c, "n3", bank_y[:, :, :], lambda eng, b: eng.wait_ge(pe_y, b.count(1, 1)), bank_t)

        def ahead(b, u):
            return b.low == 0 and not b.looped and u < FB

        with nc.Block() as block:
            @block.tensor
            def _(eng):
                def turn_weights(b):
                    eng.wait_ge(dve_route, b.count(WEIGHT, WEIGHT))
                    if b.past(1):
                        eng.wait_ge(dve_u, b.back(1).count(UNITS_F, UNITS_F))
                    for e in range(EB):
                        for j in range(2):
                            last = eng.transpose(bank_w[e // 2][:, e % 2, j, :],
                                                 weight[b.par][:, j, e * P:(e + 1) * P], c.ident[:, :])
                    last.then_inc(pe_w, 1)

                def units(b):
                    for u in range(UNITS_F):
                        if u < 2:
                            if b.past(1):
                                eng.wait_ge(dve_u, b.back(1).count(UNITS_F, UNITS_F - 1 + u))
                        else:
                            eng.wait_ge(dve_u, b.count(UNITS_F, u - 1))
                        for w in range(2):
                            if u < FB:
                                weights, col = (c.f_gate, c.f_up)[w], u * P
                            else:
                                weights, col = c.w_down_embed, (2 * (u - FB) + w) * P
                            for i in range(DC):
                                last = eng.matmul(bank_u[u % 2][:, w, :], weights[:, i, col:col + P],
                                                  c.XT[:, bass.ds(i * B * S + S * b.n, S)],
                                                  start=i == 0, stop=i == DC - 1)
                        last.then_inc(pe_u, 1)
                        if u == FB - 1 and ahead(b, u):
                            down_mlp(b)
                        if u == (FB - 1 if ahead(b, u) else FB - 2):
                            turn_weights(b)

                def down_mlp(b):
                    for k in range(FB):
                        eng.wait_ge(dve_u, b.count(UNITS_F, k + 1))
                        eng.matmul(bank_y[:, 0, :], hidden[:, k, 0:P], c.f_down[:, k, :], start=k == 0, stop=False)

                def down(b):
                    if b.past(1):
                        eng.wait_ge(norm.dve_norm, b.back(1).count(norm.PER, norm.SUMMED))
                    for t in range(2):
                        for k in range(FB if t == 0 and ahead(b, 0) else 0, FB + EB):
                            if t == 0:
                                eng.wait_ge(dve_u, b.count(UNITS_F, k + 1 if k < FB else FB + (k - FB) // 2 + 1))
                            weights = c.f_down[:, k, :] if k < FB else c.w_up_embed[:, k - FB, :]
                            last = eng.matmul(bank_y[:, t, :], hidden[:, k, t * P:(t + 1) * P], weights,
                                              start=k == 0, stop=k == FB + EB - 1)
                    last.then_inc(pe_y, 1)

                laps(eng, [(units, (1,)), (norm.pe(eng), (2,)), (down, (1,))], 4)

            @block.scalar
            def _(eng):
                def exps(b):
                    eng.wait_ge(dve_route, b.count(WEIGHT, BEST))
                    for j in range(2):
                        if b.past(1):
                            eng.wait_ge(dve_route, b.back(1).count(WEIGHT, SCALED))
                        eng.activation(e_first[:, j, :], rt[b.par][:, 0, j, 0:TOP], ACT.Exp,
                                       bias=neg_best[:, 0, j:j + 1]).then_inc(act_route, 1)
                        if b.past(1):
                            eng.wait_ge(pool_weight, b.back(1).count(2, 1))
                        eng.activation(e_second[:, j, :], rt[b.par][:, 1, j, :], ACT.Exp,
                                       bias=neg_best[:, 1, j:j + 1]).then_inc(act_route, 1)
                    eng.wait_ge(dve_route, b.count(WEIGHT, TOP_SUMS))
                    for j in range(2):
                        eng.wait_ge(act_route, b.count(6, 4 + j))
                        eng.activation(e_top[:, :], top[:, j, :], ACT.Exp, bias=neg_top[:, j:j + 1],
                                       accum_out=total[:, j:j + 1]).then_inc(act_route, 1)

                def silu(b, u):
                    eng.wait_ge(pe_u, b.count(UNITS_F, u + 1))
                    if u < 2:
                        if b.past(1):
                            eng.wait_ge(dve_u, b.back(1).count(UNITS_F, UNITS_F - 1 + u))
                    else:
                        eng.wait_ge(dve_u, b.count(UNITS_F, u - 1))
                    n = 1 if u < FB else 2
                    eng.activation(act[u % 2][:, 0:n, :], bank_u[u % 2][:, 0:n, :], ACT.Silu).then_inc(act_u, 1)

                def main(a, b):
                    for u in range(UNITS_F):
                        if b and not ahead(b, u):
                            silu(b, u)
                        if a and ahead(a, u):
                            silu(a, u)
                        if a and u == (1 if ahead(a, 0) else 5):
                            exps(a)
                laps(eng, [(main, (0, 1)), (norm.act(eng), (2,))], 4)

            @block.vector
            def _(eng):
                chain = Count(WEIGHT)
                half_keys = [P, 2, TOP, TOP]

                def best_scores(b):
                    chain.begin(b)
                    eng.wait_ge(pool_rt, b.count(2, 2))
                    if b.past(1):
                        eng.wait_ge(dve_route, b.back(1).count(WEIGHT, WEIGHT))
                    apart(c, eng)
                    for table in range(2):
                        for j in range(2):
                            eng.max(best[:, table, j, :], rt[b.par][:, table, j, :]).then_inc(dve_route, chain.one())

                def best_keys(b):
                    eng.wait_ge(dve_route, chain.so_far())
                    apart(c, eng)
                    for table in range(2):
                        for j in range(2):
                            eng.max_index(best_i[:, table, j, :], best[:, table, j, :], rt[b.par][:, table, j, :]).then_inc(dve_route, chain.one())
                    eng.wait_ge(dve_route, chain.so_far())
                    eng.tensor_copy(best_f[:, :, :, :], best_i[:, :, :, :]).then_inc(dve_route, chain.one())
                    if b.past(1):
                        eng.wait_ge(act_route, b.back(1).count(6, 4))
                    eng.tensor_scalar(neg_best[:, :, :], best[:, :, :, 0], -1.0, None, ALU.mult).then_inc(dve_route, chain.one())
                    assert chain.k == BEST

                def best_sums(b):
                    eng.tensor_tensor(sums[:, :, :, :], best[:, 0, :, :].unsqueeze(3).broadcast_to(half_keys),
                                      best[:, 1, :, :].unsqueeze(2).broadcast_to(half_keys), ALU.add).then_inc(dve_route, chain.one())
                    eng.wait_ge(dve_route, chain.so_far())
                    if b.past(1):
                        eng.wait_ge(act_route, b.back(1).count(6, 6))
                    apart(c, eng)
                    for j in range(2):
                        eng.max(top[:, j, :], sums[:, j, :, :].rearrange("p a b -> p (a b)")).then_inc(dve_route, chain.one())
                    eng.wait_ge(dve_route, chain.so_far())
                    apart(c, eng)
                    for j in range(2):
                        eng.match_replace(left[:, j, :, :].rearrange("p a b -> p (a b)"), top[:, j, :],
                                          sums[:, j, :, :].rearrange("p a b -> p (a b)"), LOWEST).then_inc(dve_route, chain.one())
                    eng.tensor_scalar(neg_top[:, :], top[:, :, 0], -1.0, None, ALU.mult).then_inc(dve_route, chain.one())
                    assert chain.k == TOP_SUMS

                def staircase(b):
                    eng.wait_ge(dve_route, chain.so_far())
                    eng.tensor_tensor(taken[:, :, :, :], left[:, :, :, :], sums[:, :, :, :], ALU.not_equal).then_inc(dve_route, chain.one())
                    eng.wait_ge(dve_route, chain.so_far())
                    eng.tensor_reduce(count[:, :, :], taken[:, :, :, :], AX.X, ALU.add).then_inc(dve_route, chain.one())
                    eng.tensor_tensor(stairs[:, :, :, :],
                                      c.iota[:, 0:TOP].unsqueeze(1).unsqueeze(3).broadcast_to(half_keys),
                                      best_f[:, 0, :, :].unsqueeze(2).broadcast_to(half_keys), ALU.is_equal).then_inc(dve_route, chain.one())
                    eng.wait_ge(dve_route, chain.so_far())
                    eng.tensor_tensor(stairs[:, :, :, :], stairs[:, :, :, :],
                                      count[:, :, :].unsqueeze(2).broadcast_to(half_keys), ALU.mult).then_inc(dve_route, chain.one())
                    eng.wait_ge(dve_route, chain.so_far())
                    eng.tensor_reduce(stair[:, :, :], stairs[:, :, :, :], AX.X, ALU.add).then_inc(dve_route, chain.one())
                    eng.wait_ge(dve_route, chain.so_far())
                    eng.tensor_scalar(stair[:, :, :], stair[:, :, :], -float(TOP), None, ALU.add).then_inc(dve_route, chain.one())

                key_ranks = [P, 2, NKEYS, TOP]

                def find_ranks(b):
                    eng.tensor_tensor(places[:, :, :, :],
                                      c.iota[:, 0:NKEYS].unsqueeze(1).unsqueeze(3).broadcast_to(key_ranks),
                                      best_f[:, 1, :, :].unsqueeze(2).broadcast_to(key_ranks), ALU.is_equal).then_inc(dve_route, chain.one())

                def scale_ranks(b):
                    eng.wait_ge(dve_route, chain.so_far())
                    eng.tensor_tensor(places[:, :, :, :], places[:, :, :, :],
                                      c.rank[:, 0:TOP].unsqueeze(1).unsqueeze(2).broadcast_to(key_ranks), ALU.mult).then_inc(dve_route, chain.one())

                def rank_keys(b):
                    eng.wait_ge(dve_route, chain.so_far())
                    eng.tensor_reduce(rank[:, :, :], places[:, :, :, :], AX.X, ALU.add).then_inc(dve_route, chain.one())

                def choose(b):
                    eng.wait_ge(dve_route, chain.so_far())
                    if b.past(1):
                        eng.wait_ge(pool_weight, b.back(1).count(2, 2))
                    shape = [P, 2, TOP, NKEYS]
                    eng.tensor_tensor(chosen[:, :, :, :], rank[:, :, :].unsqueeze(2).broadcast_to(shape),
                                      stair[:, :, :].unsqueeze(3).broadcast_to(shape), ALU.is_lt).then_inc(dve_route, chain.one())
                    assert chain.k == CHOSEN

                def scale_first(b):
                    eng.wait_ge(act_route, b.count(6, 6))
                    eng.reciprocal(r_total[:, :], total[:, :]).then_inc(dve_route, chain.one())
                    eng.wait_ge(dve_route, chain.so_far())
                    eng.tensor_tensor(scaled[:, :, :], e_first[:, :, :],
                                      r_total[:, :].unsqueeze(2).broadcast_to([P, 2, TOP]), ALU.mult).then_inc(dve_route, chain.one())
                    assert chain.k == SCALED

                def weigh_last(b):
                    eng.wait_ge(pool_weight, b.count(2, 2))
                    eng.tensor_reduce(inside[:, :], weight[b.par][:, :, 0:EXPERTS - 1], AX.X, ALU.add).then_inc(dve_route, chain.one())
                    eng.wait_ge(dve_route, chain.so_far())
                    eng.tensor_scalar(weight[b.par][:, :, EXPERTS - 1], inside[:, :], -1.0, 1.0,
                                      ALU.mult, ALU.add).then_inc(dve_route, chain.one())
                    chain.end()

                routing = (best_scores, best_keys, best_sums, staircase, find_ranks, scale_ranks, rank_keys, choose,
                           scale_first)

                def hide(b, u):
                    eng.wait_ge(act_u, b.count(UNITS_F, u + 1))
                    if b.past(1):
                        eng.wait_ge(pe_y, b.back(1).count(1, 1))
                    if u < FB:
                        eng.tensor_tensor(hidden[:, u, :], act[u % 2][:, 0, :], bank_u[u % 2][:, 1, :],
                                          ALU.mult).then_inc(dve_u, 1)
                    else:
                        eng.wait_ge(pe_w, b.count(1, 1))
                        e = u - FB
                        dst, src = (x.rearrange("p w (i j) -> p w j i", j=2)
                                    for x in (hidden[:, FB + 2 * e:FB + 2 * e + 2, :], act[u % 2][:, :, :]))
                        eng.tensor_tensor(dst, src, bank_w[e][:, :, :, :], ALU.mult).then_inc(dve_u, 1)

                sum_up, normalise = norm.dve(eng)

                def main(a, b, z):
                    for u in range(UNITS_F):
                        if b and not ahead(b, 0):
                            hide(b, u)
                        if b and ahead(b, 0) and u in (4, 5):
                            hide(b, FB + u - 4)
                        if z and u == 1:
                            sum_up(z)
                        if z and u == 3:
                            normalise(z)
                        if a:
                            for step in routing[2 * u:2 * u + 2] if ahead(a, 0) else routing[u:u + 1]:
                                step(a)
                        if a and ahead(a, u):
                            hide(a, u)

                laps(eng, [(main, (0, 1, 2)), (weigh_last, (0,))], 4)

            @block.gpsimd
            def _(eng):
                def fetch_scores(b):
                    for table in range(2):
                        if b.past(2):
                            eng.wait_ge(dve_route, b.back(2).count(WEIGHT, BEST))
                        if b.past(2):
                            eng.wait_ge(act_route, b.back(2).count(6, 4))
                        apart(c, eng)
                        eng.tensor_copy(rt[b.par][:, table, :, :].rearrange("p j k -> p (j k)"),
                                        c.R[:, bass.ds(P * b.n + table * B * P, P)]).then_inc(pool_rt, 1)

                def weigh(b):
                    eng.wait_ge(dve_route, b.count(WEIGHT, CHOSEN))
                    eng.wait_ge(act_route, b.count(6, 4))
                    shape = [P, 2, TOP, NKEYS]
                    eng.tensor_tensor(chosen[:, :, :, :], chosen[:, :, :, :],
                                      e_second[:, :, :].unsqueeze(2).broadcast_to(shape), ALU.mult).then_inc(pool_weight, 1)
                    eng.wait_ge(pool_weight, b.count(2, 1))
                    eng.wait_ge(dve_route, b.count(WEIGHT, SCALED))
                    if b.past(2):
                        eng.wait_ge(pe_w, b.back(2).count(1, 1))
                    eng.tensor_tensor(weight[b.par][:, :, :].rearrange("p j (a b) -> p j a b", b=NKEYS), chosen[:, :, :, :],
                                      scaled[:, :, :].unsqueeze(3).broadcast_to(shape), ALU.mult).then_inc(pool_weight, 1)
                laps(eng, [(fetch_scores, (0,)), (norm.pool(eng), (2,)), (weigh, (0,))], 4)




ROUND = 1.5 * 2.0 ** 23
INT8 = 127.0
HB = H // 2
SCORES = HB * CTX


class Rounding:
    PER = 8

    def __init__(self, c, name):
        self.c = c
        self.dve_done = c.sem(name + "_dve_rounded")
        self.peak, self.step, self.inv = (c.sb(name + n, [P, 2]) for n in ("_peak", "_step", "_inv"))
        self.whole = c.sb(name + "_whole", [P, 2, D])


def round_rows(c, eng, *jobs):
    counts = [Count(Rounding.PER) for _ in jobs]
    for (r, b, src, dst), count in zip(jobs, counts):
        count.begin(b)
        if b.past(1):
            eng.wait_ge(r.dve_done, b.back(1).count(Rounding.PER, Rounding.PER))
        apart(c, eng)
        eng.tensor_reduce(r.peak[:, :], src, AX.X, ALU.max, apply_absolute_value=True).then_inc(r.dve_done, count.one())
    for (r, b, src, dst), count in zip(jobs, counts):
        eng.wait_ge(r.dve_done, count.so_far())
        eng.tensor_scalar(r.step[:, :], r.peak[:, :], 1 / INT8, 1e-8, ALU.mult, ALU.max).then_inc(r.dve_done, count.one())
    for (r, b, src, dst), count in zip(jobs, counts):
        eng.wait_ge(r.dve_done, count.so_far())
        eng.reciprocal(r.inv[:, :], r.step[:, :]).then_inc(r.dve_done, count.one())
    for (r, b, src, dst), count in zip(jobs, counts):
        eng.wait_ge(r.dve_done, count.so_far())
        for t in range(2):
            eng.tensor_scalar(r.whole[:, t, :], src[:, t, :], r.inv[:, t:t + 1], INT8, ALU.mult,
                              ALU.min).then_inc(r.dve_done, count.one())
    for (r, b, src, dst), count in zip(jobs, counts):
        eng.wait_ge(r.dve_done, count.so_far())
        eng.tensor_scalar(r.whole[:, :, :], r.whole[:, :, :], -INT8, ROUND, ALU.max, ALU.add).then_inc(r.dve_done, count.one())
    for (r, b, src, dst), count in zip(jobs, counts):
        eng.wait_ge(r.dve_done, count.so_far())
        for t in range(2):
            eng.tensor_scalar(dst[:, t, :], r.whole[:, t, :], ROUND, r.step[:, t:t + 1],
                              ALU.subtract, ALU.mult).then_inc(r.dve_done, count.one())
        count.end()


def turn_tiles(c, eng, bank, src):
    for t in range(2):
        for j in range(DC):
            last = eng.transpose(bank[:, j, t * P:(t + 1) * P], src[:, t, j * P:(j + 1) * P], c.ident[:, :])
    return last


def running_sum(c):
    nc = c.nc
    with ExitStack() as stack:
        c.stack = stack
        bank_kv = [c.psum(f"rs_kv{t}") for t in range(2)]
        bank_q, bank_c = c.psum("rs_q", (P, DC, S)), c.psum("rs_c", (P, DC, S))
        bank_y, bank_t = c.psum("rs_y", (P, 2, D)), c.psum("rs_t")
        side = [c.psum(f"rs_side{n}") for n in range(2)]
        k = c.sb("rs_k", [P, 2, D])
        kv = [c.sb(f"rs_kv_sb{p}", [P, 2, D]) for p in range(2)]
        q = [c.sb(f"rs_q_sb{p}", [P, DC, S]) for p in range(2)]
        o_t = [c.sb(f"rs_o_t{p}", [P, DC, S]) for p in range(2)]
        pe_kv, act_k, dve_kv = c.sem("rs_pe_kv"), c.sem("rs_act_k"), c.sem("rs_dve_kv")
        pe_q, act_q, pe_c = c.sem("rs_pe_q"), c.sem("rs_act_q"), c.sem("rs_pe_c")
        dve_o, pe_y = c.sem("rs_dve_o"), c.sem("rs_pe_y")
        norm = Norm(c, "n4", bank_y[:, :, :], lambda eng, b: eng.wait_ge(pe_y, b.count(1, 1)), bank_t)
        fetch = Fetch(c, "rs", lambda eng, b: eng.wait_ge(pe_q, b.count(1, 1)))

        rounded_w = [c.sb(f"rs_rounded_{n}", [P, DC, D]) for n in "qp"]
        w_round = Rounding(c, "rs_w")
        pe_side, act_side, dve_side = c.sem("rs_pe_side"), c.sem("rs_act_side"), c.sem("rs_dve_side")

        def weights_of(b, first):
            return None if b.looped or b.low not in (first, first + 1) else b.low - first

        with nc.Block() as block:
            @block.sync
            def _(eng):
                c.load_mixture(eng)

            @block.tensor
            def _(eng):
                for j in range(DC):
                    for i in range(DC):
                        last = eng.matmul(side[j][:, :], c.a_k[:, i, j * P:(j + 1) * P], c.ctx_all[:, i, :],
                                          start=i == 0, stop=i == DC - 1)
                    last.then_inc(pe_side, 1)
                for b in range(B):
                    if b < 2:
                        eng.wait_ge(act_side, b + 1)
                    else:
                        eng.wait_ge(dve_side, b - 1)
                    for i in range(DC):
                        last = eng.matmul(side[b % 2][:, 0:D], c.ctx_twice[:, i, b * P:(b + 1) * P],
                                          c.a_v[:, i, :], start=i == 0, stop=i == DC - 1)
                    last.then_inc(pe_side, 1)

                def turn_weights(b):
                    w = weights_of(b, 2)
                    if w is not None:
                        eng.wait_ge(w_round.dve_done, w_round.PER * (w + 1))
                        eng.wait_ge(dve_side, B)
                        turn_tiles(c, eng, side[w][:, :].rearrange("p (j t) -> p j t", j=DC), rounded_w[w]
                                   ).then_inc(pe_side, 1)

                def project(b):
                    x = fetch.tile[b.par]
                    fetch.ready(eng, b)
                    for t in range(2):
                        if b.past(1):
                            eng.wait_ge(dve_kv, b.back(1).count(2, t + 1))
                        for i in range(DC):
                            last = eng.matmul(bank_kv[t][:, :], x[:, i, t * P:(t + 1) * P], c.r_kv[:, i, :],
                                              start=i == 0, stop=i == DC - 1)
                        last.then_inc(pe_kv, 1)
                    if b.past(1):
                        eng.wait_ge(act_q, b.back(1).count(1, 1))
                    for j in range(DC):
                        for i in range(DC):
                            last = eng.matmul(bank_q[:, j, :], c.r_q[:, i, j * P:(j + 1) * P], x[:, i, :],
                                              start=i == 0, stop=i == DC - 1)
                    last.then_inc(pe_q, 1)

                def out(b):
                    eng.wait_ge(dve_o, b.count(1, 1))
                    if b.past(1):
                        eng.wait_ge(norm.dve_norm, b.back(1).count(norm.PER, norm.SUMMED))
                    for t in range(2):
                        for i in range(DC):
                            last = eng.matmul(bank_y[:, t, :], o_t[b.par][:, i, t * P:(t + 1) * P], c.r_o[:, i, :],
                                              start=i == 0, stop=i == DC - 1)
                    last.then_inc(pe_y, 1)

                def add_up(b):
                    eng.wait_ge(dve_kv, b.count(2, 2))
                    if b.past(1):
                        eng.wait_ge(dve_o, b.back(1).count(1, 1))
                    for j in range(DC):
                        cols = slice(j * P, (j + 1) * P)
                        eng.matmul(bank_c[:, j, :], kv[b.par][:, 0, cols], c.tri[:, :], start=True, stop=False)
                        last = eng.matmul(bank_c[:, j, P:], kv[b.par][:, 1, cols], c.tri[:, 0:P], start=False, stop=True)
                    last.then_inc(pe_c, 1)

                laps(eng, [(project, (0,)), (out, (1,)), (add_up, (0,)), (norm.pe(eng), (2,)), (turn_weights, (0,))], 4)

            @block.scalar
            def _(eng):
                for j in range(DC):
                    eng.wait_ge(pe_side, j + 1)
                    eng.activation(c.cross_k[:, j * B * CTX:(j + 1) * B * CTX], side[j][:, :], ACT.Identity,
                                   bias=c.a_bk[:, j:j + 1]).then_inc(act_side, 1)

                def keep_weights(b):
                    w = weights_of(b, 2)
                    if w is not None:
                        eng.wait_ge(pe_side, DC + B + w + 1)
                        eng.activation(c.cross_weight[w][:, :, :].rearrange("p i n -> p (i n)"), side[w][:, :],
                                       ACT.Copy).then_inc(act_side, 1)

                def keep(b):
                    for t in range(2):
                        eng.wait_ge(pe_kv, b.count(2, t + 1))
                        if b.past(1):
                            eng.wait_ge(dve_kv, b.back(1).count(2, t + 1))
                        eng.activation(k[:, t, :], bank_kv[t][:, 0:D], ACT.Copy).then_inc(act_k, 1)
                    eng.wait_ge(pe_q, b.count(1, 1))
                    if b.past(2):
                        eng.wait_ge(dve_o, b.back(2).count(1, 1))
                    eng.activation(q[b.par][:, :, :], bank_q[:, :, :], ACT.Copy).then_inc(act_q, 1)
                laps(eng, [(keep, (0,)), (norm.act(eng), (2,)), (keep_weights, (0,))], 4)

            @block.vector
            def _(eng):
                for b in range(B):
                    eng.wait_ge(pe_side, DC + b + 1)
                    eng.tensor_tensor(c.cross_v[:, b * D:(b + 1) * D], side[b % 2][:, 0:D], c.a_bv[:, :],
                                      ALU.add).then_inc(dve_side, 1)

                def round_weights(b):
                    w = weights_of(b, 1)
                    if w is not None:
                        round_rows(c, eng, (w_round, Lap(w), (c.a_q, c.a_p)[w], rounded_w[w]))

                def products(b):
                    for t in range(2):
                        eng.wait_ge(act_k, b.count(2, t + 1))
                        if b.past(2):
                            eng.wait_ge(pe_c, b.back(2).count(1, 1))
                        eng.tensor_tensor(kv[b.par][:, t, :], bank_kv[t][:, D:], k[:, t, :], ALU.mult).then_inc(dve_kv, 1)

                def gate(b):
                    eng.wait_ge(pe_c, b.count(1, 1))
                    eng.wait_ge(act_q, b.count(1, 1))
                    if b.past(2):
                        eng.wait_ge(pe_y, b.back(2).count(1, 1))
                    eng.tensor_tensor(o_t[b.par][:, :, :], bank_c[:, :, :], q[b.par][:, :, :],
                                      ALU.mult).then_inc(dve_o, 1)
                laps(eng, [(products, (0,)), *((step, (1,)) for step in norm.dve(eng)), (gate, (0,)), (round_weights, (0,))], 4)

            @block.gpsimd
            def _(eng):
                laps(eng, [(fetch.pool(eng), (0,)), (norm.pool(eng), (2,))], 4)


def rounded_attention(c):
    nc = c.nc
    with ExitStack() as stack:
        c.stack = stack
        bank_s = c.psum("ra_s", (P, 2, SCORES))
        bank_p = c.psum("ra_p", (P, HB, P))
        bank_a, bank_q = c.psum("ra_a", (P, 2, S)), c.psum("ra_q", (P, DC, S))
        bank_o, bank_y = c.psum("ra_o", (P, 2, S)), c.psum("ra_y", (P, 2, D))
        weight, k_all, v_all = c.cross_weight, c.cross_k, c.cross_v
        k_diag = [c.sb(f"ra_k_diag{p}", [P, DC, HB, CTX]) for p in range(2)]
        v_diag = [c.sb(f"ra_v_diag{p}", [P, HB, 2 * HD]) for p in range(2)]
        x_round = [c.sb(f"ra_x_round{p}", [P, 2, D]) for p in range(2)]
        x_t, q_t = c.sb("ra_x_t", [P, DC, S]), c.sb("ra_q_t", [P, DC, S])
        probs = c.sb("ra_probs", [P, 2, H, CTX])
        peak = c.sb("ra_peak_s", [P, 2, H])
        total = c.sb("ra_total", [P, 2, H])
        recip = [c.sb(f"ra_recip{p}", [P, 2, H]) for p in range(2)]
        probs_t = c.sb("ra_probs_t", [P, HB, S])
        o_t, o_rows = c.sb("ra_o_t", [P, 2, S]), c.sb("ra_o_rows", [P, 2, D])
        o_round, o_round_t = c.sb("ra_o_round", [P, 2, D]), c.sb("ra_o_round_t", [P, DC, S])
        residual = c.sb("ra_residual", [P, 2, D])

        x_rounding, o_rounding = Rounding(c, "ra_x"), Rounding(c, "ra_o")
        pool_diag = c.sem("ra_pool_diag")
        pool_res = c.sem("ra_pool_res")
        pe_x, act_x, pe_q, act_q = (c.sem("ra_" + n) for n in ("pe_x", "act_x", "pe_q", "act_q"))
        pe_s, act_exp = c.sem("ra_pe_s"), c.sem("ra_act_exp")
        SOFT = 7
        dve_soft = c.sem("ra_dve_soft")
        pe_p, act_p = c.sem("ra_pe_p"), c.sem("ra_act_p")
        pe_pv, act_o, pe_rows, dve_rows = (c.sem("ra_" + n) for n in ("pe_pv", "act_o", "pe_rows", "dve_rows"))
        pe_logits, act_logits = c.sem("ra_pe_logits"), c.sem("ra_act_logits")
        pe_or, act_or, pe_y = c.sem("ra_pe_or"), c.sem("ra_act_or"), c.sem("ra_pe_y")
        norm = Norm(c, "n5", bank_y[:, :, :], lambda eng, b: eng.wait_ge(pe_y, b.count(1, 1)),
                    bank_a[:, :, :].rearrange("p j t -> p (j t)"),
                    residual=(residual[:, :, :], lambda eng, b: eng.wait_ge(pool_res, b.count(1, 1))))

        with nc.Block() as block:
            @block.tensor
            def _(eng):
                def turn_x(a):
                    eng.wait_ge(x_rounding.dve_done, a.count(Rounding.PER, Rounding.PER))
                    if a.past(1):
                        eng.wait_ge(act_x, a.back(1).count(1, 1))
                    if a.past(2):
                        eng.wait_ge(dve_rows, a.back(2).count(1, 1))
                    if a.past(3):
                        eng.wait_ge(act_or, a.back(3).count(1, 1))
                    if a.past(4):
                        eng.wait_ge(norm.act_turned, a.back(4).count(1, 1))
                    turn_tiles(c, eng, bank_a, x_round[a.par]).then_inc(pe_x, 1)

                def project_q(a):
                    eng.wait_ge(act_x, a.count(1, 1))
                    if a.past(1):
                        eng.wait_ge(act_q, a.back(1).count(1, 1))
                    if a.past(4):
                        eng.wait_ge(act_logits, a.back(4).count(1, 1))
                    for j in range(DC):
                        for i in range(DC):
                            last = eng.matmul(bank_q[:, j, :], weight[0][:, i, j * P:(j + 1) * P], x_t[:, i, :],
                                              start=i == 0, stop=i == DC - 1)
                    last.then_inc(pe_q, 1)

                def score(a, t):
                    eng.wait_ge(act_q, a.count(1, 1))
                    eng.wait_ge(pool_diag, a.count(3, 2))
                    if t:
                        eng.wait_ge(dve_soft, a.count(SOFT, 2))
                    else:
                        if a.past(1):
                            eng.wait_ge(dve_soft, a.back(1).count(SOFT, 4))
                    for j in range(DC):
                        last = eng.matmul(bank_s[:, j, :], q_t[:, j, t * P:(t + 1) * P],
                                          k_diag[a.par][:, j, :, :].rearrange("p h k -> p (h k)"), start=True, stop=True)
                    last.then_inc(pe_s, 1)

                def turn_probs(b, t):
                    eng.wait_ge(act_exp, b.count(2, t + 1))
                    if t:
                        eng.wait_ge(act_p, b.count(2, 1))
                    else:
                        if b.past(1):
                            eng.wait_ge(act_p, b.back(1).count(2, 2))
                    for h in range(HB):
                        last = eng.transpose(bank_p[:, h, :],
                                             probs[:, t, 2 * h:2 * h + 2, :].rearrange("p h k -> p (h k)"), c.ident[:, :])
                    last.then_inc(pe_p, 1)

                def pv(b):
                    eng.wait_ge(act_p, b.count(2, 2))
                    eng.wait_ge(pool_diag, b.count(3, 3))
                    if b.past(1):
                        eng.wait_ge(act_o, b.back(1).count(1, 1))
                    for h in range(HB):
                        at = 32 * (h % 4)
                        last = eng.matmul(bank_o[at:at + 32, h // 4, :], v_diag[b.par][:, h, :], probs_t[:, h, :],
                                          start=True, stop=True)
                    last.then_inc(pe_pv, 1)

                def turn_o(a, b, z):
                    eng.wait_ge(act_o, b.count(1, 1))
                    if z:
                        eng.wait_ge(act_or, z.count(1, 1))
                    elif a:
                        eng.wait_ge(act_x, a.count(1, 1))
                    turn_tiles(c, eng, bank_a, o_t).then_inc(pe_rows, 1)

                def turn_rounded(a, z, y):
                    eng.wait_ge(o_rounding.dve_done, z.count(Rounding.PER, Rounding.PER))
                    if y:
                        eng.wait_ge(norm.act_turned, y.count(1, 1))
                    elif a:
                        eng.wait_ge(act_x, a.count(1, 1))
                    turn_tiles(c, eng, bank_a, o_round).then_inc(pe_or, 1)

                def out(b):
                    eng.wait_ge(act_or, b.count(1, 1))
                    if b.past(1):
                        eng.wait_ge(norm.dve_norm, b.back(1).count(norm.PER, norm.SUMMED))
                    for t in range(2):
                        for i in range(DC):
                            last = eng.matmul(bank_y[:, t, :], o_round_t[:, i, t * P:(t + 1) * P], weight[1][:, i, :],
                                              start=i == 0, stop=i == DC - 1)
                    last.then_inc(pe_y, 1)

                def router_logits(b, y):
                    eng.wait_ge(norm.act_turned, y.count(1, 1))
                    if b:
                        eng.wait_ge(act_q, b.count(1, 1))
                    elif y.past(1):
                        eng.wait_ge(act_logits, y.back(1).count(1, 1))
                    for i in range(DC):
                        last = eng.matmul(bank_q[0:E, 0, :], c.m_router[:, i, :],
                                          c.XT[:, bass.ds(i * B * S + S * y.n, S)], start=i == 0, stop=i == DC - 1)
                    last.then_inc(pe_logits, 1)

                turn_normed = norm.pe(eng)

                def turn_rows(a, z, y):
                    if a:
                        eng.wait_ge(act_x, a.count(1, 1))
                    elif z:
                        eng.wait_ge(dve_rows, z.count(1, 1))
                    else:
                        eng.wait_ge(act_or, y.count(1, 1))
                    turn_normed(y)

                def main(a, b, z, y, normed):
                    if normed:
                        router_logits(b, normed)
                    if a:
                        turn_x(a)
                    if b:
                        turn_probs(b, 0)
                    if y:
                        turn_rows(a, z, y)
                    if a:
                        project_q(a)
                    if z:
                        turn_rounded(a, z, y)
                    if b:
                        turn_probs(b, 1)
                    if z:
                        out(z)
                    if a:
                        score(a, 0)
                    if b:
                        pv(b)
                    if a:
                        score(a, 1)
                    if b:
                        turn_o(a, b, z)
                eng.wait_ge(c.in_mixture, 32)
                laps(eng, [(main, (1, 2, 3, 4, 5))], 6)

            @block.scalar
            def _(eng):
                def keep_x(a):
                    eng.wait_ge(pe_x, a.count(1, 1))
                    if a.past(1):
                        eng.wait_ge(pe_q, a.back(1).count(1, 1))
                    eng.activation(x_t[:, :, :], bank_a[:, :, :], ACT.Copy).then_inc(act_x, 1)

                def keep_probs(b, t):
                    eng.wait_ge(pe_p, b.count(2, t + 1))
                    if b.past(1):
                        eng.wait_ge(pe_pv, b.back(1).count(1, 1))
                    eng.activation(probs_t[:, :, t * P:(t + 1) * P], bank_p[:, :, :], ACT.Copy).then_inc(act_p, 1)

                def keep_q(a):
                    eng.wait_ge(pe_q, a.count(1, 1))
                    if a.past(1):
                        eng.wait_ge(pe_s, a.back(1).count(2, 2))
                    for j in range(DC):
                        last = eng.activation(q_t[:, j, :], bank_q[:, j, :], ACT.Identity, bias=c.a_bq[:, j:j + 1])
                    last.then_inc(act_q, 1)

                def exps(a, t):
                    eng.wait_ge(dve_soft, a.count(SOFT, 2 * t + 2))
                    eng.activation(probs[:, t, :, :], probs[:, t, :, :], ACT.Exp, scale=HD ** -0.5).then_inc(act_exp, 1)

                def keep_o(b):
                    eng.wait_ge(pe_pv, b.count(1, 1))
                    if b.past(1):
                        eng.wait_ge(pe_rows, b.back(1).count(1, 1))
                    eng.activation(o_t[:, :, :], bank_o[:, :, :], ACT.Copy).then_inc(act_o, 1)

                def keep_rounded(b):
                    eng.wait_ge(pe_or, b.count(1, 1))
                    if b.past(1):
                        eng.wait_ge(pe_y, b.back(1).count(1, 1))
                    eng.activation(o_round_t[:, :, :], bank_a[:, :, :], ACT.Copy).then_inc(act_or, 1)

                def keep_logits(y):
                    eng.wait_ge(pe_logits, y.count(1, 1))
                    eng.activation(c.logits_t[:, bass.ds(S * y.n, S)], bank_q[0:E, 0, :], ACT.Copy).then_inc(act_logits, 1)

                turned = norm.act(eng)

                def main(a, b, z, y, normed):
                    if normed:
                        keep_logits(normed)
                    if a:
                        keep_x(a)
                    if b:
                        keep_probs(b, 0)
                    if y:
                        turned(y)
                    if a:
                        keep_q(a)
                    if z:
                        keep_rounded(z)
                    if b:
                        keep_probs(b, 1)
                    if a:
                        exps(a, 0)
                    if b:
                        keep_o(b)
                    if a:
                        exps(a, 1)
                laps(eng, [(main, (1, 2, 3, 4, 5))], 6)

            @block.vector
            def _(eng):
                chain = Count(SOFT)

                def less_peak(a, t):
                    if t == 0:
                        chain.begin(a)
                        if a.past(1):
                            eng.wait_ge(dve_soft, a.back(1).count(SOFT, 6))
                    eng.wait_ge(pe_s, a.count(2, t + 1))
                    scores = bank_s[:, :, :].rearrange("p j (h k) -> p (j h) k", k=CTX)
                    eng.tensor_reduce(peak[:, t, :], scores, AX.X, ALU.max).then_inc(dve_soft, chain.one())
                    eng.wait_ge(dve_soft, chain.so_far())
                    if a.past(1):
                        eng.wait_ge(pe_p, a.back(1).count(2, t + 1))
                    eng.tensor_tensor(probs[:, t, :, :], scores,
                                      peak[:, t, :].unsqueeze(2).broadcast_to([P, H, CTX]), ALU.subtract).then_inc(dve_soft, chain.one())

                def add_up(a):
                    if a.past(1):
                        eng.wait_ge(dve_soft, a.back(1).count(SOFT, SOFT))
                    for t in range(2):
                        eng.wait_ge(act_exp, a.count(2, t + 1))
                        eng.tensor_reduce(total[:, t, :], probs[:, t, :, :], AX.X, ALU.add).then_inc(dve_soft, chain.one())
                    eng.wait_ge(dve_soft, chain.so_far())
                    if a.past(2):
                        eng.wait_ge(dve_rows, a.back(2).count(1, 1))
                    eng.reciprocal(recip[a.par][:, :, :], total[:, :, :]).then_inc(dve_soft, chain.one())
                    chain.end()

                def divide(b):
                    eng.wait_ge(pe_rows, b.count(1, 1))
                    eng.wait_ge(dve_soft, b.count(SOFT, SOFT))
                    if b.past(1):
                        eng.wait_ge(o_rounding.dve_done, b.back(1).count(Rounding.PER, Rounding.PER))
                    eng.tensor_tensor(o_rows[:, :, :].rearrange("p t (h d) -> p (t h) d", d=HD),
                                      bank_a[:, :, :].rearrange("p t (h d) -> p (t h) d", d=HD),
                                      recip[b.par][:, :, :].rearrange("p t h -> p (t h)").unsqueeze(2).broadcast_to(
                                          [P, 2 * H, HD]), ALU.mult).then_inc(dve_rows, 1)

                def round_o(b):
                    eng.wait_ge(dve_rows, b.count(1, 1))
                    if b.past(1):
                        eng.wait_ge(pe_or, b.back(1).count(1, 1))
                    return o_rounding, b, o_rows[:, :, :], o_round

                def round_x(n):
                    x = c.X[:, bass.ds(2 * D * n.n, 2 * D)].rearrange("p (t d) -> p t d", t=2)
                    if n.past(2):
                        eng.wait_ge(pe_x, n.back(2).count(1, 1))
                    return x_rounding, n, x, x_round[n.par]

                sum_up, normalise = norm.dve(eng)

                def main(n, a, b, z):
                    round_rows(c, eng, *([round_o(z)] if z else []), *([round_x(n)] if n else []))
                    if a:
                        less_peak(a, 0)
                    if z:
                        sum_up(z)
                    if a:
                        less_peak(a, 1)
                    if z:
                        normalise(z)
                    if b:
                        divide(b)
                    if a:
                        add_up(a)
                laps(eng, [(main, (0, 1, 2, 3))], 6)

            @block.gpsimd
            def _(eng):
                def diagonals(n):
                    for j in range(DC):
                        if n.past(2):
                            eng.wait_ge(pe_s, n.back(2).count(2, 2))
                        apart(c, eng)
                        eng.tensor_tensor(k_diag[n.par][:, j, :, :],
                                          k_all[:, bass.ds(j * B * CTX + CTX * n.n, CTX)].unsqueeze(1).broadcast_to(
                                              [P, HB, CTX]),
                                          c.head_of[:, :].unsqueeze(2).broadcast_to([P, HB, CTX]),
                                          ALU.mult).then_inc(pool_diag, 1)
                    if n.past(2):
                        eng.wait_ge(pe_pv, n.back(2).count(1, 1))
                    apart(c, eng)
                    eng.tensor_tensor(v_diag[n.par][:, :, :],
                                      v_all[:, bass.ds(D * n.n, D)].rearrange("p (h d) -> p h d", h=HB),
                                      c.half_of[:, :].unsqueeze(1).broadcast_to([P, HB, 2 * HD]),
                                      ALU.mult).then_inc(pool_diag, 1)

                def add_bias(b):
                    if b.past(1):
                        eng.wait_ge(norm.dve_norm, b.back(1).count(norm.PER, norm.SUMMED))
                    apart(c, eng)
                    eng.tensor_tensor(residual[:, :, :],
                                      c.X[:, bass.ds(2 * D * b.n, 2 * D)].rearrange("p (t d) -> p t d", t=2),
                                      c.a_bp[:, :].rearrange("p (t d) -> p t d", t=2), ALU.add).then_inc(pool_res, 1)

                laps(eng, [(add_bias, (3,)), (norm.pool(eng), (3,)), (diagonals, (0,))], 6)




E = 16
KE = 2
F = 176
FP = 2 * P
SLOTS_E = TILES * KE
MTILES = B * S * KE // P + E
AHEAD = 4
EARLY = 3 * B // 4
I32 = mybir.dt.int32


def route_experts(c):
    nc = c.nc
    with ExitStack() as stack:
        c.stack = stack
        bank_l, bank_r, bank_n = c.psum("re_l", (P, TILES, E)), c.psum("re_r", (P, TILES, E)), c.psum("re_n", (P, E))
        biased = c.sb("re_biased", [P, TILES, E])
        best, best_i = c.sb("re_best", [P, TILES, TOP]), c.sb("re_best_i", [P, TILES, TOP], U32)
        best_f = c.sb("re_best_f", [P, TILES, KE])
        peak, less = c.sb("re_peak", [P, TILES]), c.sb("re_less", [P, TILES, E])
        exps = c.sb("re_exps", [P, TILES, E])
        chosen, picked = c.sb("re_chosen", [P, TILES, KE, E]), c.sb("re_picked", [P, TILES, KE, E])
        both = c.sb("re_both", [P, 2 * TILES, E], BF16)
        w, w_sum, w_inv = c.sb("re_w", [P, TILES, KE]), c.sb("re_w_sum", [P, TILES]), c.sb("re_w_inv", [P, TILES])
        ranks = c.sb("re_ranks", [P, SLOTS_E])
        counts, tiles_of = c.sb("re_counts", [P, E]), c.sb("re_tiles", [P, E])
        before, start, end = c.sb("re_before", [P, E, E]), c.sb("re_start", [P, E]), c.sb("re_end", [P, E])
        starts = c.sb("re_starts", [P, SLOTS_E])
        done, expert = c.sb("re_done", [P, MTILES, E]), c.sb("re_expert", [P, MTILES])
        place = c.sb("re_place", [P, SLOTS_E])
        pe, act_exps, dve_route = (c.sem("re_" + n) for n in ("pe", "act_exps", "dve"))
        LOGITS, RANKS = 1, 2
        EXP_READY, BOTH_READY = [0], [0]

        with nc.Block() as block:
            @block.sync
            def _(eng):
                c.load_down(eng)

            @block.vector
            def _(eng):
                chain = Count(0)
                eng.memset(both[:, 0:TILES, :], 0.0).then_inc(dve_route, chain.one())
                eng.wait_ge(pe, LOGITS)
                eng.tensor_tensor(biased[:, :, :], bank_l[:, :, :],
                                  c.m_bias[:, :].unsqueeze(1).broadcast_to([P, TILES, E]), ALU.add).then_inc(dve_route, chain.one())
                eng.tensor_reduce(peak[:, :], bank_l[:, :, :], AX.X, ALU.max).then_inc(dve_route, chain.one())
                eng.wait_ge(dve_route, chain.so_far())
                eng.tensor_tensor(less[:, :, :], bank_l[:, :, :],
                                  peak[:, :].unsqueeze(2).broadcast_to([P, TILES, E]), ALU.subtract).then_inc(dve_route, chain.one())
                EXP_READY[0] = chain.k
                for t in range(TILES):
                    eng.max(best[:, t, :], biased[:, t, :]).then_inc(dve_route, chain.one())
                eng.wait_ge(dve_route, chain.so_far())
                for t in range(TILES):
                    eng.max_index(best_i[:, t, :], best[:, t, :], biased[:, t, :]).then_inc(dve_route, chain.one())
                eng.wait_ge(dve_route, chain.so_far())
                eng.tensor_copy(best_f[:, :, :], best_i[:, :, 0:KE]).then_inc(dve_route, chain.one())
                eng.wait_ge(dve_route, chain.so_far())
                shape = [P, SLOTS_E, E]
                flat = "p t k e -> p (t k) e"
                eng.tensor_tensor(chosen[:, :, :, :].rearrange(flat), c.iota[:, 0:E].unsqueeze(1).broadcast_to(shape),
                                  best_f[:, :, :].rearrange("p t k -> p (t k)").unsqueeze(2).broadcast_to(shape),
                                  ALU.is_equal).then_inc(dve_route, chain.one())
                eng.wait_ge(dve_route, chain.so_far())
                eng.tensor_tensor(both[:, TILES:, :], chosen[:, :, 0, :], chosen[:, :, 1, :], ALU.add).then_inc(dve_route, chain.one())
                BOTH_READY[0] = chain.k
                eng.wait_ge(act_exps, 1)
                eng.tensor_tensor(picked[:, :, :, :], chosen[:, :, :, :],
                                  exps[:, :, :].unsqueeze(2).broadcast_to([P, TILES, KE, E]), ALU.mult).then_inc(dve_route, chain.one())
                eng.wait_ge(dve_route, chain.so_far())
                eng.tensor_reduce(w[:, :, :], picked[:, :, :, :], AX.X, ALU.add).then_inc(dve_route, chain.one())
                eng.wait_ge(dve_route, chain.so_far())
                eng.tensor_reduce(w_sum[:, :], w[:, :, :], AX.X, ALU.add).then_inc(dve_route, chain.one())
                eng.wait_ge(dve_route, chain.so_far())
                eng.reciprocal(w_inv[:, :], w_sum[:, :]).then_inc(dve_route, chain.one())
                eng.wait_ge(dve_route, chain.so_far())
                eng.tensor_tensor(c.row_weights[:, :].rearrange("p (t k) -> p t k", k=KE), w[:, :, :],
                                  w_inv[:, :].unsqueeze(2).broadcast_to([P, TILES, KE]), ALU.mult).then_inc(dve_route, chain.one())
                eng.wait_ge(pe, RANKS)
                eng.tensor_tensor(picked[:, :, :, :], chosen[:, :, :, :],
                                  bank_r[:, :, :].unsqueeze(2).broadcast_to([P, TILES, KE, E]), ALU.mult).then_inc(dve_route, chain.one())
                eng.wait_ge(dve_route, chain.so_far())
                eng.tensor_reduce(ranks[:, :], picked[:, :, :, :].rearrange(flat), AX.X, ALU.add).then_inc(dve_route, chain.one())
                eng.tensor_scalar(counts[:, :], bank_n[:, :], 1 / P, (P - 1) / P - 0.5 + 0.25 / P, ALU.mult, ALU.add).then_inc(dve_route, chain.one())
                eng.wait_ge(dve_route, chain.so_far())
                eng.tensor_scalar(counts[:, :], counts[:, :], ROUND, None, ALU.add).then_inc(dve_route, chain.one())
                eng.wait_ge(dve_route, chain.so_far())
                eng.tensor_scalar(tiles_of[:, :], counts[:, :], ROUND, None, ALU.subtract).then_inc(dve_route, chain.one())
                eng.wait_ge(dve_route, chain.so_far())
                eng.tensor_tensor(before[:, :, :], tiles_of[:, :].unsqueeze(1).broadcast_to([P, E, E]),
                                  c.earlier[:, :].rearrange("p (e f) -> p e f", e=E), ALU.mult).then_inc(dve_route, chain.one())
                eng.wait_ge(dve_route, chain.so_far())
                eng.tensor_reduce(start[:, :], before[:, :, :], AX.X, ALU.add).then_inc(dve_route, chain.one())
                eng.wait_ge(dve_route, chain.so_far())
                eng.tensor_tensor(end[:, :], start[:, :], tiles_of[:, :], ALU.add).then_inc(dve_route, chain.one())
                eng.tensor_tensor(picked[:, :, :, :].rearrange(flat), chosen[:, :, :, :].rearrange(flat),
                                  start[:, :].unsqueeze(1).broadcast_to(shape), ALU.mult).then_inc(dve_route, chain.one())
                eng.wait_ge(dve_route, chain.so_far())
                eng.tensor_reduce(starts[:, :], picked[:, :, :, :].rearrange(flat), AX.X, ALU.add).then_inc(dve_route, chain.one())
                eng.wait_ge(dve_route, chain.so_far())
                eng.scalar_tensor_tensor(place[:, :], starts[:, :], float(P), ranks[:, :], ALU.mult, ALU.add).then_inc(dve_route, chain.one())
                eng.wait_ge(dve_route, chain.so_far())
                eng.tensor_copy(c.places[:, :], place[:, :]).then_inc(dve_route, chain.one())
                eng.tensor_tensor(done[:, :, :], end[:, :].unsqueeze(1).broadcast_to([P, MTILES, E]),
                                  c.iota[:, 0:MTILES].unsqueeze(2).broadcast_to([P, MTILES, E]), ALU.is_le).then_inc(dve_route, chain.one())
                eng.wait_ge(dve_route, chain.so_far())
                eng.tensor_reduce(expert[:, :], done[:, :, :], AX.X, ALU.add).then_inc(dve_route, chain.one())
                eng.wait_ge(dve_route, chain.so_far())
                eng.tensor_scalar(c.tile_expert[:, :], expert[:, :], float(E - 1), None, ALU.min).then_inc(dve_route, chain.one())
                eng.wait_ge(dve_route, chain.so_far())

            @block.tensor
            def _(eng):
                for t in range(TILES):
                    last = eng.transpose(bank_l[:, t, :], c.logits_t[:, t * P:(t + 1) * P], c.ident[0:E, 0:E])
                last.then_inc(pe, 1)
                eng.wait_ge(dve_route, BOTH_READY[0])
                eng.matmul(bank_r[:, :, :], c.below_b[:, :], both[:, TILES:, :], start=True, stop=False)
                for back in range(1, TILES):
                    eng.matmul(bank_r[:, :, :], c.ones_b[:, :], both[:, TILES - back:2 * TILES - back, :],
                               start=False, stop=back == TILES - 1)
                for t in range(TILES):
                    last = eng.matmul(bank_n[:, :], c.ones_b[:, :], both[:, TILES + t, :], start=t == 0, stop=t == TILES - 1)
                last.then_inc(pe, 1)

            @block.scalar
            def _(eng):
                eng.wait_ge(dve_route, EXP_READY[0])
                eng.activation(exps[:, :, :], less[:, :, :], ACT.Exp).then_inc(act_exps, 1)


class Shared:

    def __init__(self, c):
        self.c = c
        self.pe_u, self.act_u, self.dve_u, self.pe_y, self.dve_y = (
            c.sem("se_" + n) for n in ("pe_u", "act_u", "dve_u", "pe_y", "dve_y"))

    def place(self, name):
        c = self.c
        self.bank_u = [c.psum(f"{name}_u{k}", (P, 2, S)) for k in range(2)]
        self.bank_y = [c.psum(f"{name}_y{p}", (P, 2, D)) for p in range(2)]
        self.act = [c.sb(f"{name}_act{k}", [P, S]) for k in range(2)]
        self.hidden = [c.sb(f"{name}_hidden{p}", [P, 2, S]) for p in range(2)]

    def up(self, eng, b):
        c = self.c
        for k in range(2):
            if b.past(1):
                eng.wait_ge(self.dve_u, b.back(1).count(2, k + 1))
            for w in range(2):
                for i in range(DC):
                    last = eng.matmul(self.bank_u[k][:, w, :], (c.s_gate, c.s_up)[w][:, i, k * P:(k + 1) * P],
                                      c.XT[:, bass.ds(i * B * S + S * b.n, S)], start=i == 0, stop=i == DC - 1)
            last.then_inc(self.pe_u, 1)

    def down(self, eng, b):
        eng.wait_ge(self.dve_u, b.count(2, 2))
        if b.past(2):
            eng.wait_ge(self.dve_y, b.back(2).count(1, 1))
        for t in range(2):
            for k in range(2):
                last = eng.matmul(self.bank_y[b.par][:, t, :], self.hidden[b.par][:, k, t * P:(t + 1) * P],
                                  self.c.s_down[:, k, :], start=k == 0, stop=k == 1)
        last.then_inc(self.pe_y, 1)

    def silu(self, eng, b):
        for k in range(2):
            eng.wait_ge(self.pe_u, b.count(2, k + 1))
            if b.past(1):
                eng.wait_ge(self.dve_u, b.back(1).count(2, k + 1))
            eng.activation(self.act[k][:, :], self.bank_u[k][:, 0, :], ACT.Silu).then_inc(self.act_u, 1)

    def hide(self, eng, b):
        for k in range(2):
            eng.wait_ge(self.act_u, b.count(2, k + 1))
            if b.past(2):
                eng.wait_ge(self.pe_y, b.back(2).count(1, 1))
            eng.tensor_tensor(self.hidden[b.par][:, k, :], self.act[k][:, :], self.bank_u[k][:, 1, :],
                              ALU.mult).then_inc(self.dve_u, 1)

    def keep(self, eng, b):
        eng.wait_ge(self.pe_y, b.count(1, 1))
        at = bass.ds(2 * D * b.n, 2 * D)
        eng.tensor_tensor(self.c.with_shared[:, at].rearrange("p (t d) -> p t d", t=2), self.bank_y[b.par][:, :, :],
                          self.c.X[:, at].rearrange("p (t d) -> p t d", t=2), ALU.add).then_inc(self.dve_y, 1)


def scatter(c):
    nc = c.nc
    with ExitStack() as stack:
        c.stack = stack
        c.shared.place("sc")
        sent = c.sem("sc_rows_sent")
        with nc.Block() as block:
            @block.gpsimd
            def _(eng):
                eng.wait_ge(c.in_mixture, 32)
                for s in range(SLOTS_E):
                    t = s // KE
                    eng.indirect_dma_start(c.d_sorted, bass.IndirectOffsetOnAxis(ap=c.places[:, s:s + 1], axis=0),
                                           c.X[:, t * D:(t + 1) * D], None).then_inc(sent, 16)
                eng.wait_ge(sent, 16 * SLOTS_E)

            @block.tensor
            def _(eng):
                laps(eng, [(lambda b: c.shared.up(eng, b), (0,)), (lambda b: c.shared.down(eng, b), (1,))], EARLY, EARLY)

            @block.scalar
            def _(eng):
                laps(eng, [(lambda b: c.shared.silu(eng, b), (0,))], EARLY, EARLY)

            @block.vector
            def _(eng):
                laps(eng, [(lambda b: c.shared.hide(eng, b), (0,)), (lambda b: c.shared.keep(eng, b), (1,))], EARLY, EARLY)


def experts(c):
    nc = c.nc
    with ExitStack() as stack:
        c.stack = stack
        bank_x = [c.psum(f"ex_x{p}", (P, DC, P)) for p in range(2)]
        bank_u = [c.psum(f"ex_u{p}", (P, 2 * F)) for p in range(2)]
        bank_h = [c.psum(f"ex_h{p}", (P, 2, P)) for p in range(2)]
        bank_y = [c.psum(f"ex_y{p}", (P, D)) for p in range(2)]
        rows = [c.sb(f"ex_rows{q}", [P, D]) for q in range(AHEAD)]
        x_t = [c.sb(f"ex_x_t{p}", [P, DC, P]) for p in range(2)]
        act = [c.sb(f"ex_act{p}", [P, F]) for p in range(2)]
        hidden = [c.sb(f"ex_hidden{p}", [P, FP]) for p in range(2)]
        hidden_t = [c.sb(f"ex_hidden_t{p}", [P, 2, P]) for p in range(2)]
        y = [c.sb(f"ex_y_sb{p}", [P, D]) for p in range(2)]
        loaded = [c.sem(f"ex_loaded{q}") for q in range(AHEAD)]
        kept = c.sems("ex_kept")
        pe_x, act_x, pe_u, act_u, dve_h = (c.sem("ex_" + n) for n in ("pe_x", "act_x", "pe_u", "act_u", "dve_h"))
        pe_h, dve_ht, pe_y, act_y = (c.sem("ex_" + n) for n in ("pe_h", "dve_ht", "pe_y", "act_y"))
        dve_init = c.sem("ex_dve_init")
        with nc.Block() as block:
            @block.sync
            def _(eng):
                def load(n):
                    if n.past(AHEAD):
                        eng.wait_ge(pe_x, n.back(AHEAD).count(1, 1))
                    eng.dma_start(rows[n.low % AHEAD][:, :], c.d_sorted[bass.ds(P * n.n, P), :]
                                  ).then_inc(loaded[n.low % AHEAD], 16)
                laps(eng, [(load, (0,))], AHEAD, MTILES, AHEAD)

            @block.gpsimd
            def _(eng):

                def store(n):
                    eng.wait_ge(act_y, n.count(1, 1))
                    eng.dma_start(c.d_expert_out[bass.ds(P * n.n, P), :], y[n.par][:, :]).then_inc(kept[n.par], 16)
                laps(eng, [(store, (0,))], 2, MTILES)
                for p in range(2):
                    eng.wait_ge(kept[p], 16 * (MTILES // 2))

            @block.tensor
            def _(eng):
                eng.wait_ge(dve_init, 2)
                eng.wait_ge(c.in_w7, 16)

                def turn_x(n):
                    eng.wait_ge(loaded[n.low % AHEAD], n.landed(1, AHEAD))
                    if n.past(2):
                        eng.wait_ge(act_x, n.back(2).count(1, 1))
                    for i in range(DC):
                        last = eng.transpose(bank_x[n.par][:, i, :], rows[n.low % AHEAD][:, i * P:(i + 1) * P], c.ident[:, :])
                    last.then_inc(pe_x, 1)

                def turn_hidden(n):
                    eng.wait_ge(dve_h, n.count(1, 1))
                    if n.past(2):
                        eng.wait_ge(dve_ht, n.back(2).count(1, 1))
                    for k in range(2):
                        last = eng.transpose(bank_h[n.par][:, k, :], hidden[n.par][:, k * P:(k + 1) * P], c.ident[:, :])
                    last.then_inc(pe_h, 1)

                def expert_of(n):
                    return eng.value_load(c.tile_expert[0:1, bass.ds(n.n, 1)], min_val=0, max_val=E - 1)

                def up(n, expert):
                    eng.wait_ge(act_x, n.count(1, 1))
                    if n.past(2):
                        eng.wait_ge(dve_h, n.back(2).count(1, 1))
                    for i in range(DC):
                        last = eng.matmul(bank_u[n.par][:, :], x_t[n.par][:, i, :],
                                          c.m_up[:, bass.ds(expert * (2 * F) + i * E * 2 * F, 2 * F)],
                                          start=i == 0, stop=i == DC - 1)
                    last.then_inc(pe_u, 1)

                def down(n, expert):
                    eng.wait_ge(dve_ht, n.count(1, 1))
                    if n.past(2):
                        eng.wait_ge(act_y, n.back(2).count(1, 1))
                    for k in range(2):
                        last = eng.matmul(bank_y[n.par][:, :], hidden_t[n.par][:, k, :],
                                          c.m_down[:, bass.ds(expert * D + k * E * D, D)], start=k == 0, stop=k == 1)
                    last.then_inc(pe_y, 1)

                def main(n, a, b):
                    if a:
                        expert_a = expert_of(a)
                    if b:
                        expert_b = expert_of(b)
                    if n:
                        turn_x(n)
                    if b:
                        turn_hidden(b)
                    if a:
                        up(a, expert_a)
                    if b:
                        down(b, expert_b)
                laps(eng, [(main, (0, 1, 2))], 4, MTILES, 4)

            @block.scalar
            def _(eng):
                def keep_x(n):
                    eng.wait_ge(pe_x, n.count(1, 1))
                    if n.past(2):
                        eng.wait_ge(pe_u, n.back(2).count(1, 1))
                    eng.activation(x_t[n.par][:, :, :], bank_x[n.par][:, :, :], ACT.Copy).then_inc(act_x, 1)

                def silu(n):
                    eng.wait_ge(pe_u, n.count(1, 1))
                    if n.past(2):
                        eng.wait_ge(dve_h, n.back(2).count(1, 1))
                    eng.activation(act[n.par][:, :], bank_u[n.par][:, 0:F], ACT.Silu).then_inc(act_u, 1)

                def keep_y(n):
                    eng.wait_ge(pe_y, n.count(1, 1))
                    if n.past(2):
                        eng.wait_ge(kept[n.back(2).par], n.back(2).landed(1))
                    eng.activation(y[n.par][:, :], bank_y[n.par][:, :], ACT.Copy).then_inc(act_y, 1)
                laps(eng, [(keep_x, (0,)), (silu, (1,)), (keep_y, (2,))], 4, MTILES, 4)

            @block.vector
            def _(eng):
                for p in range(2):
                    eng.memset(hidden[p][:, F:FP], 0.0).then_inc(dve_init, 1)

                def turn(n):
                    eng.wait_ge(pe_h, n.count(1, 1))
                    if n.past(2):
                        eng.wait_ge(pe_y, n.back(2).count(1, 1))
                    eng.tensor_copy(hidden_t[n.par][:, :, :], bank_h[n.par][:, :, :]).then_inc(dve_ht, 1)

                def hide(n):
                    eng.wait_ge(act_u, n.count(1, 1))
                    if n.past(2):
                        eng.wait_ge(pe_h, n.back(2).count(1, 1))
                    eng.tensor_tensor(hidden[n.par][:, 0:F], act[n.par][:, :], bank_u[n.par][:, F:], ALU.mult).then_inc(dve_h, 1)
                laps(eng, [(turn, (2,)), (hide, (1,))], 4, MTILES, 4)


def combine(c, out):
    nc = c.nc
    with ExitStack() as stack:
        c.stack = stack
        c.shared.place("co_shared")
        got = [c.sb(f"co_got{q}", [P, 2, KE, D]) for q in range(AHEAD)]
        total = [c.sb(f"co_total{p}", [P, 2, D]) for p in range(2)]
        stats, moments = c.sb("co_stats", [P, 2, 6]), [c.sb(f"co_moments{p}", [P, 2, 2]) for p in range(2)]
        spread, rstd = c.sb("co_spread", [P, 2]), [c.sb(f"co_rstd{p}", [P, 2]) for p in range(2)]
        rows = [c.sb(f"co_rows{p}", [P, 2, D]) for p in range(2)]
        fetched, stored = [c.sem(f"co_fetched{q}") for q in range(AHEAD)], c.sems("co_stored")
        SUMMED, MOMENTS, NORMED, SCALED = 2 * KE, 2 * KE + 4, 2, 2
        dve_sum, dve_norm, pool_rstd = c.sem("co_dve_sum"), c.sem("co_dve_norm"), c.sem("co_pool_rstd")
        dst = out.rearrange("b (t p) d -> b p t d", p=P)
        with nc.Block() as block:
            @block.gpsimd
            def _(eng):
                def fetch(b):
                    if b.past(AHEAD):
                        eng.wait_ge(dve_sum, b.back(AHEAD).count(MOMENTS, SUMMED))
                    for t in range(2):
                        for k in range(KE):
                            s = (2 * b.n + t) * KE + k
                            eng.indirect_dma_start(got[b.low % AHEAD][:, t, k, :], None, c.d_expert_out,
                                                   bass.IndirectOffsetOnAxis(ap=c.places[:, s:s + 1], axis=0)
                                                   ).then_inc(fetched[b.low % AHEAD], 16)

                def scale(b):
                    eng.wait_ge(dve_sum, b.count(MOMENTS, MOMENTS))
                    if b.past(1):
                        eng.wait_ge(pool_rstd, b.back(1).count(SCALED, SCALED))
                    eng.tensor_scalar(spread[:, :], moments[b.par][:, :, 1], EPS, None, ALU.add).then_inc(pool_rstd, 1)
                    eng.wait_ge(pool_rstd, b.count(SCALED, 1))
                    if b.past(2):
                        eng.wait_ge(dve_norm, b.back(2).count(NORMED, NORMED))
                    eng.tensor_tensor(rstd[b.par][:, :], spread[:, :], c.minus_half[:, :], ALU.pow).then_inc(pool_rstd, 1)
                laps(eng, [(fetch, (0,)), (scale, (2,))], B, unroll=AHEAD)

            @block.tensor
            def _(eng):
                laps(eng, [(lambda b: c.shared.up(eng, b), (0,)), (lambda b: c.shared.down(eng, b), (1,))], B, B, begin=EARLY)

            @block.scalar
            def _(eng):
                laps(eng, [(lambda b: c.shared.silu(eng, b), (0,))], B, B, begin=EARLY)

            @block.vector
            def _(eng):
                def share(b):
                    if b.low + EARLY < B:
                        c.shared.hide(eng, Lap(b.low + EARLY))
                    if 0 < b.low <= B - EARLY:
                        c.shared.keep(eng, Lap(b.low + EARLY - 1))

                sums = Count(MOMENTS)

                def add_up(b):
                    sums.begin(b)
                    eng.wait_ge(fetched[b.low % AHEAD], b.landed(2 * KE, AHEAD))
                    if b.past(2):
                        eng.wait_ge(dve_norm, b.back(2).count(NORMED, NORMED))
                    eng.wait_ge(c.shared.dve_y, b.count(1, 1))
                    for k in range(KE):
                        for t in range(2):
                            s = (2 * b.n + t) * KE + k
                            before = (total[b.par][:, t, :] if k else
                                      c.with_shared[:, (2 * b.n + t) * D:(2 * b.n + t + 1) * D])
                            eng.scalar_tensor_tensor(total[b.par][:, t, :], got[b.low % AHEAD][:, t, k, :],
                                                     c.row_weights[:, s:s + 1], before, ALU.mult, ALU.add).then_inc(dve_sum, sums.one())
                        eng.wait_ge(dve_sum, sums.so_far())
                    for t in range(2):
                        eng.bn_stats(stats[:, t, :], total[b.par][:, t, :]).then_inc(dve_sum, sums.one())
                    eng.wait_ge(dve_sum, sums.so_far())
                    if b.past(2):
                        eng.wait_ge(pool_rstd, b.back(2).count(SCALED, 1))
                    for t in range(2):
                        eng.bn_aggr(moments[b.par][:, t, :], stats[:, t, :]).then_inc(dve_sum, sums.one())
                    eng.wait_ge(dve_sum, sums.so_far())
                    sums.end()

                def normalise(b):
                    eng.wait_ge(pool_rstd, b.count(SCALED, SCALED))
                    if b.past(2):
                        eng.wait_ge(stored[b.back(2).par], b.back(2).landed(1))
                    for t in range(2):
                        eng.tensor_scalar(rows[b.par][:, t, :], total[b.par][:, t, :], moments[b.par][:, t, 0:1],
                                          rstd[b.par][:, t:t + 1], ALU.subtract, ALU.mult).then_inc(dve_norm, 1)
                laps(eng, [(share, (0,)), (add_up, (0,)), (normalise, (1,))], B, unroll=AHEAD)

            @block.sync
            def _(eng):
                def store(b):
                    eng.wait_ge(dve_norm, b.count(NORMED, NORMED))
                    eng.dma_start(dst[b.n], rows[b.par][:, :, :]).then_inc(stored[b.par], 16)
                laps(eng, [(store, (0,))], B)
                for p in range(2):
                    eng.wait_ge(stored[p], 16 * (B // 2))




CONST = {"ident": P, "iota": NKEYS, "rank": TOP, "tri": S, "earlier": E * E}
CONST_B = {"ident": P, "below": P, "ones": P}
PACK2 = {"q": DC * D, "k": DC * D, "v": DC * D, "o": DC * D}
PACK3 = {"query": DC * RETR, "keys": 2 * P, "down_embed": DC * EXPERTS, "up_embed": EB * D, "gate": DC * INTER,
         "up": DC * INTER, "down": FB * D}
PACK4 = {"kv": DC * 2 * D, "q": DC * D, "o": DC * D}
PACK5 = {"q": DC * D, "p": DC * D, "k": DC * D, "v": DC * D, "ctx_all": DC * B * CTX, "ctx_twice": DC * B * P,
         "bq": DC, "bk": DC, "bv": D, "bp": 2 * D, "head_of": HB, "half_of": 2 * HD}
PACK6 = {"router": DC * E, "bias": E, "s_gate": DC * FP, "s_up": DC * FP, "s_down": DC * D, "up": DC * E * 2 * F}
PACK1 = {"w_q": DC * D, "w_k": DC * D, "b_q": DC, "b_k": DC, "w_v": DC * D, "w_o": GROUPS * D, "bv_twice": 2 * D}
FIRST = 2 * (DC * D + DC)


def views(tile, widths):
    at, out = 0, {}
    for name, n in widths.items():
        out[name] = tile[:, at:at + n]
        at += n
    return out


def blocks(view, n):
    return view.rearrange("p (k n) -> p k n", k=n)


def decoder(nc, x, xt, const, const_b, pack1, pack2, pack3, pack4, pack5, pack6, pack7, ctx, ctx_t, out):
    c = Chip(nc)
    with c.whole:
        c.X = c.sb("X", [P, TILES * D])
        c.XT = c.sb("XT", [P, DC * B * S])
        c.minus_half = c.sb("minus_half", [P, 2])
        const_sb = c.sb("const", [P, sum(CONST.values())])
        c.ident, c.iota, c.rank, c.tri, c.earlier = views(const_sb, CONST).values()
        const_b_sb = c.sb("const_b", [P, sum(CONST_B.values())], BF16)
        c.ident_b, c.below_b, c.ones_b = views(const_b_sb, CONST_B).values()
        c.pool_const = c.sem("pool_const")
        c.in_first, c.in_xt, c.in_x, c.in_packs, c.in_mixture, c.in_w7 = (c.sem("in_" + n) for n in ("first", "xt", "x", "packs", "mixture", "w7"))
        c.d_parts = [nc.dram_tensor(f"parts_{w}", [B, 3, D, S], BF16, kind="Internal").ap() for w in "qk"]
        c.d_sorted = nc.dram_tensor("sorted_rows", [MTILES * P, D], F32, kind="Internal").ap()
        c.d_expert_out = nc.dram_tensor("expert_out", [MTILES * P, D], F32, kind="Internal").ap()
        c.d_ctx, c.d_ctx_t = ctx, ctx_t
        zeros = c.sb("zeros", [P, D])
        w4, w5 = c.sb("pack4", [P, sum(PACK4.values())]), c.sb("pack5", [P, sum(PACK5.values())])
        v4, v5 = views(w4, PACK4), views(w5, PACK5)
        c.r_kv, c.r_q, c.r_o = (blocks(v4[n], DC) for n in ("kv", "q", "o"))
        c.a_q, c.a_p, c.a_k, c.a_v, c.ctx_all, c.ctx_twice = (
            blocks(v5[n], DC) for n in ("q", "p", "k", "v", "ctx_all", "ctx_twice"))
        c.a_bq, c.a_bk, c.a_bv, c.a_bp, c.head_of, c.half_of = (
            v5[n] for n in ("bq", "bk", "bv", "bp", "head_of", "half_of"))
        with ExitStack() as first_layer:
            c.stack = first_layer
            w1, w2, w3 = (c.sb(n, [P, sum(pack.values())])
                          for n, pack in (("pack1", PACK1), ("pack2", PACK2), ("pack3", PACK3)))
            v1, v2, v3 = views(w1, PACK1), views(w2, PACK2), views(w3, PACK3)
            c.w_qk, c.b_qk = [blocks(v1["w_q"], DC), blocks(v1["w_k"], DC)], [v1["b_q"], v1["b_k"]]
            c.w_v, c.w_o, c.bv_twice = blocks(v1["w_v"], DC), blocks(v1["w_o"], GROUPS), v1["bv_twice"]
            c.x0_q, c.x0_k, c.x0_v, c.x0_o = (blocks(v2[n], DC) for n in "qkvo")
            c.w_query, c.keys, c.w_down_embed = (
                blocks(v3["query"], DC), blocks(v3["keys"], 2), blocks(v3["down_embed"], DC))
            c.w_up_embed, c.f_gate, c.f_up = blocks(v3["up_embed"], EB), blocks(v3["gate"], DC), blocks(v3["up"], DC)
            c.f_down = blocks(v3["down"], FB)
            attention_operands = first_layer.enter_context(ExitStack())
            c.stack = attention_operands
            c.qs = [c.sb(f"qs{p}", [P, H, S], BF16) for p in range(2)]
            c.ks = [c.sb(f"ks{p}", [P, H, S], BF16) for p in range(2)]
            c.v = [c.sb(f"v{p}", [P, 2, H, 2 * HD]) for p in range(2)]
            quarter = sum(PACK3.values()) // 4
            w3_pieces = [(w3[:, n * quarter:(n + 1) * quarter], pack3[:, n * quarter:(n + 1) * quarter]) for n in range(4)]
            c.later_packs = [[(w2[:, :], pack2), (w4[:, :], pack4)], w3_pieces[0:2], w3_pieces[2:4], [(w5[:, :], pack5)]]
            c.operands_init, c.parts_in = c.sem("operands_init"), [c.sems("parts_in_first"), c.sems("parts_in_second")]
            with nc.Block() as block:
                @block.sync
                def _(eng):
                    XT, src = (a.rearrange("p (j t) -> p j t", j=DC) for a in (c.XT[:, :], xt))
                    eng.dma_start(w1[:, 0:FIRST], pack1[:, 0:FIRST]).then_inc(c.in_first, 16)
                    eng.dma_start(XT[:, :, 0:2 * S], src[:, :, 0:2 * S]).then_inc(c.in_first, 16)
                    eng.dma_start(XT[:, :, 2 * S:], src[:, :, 2 * S:]).then_inc(c.in_xt, 16)
                    eng.dma_start(w1[:, FIRST:], pack1[:, FIRST:]).then_inc(c.in_x, 16)
                    eng.dma_start(c.X[:, :], x).then_inc(c.in_x, 16)
                    eng.dma_start(const_sb[:, :], const).then_inc(c.in_x, 16)
                    eng.dma_start(const_b_sb[:, :], const_b).then_inc(c.in_x, 16)

                @block.gpsimd
                def _(eng):
                    eng.memset(zeros[:, :], 0.0).then_inc(c.pool_const, 1)
                    eng.memset(c.minus_half[:, :], -0.5).then_inc(c.pool_const, 1)
            project_heads(c)
            attention(c)
            attention_operands.close()
            c.stack = first_layer
            c.R = c.sb("R", [P, TILES * P])
            context_attention(c)
            route_scores(c)
            feed_forward(c)
        with ExitStack() as mixture:
            c.stack = mixture
            w6 = c.sb("pack6", [P, sum(PACK6.values())])
            v6 = views(w6, PACK6)
            c.m_router, c.s_gate, c.s_up, c.s_down = (blocks(v6[n], DC) for n in ("router", "s_gate", "s_up", "s_down"))
            c.m_bias, c.m_up = v6["bias"], v6["up"]
            def load_mixture(eng):
                eng.dma_start(w6[:, :], pack6).then_inc(c.in_mixture, 16)
                eng.dma_start(c.d_sorted.rearrange("(n p) d -> p n d", p=P),
                              zeros[:, :].unsqueeze(1).broadcast_to([P, MTILES, D])).then_inc(c.in_mixture, 16)
            c.load_mixture = load_mixture
            c.logits_t = c.sb("logits_t", [E, B * S])
            between = ExitStack()
            c.stack = between
            c.cross_weight = [c.sb(f"cross_weight_{n}", [P, DC, D]) for n in "qp"]
            c.cross_k, c.cross_v = c.sb("cross_k", [P, DC * B * CTX]), c.sb("cross_v", [P, B * D])
            running_sum(c)
            rounded_attention(c)
            between.close()
            c.stack = mixture
            c.with_shared = c.sb("with_shared", [P, TILES * D])
            c.row_weights, c.places = c.sb("row_weights", [P, SLOTS_E]), c.sb("places", [P, SLOTS_E], U32)
            c.tile_expert = c.sb("tile_expert", [P, MTILES], I32)
            c.m_down = c.sb("m_down", [P, DC * E * D])
            c.load_down = lambda eng: eng.dma_start(c.m_down[:, :], pack7).then_inc(c.in_w7, 16)
            route_experts(c)
            c.shared = Shared(c)
            scatter(c)
            experts(c)
            combine(c, out)


def k_major(w):
    k, n = w.shape
    return np.ascontiguousarray(w.reshape(k // P, P, n).transpose(1, 0, 2)).reshape(P, -1)


def by_feature(w):
    return w.reshape(-1, H, HD).transpose(0, 2, 1).reshape(-1, D)


def padded_out_weight(wo, bo):
    w = np.zeros((GROUPS, G, 2 * HD, D), np.float32)
    w[:, :, :HD] = wo.reshape(GROUPS, G, HD, D)
    w[0, 0, HD] = bo
    return np.ascontiguousarray(w.transpose(1, 2, 0, 3)).reshape(P, -1)


def kernel(**inputs):
    import concourse.bacc as bacc
    from concourse.bass_utils import run_bass_kernel_spmd

    a = {k: np.asarray(v) for k, v in inputs.items()}
    x = a["x"].reshape(B * S, D)
    ident = np.eye(P, dtype=np.float32)
    pack1 = np.concatenate([
        k_major(by_feature(a["L0_attn_wq"])), k_major(by_feature(a["L0_attn_wk"])),
        by_feature(a["L0_attn_bq"]).reshape(DC, P).T, by_feature(a["L0_attn_bk"]).reshape(DC, P).T,
        k_major(a["L0_attn_wv"]), padded_out_weight(a["L0_attn_wo"], a["L0_attn_bo"]),
        np.tile(a["L0_attn_bv"][None, :], (P, 2))], axis=1)
    keys = np.zeros((2, P, P), np.float32)
    for half in range(2):
        keys[:, half * NKEYS:(half + 1) * NKEYS, half * NKEYS:(half + 1) * NKEYS] = a["L0_ffn_keys"]
    pack2 = np.concatenate([k_major(a["L0_xattn_w" + n].T) for n in "qkvo"], axis=1)
    pack3 = np.concatenate([k_major(a["L0_ffn_W_q"]), k_major(keys.reshape(2 * P, P)), k_major(a["L0_ffn_down_embed"].T),
                            k_major(a["L0_ffn_up_embed"]), k_major(a["L0_ffn_gate_w"]), k_major(a["L0_ffn_up_w"]),
                            k_major(a["L0_ffn_down_w"])], axis=1)
    pack4 = np.concatenate([k_major(np.concatenate([a["L1_attn_Wk"].T, a["L1_attn_Wv"].T], axis=1)),
                            k_major(a["L1_attn_Wq"].T), k_major(a["L1_attn_Wo"].T)], axis=1)
    ctx = a["ctx_2048"]
    ctx_t_all = np.ascontiguousarray(ctx.reshape(B * CTX, D).T)
    part = np.arange(P)[:, None]
    pack5 = np.concatenate([
        k_major(a["L1_xattn_wq"]), k_major(a["L1_xattn_wp"]), k_major(a["L1_xattn_wkv"][:D].T),
        k_major(a["L1_xattn_wkv"][D:].T), k_major(ctx_t_all),
        k_major(np.repeat(ctx_t_all.reshape(D, B, 1, CTX), 2, axis=2).reshape(D, B * P)),
        a["L1_xattn_bq"].reshape(DC, P).T, a["L1_xattn_bkv"][:D].reshape(DC, P).T,
        np.tile(a["L1_xattn_bkv"][None, D:], (P, 1)), np.tile(a["L1_xattn_bp"][None, :], (P, 2)),
        (part // HD == np.arange(HB)).astype(np.float32),
        (part // CTX == np.arange(2 * HD) // HD).astype(np.float32)], axis=1)
    up = np.concatenate([a["L1_ffn_w_gate"], a["L1_ffn_w_up"]], axis=1)
    down = np.pad(a["L1_ffn_w_down"].transpose(2, 0, 1), ((0, FP - F), (0, 0), (0, 0)))
    pad = ((0, 0), (0, FP - F))
    pack6 = np.concatenate([
        k_major(a["L1_ffn_gate_w"].T), np.tile(a["L1_ffn_expert_bias"][None, :], (P, 1)),
        k_major(np.pad(a["L1_ffn_sw_gate"].T, pad)), k_major(np.pad(a["L1_ffn_sw_up"].T, pad)),
        k_major(np.pad(a["L1_ffn_sw_down"].T, pad[::-1])), k_major(up.transpose(2, 0, 1).reshape(D, -1))],
        axis=1)
    earlier = np.tile(np.tri(E, E, -1, dtype=np.float32).reshape(1, -1), (P, 1))
    iota = np.tile(np.arange(NKEYS, dtype=np.float32), (P, 1))
    tri = np.triu(np.full((P, S), D ** 0.5 / S, np.float32))
    arrays = {
        "x": k_major(x), "xt": k_major(np.ascontiguousarray(x.T)),
        "const": np.concatenate([ident, iota, iota[:, :TOP] - TOP, tri, earlier], axis=1),
        "const_b": np.concatenate([ident, np.triu(np.ones((P, P)), 1), np.ones((P, P))], axis=1).astype(np_bf16()),
        "pack1": pack1, "pack2": pack2, "pack3": pack3, "pack4": pack4, "pack5": pack5, "pack6": pack6, "pack7": k_major(down.reshape(FP, -1)), "ctx": ctx,
        "ctx_t": np.ascontiguousarray(ctx.transpose(0, 2, 1).reshape(B, DC, P, CTX).transpose(0, 2, 1, 3))}
    nc = bacc.Bacc("TRN2", target_bir_lowering=False, num_devices=1)
    args = [nc.dram_tensor("in_" + n, v.shape, mybir.dt.from_np(v.dtype), kind="ExternalInput").ap()
            for n, v in arrays.items()]
    out = nc.dram_tensor("out", [B, S, D], F32, kind="ExternalOutput").ap()
    decoder(nc, *args, out)
    r = run_bass_kernel_spmd(nc, [{"in_" + n: v for n, v in arrays.items()}], core_ids=[0])
    return r.results[0]["out"]


def np_bf16():
    return mybir.dt.np(BF16)
```
